# Optimizing a Trainium2 kernel written in Bass

```python
import numpy as np
import jax
import jax.numpy as jnp

def _softmax(x, axis=-1):
    return jax.nn.softmax(x, axis=axis)

def _gelu(x):
    return jax.nn.gelu(x, approximate=True)

def _silu(x):
    return jax.nn.silu(x)

def _sigmoid(x):
    return jax.nn.sigmoid(x)

def _layernorm(x, axis=-1, eps=1e-05):
    m = jnp.mean(x, axis=axis, keepdims=True)
    v = jnp.var(x, axis=axis, keepdims=True)
    return (x - m) / jnp.sqrt(v + eps)

def _scatter_add(tgt, idx, src, axis=0):
    return tgt.at[idx].add(src)

def _segment_sum(src, seg, n):
    return jax.ops.segment_sum(src, seg, n)
kernel_name = 'mk_gps_d1_gnn_r8_02ce50'

def setup_inputs(seed: int=0):
    np.random.seed(seed)
    _w = jnp.asarray

    def _rec_inputs():
        import jax
        import jax.numpy as jnp
        _gk = jax.random.key(seed)
        x = -0.0003713 + 1 * jax.random.normal(jax.random.fold_in(_gk, 1), (6250, 256), jnp.float32)
        src = jax.random.randint(jax.random.fold_in(_gk, 2), (100000,), 0, 6250, jnp.int32)
        dst = jnp.minimum((6250 * jax.random.uniform(jax.random.fold_in(_gk, 3), (100000,)) ** 2.0).astype(jnp.int32), 49999)
        _o = jnp.argsort(dst, stable=True)
        src = src[_o]
        dst = dst[_o]
        edge_weight = -7.32377e-05 + 0.176746 * jax.random.normal(jax.random.fold_in(_gk, 12), (100000,), jnp.float32)
        return (x, src, dst, edge_weight)
    x, src, dst, edge_weight = _rec_inputs()

    def _L0_gnn_setup():
        import jax, jax.numpy as jnp
        import numpy as np
        N_NODES = 6250
        NNZ = 200000
        D_FEAT = 256
        key = jax.random.key(seed)
        k_x, k_v, k_r, k_c = jax.random.split(key, 4)
        x = jax.random.normal(k_x, (N_NODES, D_FEAT), dtype=jnp.float32)
        std = 1.0 / np.sqrt(NNZ / N_NODES)
        values = jax.random.normal(k_v, (NNZ,), dtype=jnp.float32) * std
        row = jax.random.randint(k_r, (NNZ,), 0, N_NODES, dtype=jnp.int64)
        col = jax.random.randint(k_c, (NNZ,), 0, N_NODES, dtype=jnp.int64)
        return {'x': x, 'values': values, 'row': row, 'col': col}
    _L0_gnn_all = _L0_gnn_setup()
    _L0_gnn_in = {k: v for k, v in _L0_gnn_all.items() if k in ()}
    del _L0_gnn_all

    def _L0_mix_setup():
        import jax, jax.numpy as jnp
        import numpy as np
        B, N, C = (8, 1024, 256)
        H, D, S = (8, 32, 32)
        HID = 4 * C

        def layernorm(x, w, b, eps=1e-05):
            mu = jnp.mean(x, axis=-1, keepdims=True)
            var = jnp.mean(jnp.square(x - mu), axis=-1, keepdims=True)
            return (x - mu) * jax.lax.rsqrt(var + eps) * w + b

        def linear_no_attn(x, Wx, bx, Wq, Wk, Wv, Wo, bo):
            x_mid = x @ Wx.T + bx
            x_mid = x_mid.reshape(x.shape[0], x.shape[1], H, D).transpose(0, 2, 1, 3)
            q = jax.nn.softmax(x_mid @ Wq.T, axis=-1)
            k = jax.nn.softmax(x_mid @ Wk.T, axis=-2)
            v = x_mid @ Wv.T
            kv = jnp.einsum('bhns,bhnd->bhsd', k, v)
            qkv = jnp.einsum('bhns,bhsd->bhnd', q, kv)
            qkv = qkv.transpose(0, 2, 1, 3).reshape(x.shape[0], x.shape[1], H * D)
            return qkv @ Wo.T + bo
        key = jax.random.key(seed)
        ks = jax.random.split(key, 16)
        s = lambda fan: 1.0 / np.sqrt(fan)
        return {'fx': jax.random.normal(ks[0], (B, N, C), jnp.float32), 'ln1_w': jnp.ones((C,), jnp.float32), 'ln1_b': jnp.zeros((C,), jnp.float32), 'Wx': jax.random.uniform(ks[1], (C, C), jnp.float32, -s(C), s(C)), 'bx': jax.random.uniform(ks[2], (C,), jnp.float32, -s(C), s(C)), 'Wq': jax.random.uniform(ks[3], (S, D), jnp.float32, -s(D), s(D)), 'Wk': jax.random.uniform(ks[4], (S, D), jnp.float32, -s(D), s(D)), 'Wv': jax.random.uniform(ks[5], (D, D), jnp.float32, -s(D), s(D)), 'Wo': jax.random.uniform(ks[6], (C, C), jnp.float32, -s(C), s(C)), 'bo': jax.random.uniform(ks[7], (C,), jnp.float32, -s(C), s(C)), 'ln2_w': jnp.ones((C,), jnp.float32), 'ln2_b': jnp.zeros((C,), jnp.float32), 'W1': jax.random.uniform(ks[8], (HID, C), jnp.float32, -s(C), s(C)), 'b1': jax.random.uniform(ks[9], (HID,), jnp.float32, -s(C), s(C)), 'W2': jax.random.uniform(ks[10], (C, HID), jnp.float32, -s(HID), s(HID)), 'b2': jax.random.uniform(ks[11], (C,), jnp.float32, -s(HID), s(HID))}
    _L0_mix_all = _L0_mix_setup()
    _L0_mix_in = {k: v for k, v in _L0_mix_all.items() if k in ('ln1_w', 'ln1_b', 'Wx', 'bx', 'Wq', 'Wk', 'Wv', 'Wo', 'bo', 'ln2_w', 'ln2_b', 'W1', 'b1', 'W2', 'b2')}
    del _L0_mix_all

    def _L0_ffn_setup():
        import jax, jax.numpy as jnp
        import numpy as np
        BN_EPS = 0.001

        def _bn(h, g, b, m, v):
            return g * (h - m) * jax.lax.rsqrt(v + BN_EPS) + b
        key = jax.random.key(seed)
        ks = jax.random.split(key, 8)
        B, F, Df = (256, 64, 256)
        E, H, D = (8, 256, 256)
        s1 = 1.0 / np.sqrt(Df)
        s2 = 1.0 / np.sqrt(H)
        return {'x': jax.random.normal(ks[0], (B, F, Df), jnp.float32), 'Wr': jax.random.normal(ks[1], (Df, E), jnp.float32) * s1, 'br': jnp.zeros((E,), jnp.float32), 'W1': jax.random.normal(ks[2], (E, Df, H), jnp.float32) * s1, 'b1': jnp.zeros((E, H), jnp.float32), 'g1': jnp.ones((E, H), jnp.float32), 'be1': jnp.zeros((E, H), jnp.float32), 'm1': jnp.zeros((E, H), jnp.float32), 'v1': jnp.ones((E, H), jnp.float32), 'W2': jax.random.normal(ks[3], (E, H, H), jnp.float32) * s2, 'b2': jnp.zeros((E, H), jnp.float32), 'g2': jnp.ones((E, H), jnp.float32), 'be2': jnp.zeros((E, H), jnp.float32), 'm2': jnp.zeros((E, H), jnp.float32), 'v2': jnp.ones((E, H), jnp.float32), 'Wo': jax.random.normal(ks[4], (E, H, D), jnp.float32) * s2, 'bo': jnp.zeros((E, D), jnp.float32)}
    _L0_ffn_all = _L0_ffn_setup()
    _L0_ffn_in = {k: v for k, v in _L0_ffn_all.items() if k in ('Wr', 'br', 'W1', 'b1', 'g1', 'be1', 'm1', 'v1', 'W2', 'b2', 'g2', 'be2', 'm2', 'v2', 'Wo', 'bo')}
    del _L0_ffn_all
    return {'x': x, 'src': src, 'dst': dst, 'edge_weight': edge_weight, 'L0_mix_ln1_w': _L0_mix_in['ln1_w'], 'L0_mix_ln1_b': _L0_mix_in['ln1_b'], 'L0_mix_Wx': _L0_mix_in['Wx'], 'L0_mix_bx': _L0_mix_in['bx'], 'L0_mix_Wq': _L0_mix_in['Wq'], 'L0_mix_Wk': _L0_mix_in['Wk'], 'L0_mix_Wv': _L0_mix_in['Wv'], 'L0_mix_Wo': _L0_mix_in['Wo'], 'L0_mix_bo': _L0_mix_in['bo'], 'L0_mix_ln2_w': _L0_mix_in['ln2_w'], 'L0_mix_ln2_b': _L0_mix_in['ln2_b'], 'L0_mix_W1': _L0_mix_in['W1'], 'L0_mix_b1': _L0_mix_in['b1'], 'L0_mix_W2': _L0_mix_in['W2'], 'L0_mix_b2': _L0_mix_in['b2'], 'L0_ffn_Wr': _L0_ffn_in['Wr'], 'L0_ffn_br': _L0_ffn_in['br'], 'L0_ffn_W1': _L0_ffn_in['W1'], 'L0_ffn_b1': _L0_ffn_in['b1'], 'L0_ffn_g1': _L0_ffn_in['g1'], 'L0_ffn_be1': _L0_ffn_in['be1'], 'L0_ffn_m1': _L0_ffn_in['m1'], 'L0_ffn_v1': _L0_ffn_in['v1'], 'L0_ffn_W2': _L0_ffn_in['W2'], 'L0_ffn_b2': _L0_ffn_in['b2'], 'L0_ffn_g2': _L0_ffn_in['g2'], 'L0_ffn_be2': _L0_ffn_in['be2'], 'L0_ffn_m2': _L0_ffn_in['m2'], 'L0_ffn_v2': _L0_ffn_in['v2'], 'L0_ffn_Wo': _L0_ffn_in['Wo'], 'L0_ffn_bo': _L0_ffn_in['bo']}

def reference(x, src, dst, edge_weight, L0_mix_ln1_w, L0_mix_ln1_b, L0_mix_Wx, L0_mix_bx, L0_mix_Wq, L0_mix_Wk, L0_mix_Wv, L0_mix_Wo, L0_mix_bo, L0_mix_ln2_w, L0_mix_ln2_b, L0_mix_W1, L0_mix_b1, L0_mix_W2, L0_mix_b2, L0_ffn_Wr, L0_ffn_br, L0_ffn_W1, L0_ffn_b1, L0_ffn_g1, L0_ffn_be1, L0_ffn_m1, L0_ffn_v1, L0_ffn_W2, L0_ffn_b2, L0_ffn_g2, L0_ffn_be2, L0_ffn_m2, L0_ffn_v2, L0_ffn_Wo, L0_ffn_bo):
    import jax
    import jax.numpy as jnp

    def _L0_gnn_ref(x, values, row, col):
        import jax, jax.numpy as jnp
        import numpy as np
        N_NODES = 6250
        NNZ = 200000
        D_FEAT = 256
        msgs = values[:, None] * x[col]
        out = jax.ops.segment_sum(msgs, row, num_segments=N_NODES)
        return out

    def _L0_mix_ref(fx, ln1_w, ln1_b, Wx, bx, Wq, Wk, Wv, Wo, bo, ln2_w, ln2_b, W1, b1, W2, b2):
        import jax, jax.numpy as jnp
        import numpy as np
        B, N, C = (8, 1024, 256)
        H, D, S = (8, 32, 32)
        HID = 4 * C

        def layernorm(x, w, b, eps=1e-05):
            mu = jnp.mean(x, axis=-1, keepdims=True)
            var = jnp.mean(jnp.square(x - mu), axis=-1, keepdims=True)
            return (x - mu) * jax.lax.rsqrt(var + eps) * w + b

        def linear_no_attn(x, Wx, bx, Wq, Wk, Wv, Wo, bo):
            x_mid = x @ Wx.T + bx
            x_mid = x_mid.reshape(x.shape[0], x.shape[1], H, D).transpose(0, 2, 1, 3)
            q = jax.nn.softmax(x_mid @ Wq.T, axis=-1)
            k = jax.nn.softmax(x_mid @ Wk.T, axis=-2)
            v = x_mid @ Wv.T
            kv = jnp.einsum('bhns,bhnd->bhsd', k, v)
            qkv = jnp.einsum('bhns,bhsd->bhnd', q, kv)
            qkv = qkv.transpose(0, 2, 1, 3).reshape(x.shape[0], x.shape[1], H * D)
            return qkv @ Wo.T + bo
        h = linear_no_attn(layernorm(fx, ln1_w, ln1_b), Wx, bx, Wq, Wk, Wv, Wo, bo) + fx
        y = layernorm(h, ln2_w, ln2_b)
        y = jax.nn.gelu(y @ W1.T + b1, approximate=False)
        y = y @ W2.T + b2
        return y + h

    def _L0_ffn_ref(x, Wr, br, W1, b1, g1, be1, m1, v1, W2, b2, g2, be2, m2, v2, Wo, bo):
        import jax, jax.numpy as jnp
        import numpy as np
        BN_EPS = 0.001

        def _bn(h, g, b, m, v):
            return g * (h - m) * jax.lax.rsqrt(v + BN_EPS) + b
        feat = jnp.mean(x, axis=0)
        w = jax.nn.softmax(feat @ Wr + br, axis=-1)
        h = jnp.einsum('bfd,edh->bfeh', x, W1) + b1
        h = jax.nn.relu(_bn(h, g1, be1, m1, v1))
        h = jnp.einsum('bfeh,ehk->bfek', h, W2) + b2
        h = jax.nn.relu(_bn(h, g2, be2, m2, v2))
        y = jnp.einsum('bfeh,ehd->bfed', h, Wo) + bo
        return jnp.einsum('bfed,fe->bfd', y, w)
    xn = _layernorm(x, axis=-1)
    x = x + _L0_gnn_ref(xn, edge_weight, src, dst) + _L0_mix_ref(xn[None], L0_mix_ln1_w, L0_mix_ln1_b, L0_mix_Wx, L0_mix_bx, L0_mix_Wq, L0_mix_Wk, L0_mix_Wv, L0_mix_Wo, L0_mix_bo, L0_mix_ln2_w, L0_mix_ln2_b, L0_mix_W1, L0_mix_b1, L0_mix_W2, L0_mix_b2)[0]
    x = x + _L0_ffn_ref(_layernorm(x, axis=-1)[None], L0_ffn_Wr, L0_ffn_br, L0_ffn_W1, L0_ffn_b1, L0_ffn_g1, L0_ffn_be1, L0_ffn_m1, L0_ffn_v1, L0_ffn_W2, L0_ffn_b2, L0_ffn_g2, L0_ffn_be2, L0_ffn_m2, L0_ffn_v2, L0_ffn_Wo, L0_ffn_bo)[0]
    return x

_drawn_inputs = setup_inputs


def setup_inputs(seed=0):
    import zlib

    import numpy as np

    out = dict(_drawn_inputs(seed))
    spreads = {'L0_mix_ln1_w': (1.0, 0.6),
     'L0_mix_ln1_b': (0.0, 0.788),
     'L0_mix_ln2_w': (1.0, 0.6),
     'L0_mix_ln2_b': (0.0, 2.0),
     'L0_ffn_br': (0.0, 2.0),
     'L0_ffn_b1': (0.0, 2.0),
     'L0_ffn_g1': (1.0, 0.6),
     'L0_ffn_be1': (0.0, 2.0),
     'L0_ffn_m1': (0.0, 2.0),
     'L0_ffn_v1': (1.0, 0.6),
     'L0_ffn_b2': (0.0, 2.0),
     'L0_ffn_g2': (1.0, 0.6),
     'L0_ffn_be2': (0.0, 2.0),
     'L0_ffn_m2': (0.0, 2.0),
     'L0_ffn_v2': (1.0, 0.6),
     'L0_ffn_bo': (0.0, 2.0)}
    factors = {'L0_mix_Wx': 5.676,
     'L0_mix_bx': 8.0,
     'L0_mix_Wq': 8.0,
     'L0_mix_Wk': 8.0,
     'L0_mix_Wv': 4.706,
     'L0_mix_Wo': 4.886,
     'L0_mix_bo': 76.301,
     'L0_mix_b1': 64.0,
     'L0_mix_b2': 52.024,
     'edge_weight': 6.815,
     'L0_mix_W1': 8.0,
     'L0_mix_W2': 8.0,
     'L0_ffn_Wr': 6.989,
     'L0_ffn_W1': 8.0,
     'L0_ffn_W2': 6.537,
     'L0_ffn_Wo': 4.803}
    for name, (base, spread) in spreads.items():
        noise = np.random.default_rng([zlib.crc32(name.encode()), seed]).standard_normal(out[name].shape)
        drawn = base * np.exp(spread * noise) if base else spread * noise
        out[name] = jnp.asarray(drawn.astype(out[name].dtype))
    for name, factor in factors.items():
        out[name] = (out[name] * factor).astype(out[name].dtype)
    return out
```

```python
import concourse.bass as bass
from concourse import mybir
from contextlib import ExitStack

F32 = mybir.dt.float32
BF16 = mybir.dt.bfloat16
I32 = mybir.dt.int32
U32 = mybir.dt.uint32
U8 = mybir.dt.uint8
ALU = mybir.AluOpType
ACT = mybir.ActivationFunctionType
AX = mybir.AxisListType

P = 128
N, D = 6250, 256
E = 100000
KF = D // P
TILES = -(-N // P)
CT = 4
CW = CT * P
CHUNKS = -(-TILES // CT)
FULL = CHUNKS - 1
TAIL_T = TILES - FULL * CT
TAIL_ROWS = N - FULL * CW
ROWS = CHUNKS * CW
LN_EPS = 1e-5

HEADS, HD = 8, 32
HID = 4 * D
HM = HID // P
EXP = 8
BN_EPS = 1e-3

EC = -(-E // P)
LAST_EC = E - (P - 1) * EC
BLOCKS = CHUNKS * CT
SGRP = 17
SPAIRS = EC // (2 * SGRP)
SEGMENTS = (0, 5, 11, 17, SPAIRS)
RING = 32
HALF = RING // 2
SUB = 4
PAIR = 2 * P
MAX_PAIRS = E // PAIR + BLOCKS + 1
MAX_ROUNDS = -(-2 * MAX_PAIRS // RING)
TT = (MAX_ROUNDS + 1) * RING
assert EC == 2 * SGRP * SPAIRS


def build(nc, x, src, dst, edge_weight, ln1_w, ln1_b, wx_t, bx, wq_t, wk_t, wv_t, wo_t, bo, ln2_w, ln2_b,
          w1_t, b1, w2_t, b2, wr, br, ew1, eb1, eg1, ebe1, em1, ev1, ew2, eb2, eg2, ebe2, em2, ev2, ewo, ebo, out):
    with ExitStack() as ctx:
        def sb(name, shape, dt=F32):
            return ctx.enter_context(nc.sbuf_tensor(name, shape, dt))

        def sem(name):
            return ctx.enter_context(nc.semaphore(name))

        def scratch(name, shape, dt=F32):
            return nc.dram_tensor(name, shape, dt).ap()

        table = scratch("edge_table", [P * TT, 4])
        xn_rows = scratch("xn_rows", [ROWS, D])
        xm_rows = scratch("xm_rows", [ROWS, D])
        xmid_d = scratch("xmid", [CHUNKS * P, KF * CW])

        ones = sb("ones", [P, P])
        ident = sb("ident", [P, P])
        lower = sb("lower", [P, P])
        iota = sb("iota", [P, P])
        zero_row = sb("zero_row", [1, D], BF16)
        eps_ln = sb("eps_ln", [P, 1])
        eps_bn = sb("eps_bn", [P, 1])
        head_mask = sb("head_mask", [P, P])
        pick = sb("pick", [EXP, EXP, P])
        lnp = sb("lnp", [P, 4, KF])
        bx_s = sb("bx_s", [P, KF])
        b1_s = sb("b1_s", [P, HM])
        bo_row = sb("bo_row", [1, D])
        b2_row = sb("b2_row", [1, D])
        br_row = sb("br_row", [1, EXP])
        ebo_s = sb("ebo_s", [EXP, D])
        bnp = sb("bnp", [P, 10, EXP * KF])
        bn_s = sb("bn_s", [P, 2, EXP * KF])
        bn_t = sb("bn_t", [P, 2, EXP * KF])
        bn_w = sb("bn_w", [P, 2, EXP * KF])

        wx_s = sb("wx_s", [P, KF, D])
        wo_s = sb("wo_s", [P, KF, D])
        w1_s = sb("w1_s", [P, KF, HID])
        w2_s = sb("w2_s", [P, HM, D])
        bdq = sb("bdq", [P, P])
        bdkv = sb("bdkv", [P, 2, P])
        wr_s = sb("wr_s", [P, KF, EXP])
        kvw = sb("kvw", [P, KF, D])

        with ExitStack() as early:
            rec = early.enter_context(nc.sbuf_tensor("rec", [P, EC, 4], F32))
        recs = sb("recs", [P, TT, 4])
        adr = sb("adr", [P, EC], I32)
        stage_idx = sb("stage_idx", [P, 2, SGRP], U32)
        stage_rec = sb("stage_rec", [P, 2, SGRP, 4])
        idx = sb("idx", [P, TT], U32)
        gather_idx = sb("gather_idx", [P, 2, HALF], U32)
        select = sb("select", [P, 2, P])
        pair_i = sb("pair_i", [P, BLOCKS + 1], I32)
        rounds_i = sb("rounds_i", [P, 1], I32)

        with ExitStack() as early:
            def eb(name, shape, dt=F32):
                return early.enter_context(nc.sbuf_tensor(name, shape, dt))

            src_i, dst_i, w_e = eb("src_i", [P, EC], I32), eb("dst_i", [P, EC], I32), eb("w_e", [P, EC])
            blk_i, blk = eb("blk_i", [P, EC], I32), eb("blk", [P, EC])
            pos, pos_i = eb("pos", [P, EC]), eb("pos_i", [P, EC], I32)
            mask = eb("mask", [P, BLOCKS, EC], U8)
            rank, zeros = eb("rank", [P, 2, EC]), eb("zeros", [P, KF * CW])
            cnt, base, pairs_f, pair_x = (eb(n, [P, BLOCKS + 1]) for n in ("cnt", "base", "pairs_f", "pair_x"))
            tot_i = eb("tot_i", [P, BLOCKS], I32)
        ew_s = sb("ew_s", [P, 3, EXP, KF, D])
        ring = sb("ring", [P, RING, D])

        with ExitStack() as early:
            def mb(name, shape, dt=F32):
                return early.enter_context(nc.sbuf_tensor(name, shape, dt))

            xa = [mb(f"xa{b}", [P, CT, D]) for b in (0, 1)]
            xa_n = [mb(f"xa_n{b}", [P, CT, D]) for b in (0, 1)]
            stats, mv = mb("stats", [P, CT, 6]), mb("mv", [P, CT, 2])
            sd, rstd = mb("sd", [P, CT]), mb("rstd", [P, CT])
            hn, hT = mb("hn", [P, CT, D]), mb("hT", [P, KF, CW])
            xmT = [mb(f"xmT{b}", [P, KF, CW]) for b in (0, 1)]
            kchunk, kmax, mrow = mb("kchunk", [P, KF]), mb("kmax", [P, KF]), mb("mrow", [1, KF, P])
            rk = mb("rk", [P, KF])
            qmax, qsum = mb("qmax", [P, CT * HEADS]), mb("qsum", [P, CT * HEADS])
            qx = mb("qx", [P, CT, D])
            h = [mb(f"h_mix{b}", [P, CT, D]) for b in (0, 1)]
            yT = [mb(f"yT{b}", [P, KF, CW]) for b in (0, 1)]
            gT = mb("gT", [P, HM, CW])
            ek, vv = (gT[:, k, :].rearrange("p (b f c) -> p b f c", b=2, f=KF) for k in (0, 1))
            kvT = gT[:, 2, 0:KF * P].rearrange("p (f c) -> p f c", f=KF)
            qT, yn, xb, xb_n = hT, hn, xa, xa_n
        cx = sb("cx", [P, CT, D])
        x1 = [sb(f"x1_{b}", [P, CT, D]) for b in (0, 1)]
        c_stats, c_mv = sb("c_stats", [P, CT, 6]), sb("c_mv", [P, CT, 2])
        c_sdt, c_rstd = sb("c_sdt", [P, CT]), sb("c_rstd", [P, CT])
        x2n = sb("x2n", [P, CT, D])
        x2T = [sb(f"x2T{b}", [P, KF, CW]) for b in (0, 1)]
        rt, rmax = sb("rt", [P, CT, EXP]), sb("rmax", [P, CT])
        wT = [sb(f"wT{b}", [EXP, CW]) for b in (0, 1)]
        h1 = sb("h1", [P, 2, KF, CW])
        h2r = sb("h2r", [P, KF, CW])
        h2 = sb("h2", [P, 2, KF, CW])
        ys = sb("ys", [P, KF, CW])
        xout = [sb(f"xout{b}", [P, CT, D]) for b in (0, 1)]

        ps = ctx.enter_context(nc.psum_tensor("ps", [P, 8, 512], F32))

        def rows(b, nt=CT):
            return ps[:, b:b + 2, :].rearrange("p a (t d) -> p (a t) d", d=D)[:, 0:nt, :]

        def tile(b, j):
            return ps[:, b + j // 2, (j % 2) * D:(j % 2) * D + D]

        pad_set, edges_loaded, consts = sem("pad_set"), sem("edges_loaded"), sem("consts")
        dve_chain, act_chain = sem("dve_chain"), sem("act_chain")
        counts_done, count_sums = sem("counts_done"), sem("count_sums")
        recs_zero, zeroed = sem("recs_zero"), sem("zeroed")
        addresses = sem("addresses")
        staged = [sem(f"staged{h_}") for h_ in (0, 1)]
        scattered = [sem(f"scattered{h_}") for h_ in (0, 1)]
        pool_go, dve_go = sem("pool_go"), sem("dve_go")
        table_loaded, idx_ready = sem("table_loaded"), sem("idx_ready")
        idx_staged = [sem(f"idx_staged{h_}") for h_ in (0, 1)]
        gathered = [sem(f"gathered{q}") for q in range(RING // SUB)]
        rows_ready, tiles_used, select_ready = sem("rows_ready"), sem("tiles_used"), sem("select_ready")
        params, diag_zero, mix_done, ew_loaded, bn_ready = (
            sem(n) for n in ("params", "diag_zero", "mix_done", "ew_loaded", "bn_ready"))
        bn_var, bn_sd = sem("bn_var"), sem("bn_sd")
        ax = [sem(f"ax{b}") for b in (0, 1)]
        ax_free, ax_stats, ax_sd, axn, hn_ready, hn_T, hT_ready, xm_ps, xm_ready, k_ps, k_max = (
            sem(n) for n in ("ax_free", "ax_stats", "ax_sd", "axn", "hn_ready", "hn_T", "hT_ready", "xm_ps",
                             "xm_ready", "k_ps", "k_max"))
        axn_stored = [sem(f"axn_stored{b}") for b in (0, 1)]
        xm_stored = [sem(f"xm_stored{b}") for b in (0, 1)]
        mrow_ps, mrow_ready = sem("mrow_ps"), sem("mrow_ready")
        kx = [sem(f"kx{b}") for b in (0, 1)]
        kv_ps, ek_ready, vv_ready, kv_added, kvT_ready, kvw_ps, kvw_ready = (
            sem(n) for n in ("kv_ps", "ek_ready", "vv_ready", "kv_added", "kvT_ready", "kvw_ps", "kvw_ready"))
        bx_in = [sem(f"bx_in{b}") for b in (0, 1)]
        q_ps, q_shift, q_exp, q_norm, q_T, qT_ready, at_ps, h_ready, y_stats, y_sd, y_ready, y_T, yT_ready = (
            sem(n) for n in ("q_ps", "q_shift", "q_exp", "q_norm", "q_T", "qT_ready", "at_ps", "h_ready", "y_stats",
                             "y_sd", "y_ready", "y_T", "yT_ready"))
        hid_ps, hid_ready, mlp_ps, xo_ready, xo_stored = (
            sem(n) for n in ("hid_ps", "hid_ready", "mlp_ps", "xo_ready", "xo_stored"))
        cx_in, block_sums, x1_ready, c_sd, x2_ready, x2_T, x2T_ready, r_ps, r_shift, r_exp, w_ready, w_T, wT_ready = (
            sem(n) for n in ("cx_in", "block_sums", "x1_ready", "c_sd", "x2_ready", "x2_T", "x2T_ready", "r_ps",
                             "r_shift", "r_exp", "w_ready", "w_T", "wT_ready"))
        z1_ps, h1_ready, wb_ps, z2_ps, h2r_ready, h2_ready, y_ps, ys_ready, y_back, xout_ready = (
            sem(n) for n in ("z1_ps", "h1_ready", "wb_ps", "z2_ps", "h2r_ready", "h2_ready", "y_ps", "ys_ready",
                             "y_back", "xout_ready"))
        out_stored = [sem(f"out_stored{b}") for b in (0, 1)]

        def mixer_chunks(eng, step):
            with eng.Fori(0, FULL // 2) as it:
                for b in (0, 1):
                    step(it * 2 + b, b, it, CT)
            step(FULL, 0, FULL // 2, TAIL_T)

        def ahead(eng, first, step, last):
            first()
            with eng.Fori(0, FULL // 2) as it:
                for b in (0, 1):
                    step(it * 2 + b, b, it)
            last(FULL, 0, FULL // 2)

        block = ctx.enter_context(nc.Block())

        @block.gpsimd
        def _(pool):
            nc.gpsimd.iota(iota[:, :], [[1, P]], base=0, channel_multiplier=0,
                           allow_small_or_imprecise_dtypes=True).then_inc(consts, 1)
            nc.gpsimd.memset(ones[:, :], 1.0).then_inc(consts, 1)
            nc.gpsimd.memset(pick[:, :, :], 1.0).then_inc(consts, 1)
            nc.gpsimd.memset(head_mask[:, :], 1.0).then_inc(consts, 1)
            pool.wait_ge(consts, 4)
            nc.gpsimd.affine_select(out=lower[:, :], in_=ones[:, :], compare_op=ALU.is_gt, fill=0.0, base=0,
                                    pattern=[[1, P]], channel_multiplier=-1).then_inc(consts, 1)
            nc.gpsimd.affine_select(out=ident[:, :], in_=ones[:, :], compare_op=ALU.is_equal, fill=0.0, base=0,
                                    pattern=[[-1, P]], channel_multiplier=1).then_inc(consts, 1)
            nc.gpsimd.affine_select(out=pick[:, :, :], in_=pick[:, :, :], compare_op=ALU.is_equal, fill=0.0, base=0,
                                    pattern=[[-1, EXP], [0, P]], channel_multiplier=1).then_inc(consts, 1)
            hm = head_mask[:, :].rearrange("p (g c) -> p g c", c=HD)
            nc.gpsimd.affine_select(out=hm, in_=hm, compare_op=ALU.is_ge, fill=0.0, base=0,
                                    pattern=[[-HD, P // HD], [0, HD]], channel_multiplier=1).then_inc(consts, 1)
            pool.wait_ge(consts, 8)
            nc.gpsimd.affine_select(out=hm, in_=hm, compare_op=ALU.is_ge, fill=0.0, base=HD - 1,
                                    pattern=[[HD, P // HD], [0, HD]], channel_multiplier=-1).then_inc(consts, 1)
            pool.wait_ge(zeroed, 16 * 7)
            with pool.Fori(0, SPAIRS) as g:
                for h_ in (0, 1):
                    pool.wait_ge(staged[h_], (g + 1) * 32)
                    pool.sem_inc(pool_go, 1)
                    for j in range(SGRP):
                        pool.indirect_dma_start(table, bass.IndirectOffsetOnAxis(ap=stage_idx[:, h_, j:j + 1], axis=0),
                                                stage_rec[:, h_, j, :], None).then_inc(scattered[h_], 16)
            pool.wait_ge(idx_ready, 1)
            for b in (0, 1):
                pool.wait_ge(axn_stored[b], 16 * (FULL // 2 + 2 - b))
            pool.wait_ge(bn_ready, 1)
            rounds = pool.value_load(rounds_i[0:1, 0:1], min_val=2, max_val=MAX_ROUNDS)

            def gather_round(r, first):
                for j in range(RING):
                    half = j // HALF
                    if j % HALF == 0:
                        pool.wait_ge(idx_staged[half], (r + 1) * 16)
                    if j % SUB == 0:
                        if not first:
                            pool.wait_ge(tiles_used, r * RING + j + SUB - RING + 2)
                        pool.sem_inc(pool_go, 1)
                    pool.indirect_dma_start(
                        ring[:, j, :], None, xn_rows,
                        bass.IndirectOffsetOnAxis(ap=gather_idx[:, half, j % HALF:j % HALF + 1], axis=0),
                    ).then_inc(gathered[j // SUB], 16)

            gather_round(0, True)
            with pool.Fori(1, rounds) as r:
                gather_round(r, False)

        @block.sync
        def _(sp):
            edge_inputs = ((src_i, src), (dst_i, dst), (w_e, edge_weight))
            sp.wait_ge(pad_set, 3)
            for t, d in edge_inputs:
                sp.dma_start(t[0:P - 1, :], d[0:(P - 1) * EC].rearrange("(p c) -> p c", p=P - 1)).then_inc(edges_loaded, 16)
            for t, d in edge_inputs:
                sp.dma_start(t[P - 1:P, 0:LAST_EC], d[(P - 1) * EC:E].rearrange("(p c) -> p c", p=1)).then_inc(edges_loaded, 16)
            sp.wait_ge(recs_zero, 1)
            tab = table.rearrange("(p t) f -> p (t f)", p=P)
            quarter = TT * 4 // 4
            for q in range(4):
                sp.dma_start(tab[:, q * quarter:(q + 1) * quarter], zeros[:, 0:quarter]).then_inc(zeroed, 16)
            for a in (xm_rows, xn_rows):
                sp.dma_start(a[TILES * P:ROWS, :].rearrange("(p r) d -> p (r d)", p=P),
                             zeros[:, 0:(ROWS // P - TILES) * D]).then_inc(zeroed, 16)
            sp.dma_start(xmid_d[FULL * P:CHUNKS * P, :], zeros[:, :]).then_inc(zeroed, 16)
            def stage(g, h_):
                k = (g * 2 + h_) * SGRP
                sp.dma_start(stage_idx[:, h_, :], adr[:, bass.ds(k, SGRP)].bitcast(U32)).then_inc(staged[h_], 16)
                sp.dma_start(stage_rec[:, h_, :, :], rec[:, bass.ds(k, SGRP), :]).then_inc(staged[h_], 16)

            for q in range(4):
                sp.wait_ge(addresses, q + 1)
                if q == 0:
                    for h_ in (0, 1):
                        stage(0, h_)
                with sp.Fori(max(SEGMENTS[q], 1), SEGMENTS[q + 1]) as g:
                    for h_ in (0, 1):
                        sp.wait_ge(scattered[h_], g * (16 * SGRP))
                        stage(g, h_)
            for h_ in (0, 1):
                sp.wait_ge(scattered[h_], SPAIRS * 16 * SGRP)
            sp.dma_start(recs[:, :, :].rearrange("p t f -> p (t f)"), tab).then_inc(table_loaded, 16)
            sp.wait_ge(idx_ready, 1)
            rounds = sp.value_load(rounds_i[0:1, 0:1], min_val=2, max_val=MAX_ROUNDS)
            for half in (0, 1):
                sp.dma_start(gather_idx[:, half, :], idx[:, half * HALF:(half + 1) * HALF]).then_inc(idx_staged[half], 16)
            with sp.Fori(0, rounds) as r:
                for q in range(RING // SUB):
                    sp.wait_ge(gathered[q], (r + 1) * (16 * SUB))
                    sp.sem_inc(rows_ready, SUB)
                    if (q + 1) * SUB % HALF == 0:
                        half = q * SUB // HALF
                        sp.dma_start(gather_idx[:, half, :],
                                     idx[:, bass.ds((r + 1) * RING + half * HALF, HALF)]).then_inc(idx_staged[half], 16)
            for half in (0, 1):
                sp.wait_ge(idx_staged[half], (rounds + 1) * 16)
                sp.sem_inc(pool_go, 1)

        @block.scalar
        def _(act):
            n = [0]

            def link(ins):
                ins.then_inc(act_chain, 1)
                n[0] += 1
                act.wait_ge(act_chain, n[0])

            def x_rows(a, i):
                return a[bass.ds(i * CW, CW), :].rearrange("(t p) d -> p t d", p=P)

            for s_ in (hT_ready, xm_ready, yT_ready, hid_ready, h1_ready, h2r_ready, ys_ready):
                act.sem_inc(s_, 1)
            for s_ in (*axn_stored, *xm_stored, *out_stored, xo_stored):
                act.sem_inc(s_, 16)
            np_ = 0
            small = [(lnp[:, 0, :], ln1_w), (lnp[:, 1, :], ln1_b), (lnp[:, 2, :], ln2_w), (lnp[:, 3, :], ln2_b),
                     (bx_s[:, :], bx), (b1_s[:, :], b1), (bo_row[0:1, :], bo), (b2_row[0:1, :], b2),
                     (br_row[0:1, :], br), (ebo_s[:, :], ebo),
                     (wx_s[:, :, :], wx_t.rearrange("(k p) m -> p k m", p=P)),
                     (wo_s[:, :, :], wo_t.rearrange("(k p) m -> p k m", p=P)),
                     (w1_s[:, :, :], w1_t.rearrange("(k p) m -> p k m", p=P)),
                     (w2_s[:, :, :], w2_t.rearrange("(k p) m -> p k m", p=P)),
                     (wr_s[:, :, :], wr.rearrange("(k p) m -> p k m", p=P))]
            small += [(bnp[:, k, :], a) for k, a in enumerate((eb1, eg1, ebe1, em1, ev1, eb2, eg2, ebe2, em2, ev2))]
            act.dma_start(xa[0][:, :, :], x_rows(x, 0)).then_inc(ax[0], 16)
            for t, a in small:
                act.dma_start(t, a).then_inc(params, 16)
                np_ += 1
            act.wait_ge(diag_zero, 2)
            for g in range(P // HD):
                s_ = slice(g * HD, (g + 1) * HD)
                for t, a in ((bdq[s_, s_], wq_t), (bdkv[s_, 0, s_], wk_t), (bdkv[s_, 1, s_], wv_t)):
                    act.dma_start(t, a).then_inc(params, 16)
                    np_ += 1
            assert np_ == N_PARAMS
            act.wait_ge(params, 16 * np_)
            act.wait_ge(bn_var, 1)
            nc.scalar.activation(bn_w[:, 0, :], bnp[:, 4, :], ACT.Sqrt, bias=eps_bn[:, 0:1])
            nc.scalar.activation(bn_w[:, 1, :], bnp[:, 9, :], ACT.Sqrt, bias=eps_bn[:, 0:1]).then_inc(bn_sd, 1)

            def a_step(i, b, it, nt):
                w = nt * P
                if nt == CT:
                    act.wait_ge(ax_free, i + 1)
                    nb = 1 - b
                    act.dma_start(xa[nb][:, :, :], x_rows(x, i + 1)).then_inc(ax[nb], 16)
                for k in (0, 1):
                    act.wait_ge(ax_stats, 2 * i + k + 1)
                    nc.scalar.activation(sd[:, 0:nt], mv[:, 0:nt, 1], ACT.Sqrt, bias=eps_ln[:, 0:1]).then_inc(ax_sd, 1)
                    if k == 0:
                        act.wait_ge(axn, i + 1)
                        act.dma_start(xn_rows[bass.ds(i * CW, w), :].rearrange("(t p) d -> p t d", p=P),
                                      xa_n[b][:, 0:nt, :]).then_inc(axn_stored[b], 16)
                act.wait_ge(hn_T, i + 2)
                for f in range(KF):
                    ins = nc.scalar.activation(hT[:, f, 0:w], ps[:, f, 0:w], ACT.Identity,
                                               scale=lnp[:, 0, f:f + 1], bias=lnp[:, 1, f:f + 1])
                ins.then_inc(hT_ready, 1)
                act.wait_ge(xm_ps, i + 1)
                act.wait_ge(xm_stored[b], 16 * (it + 1))
                for f in range(KF):
                    ins = nc.scalar.activation(xmT[b][:, f, 0:w], ps[:, 2 + f, 0:w], ACT.Identity, bias=bx_s[:, f:f + 1])
                ins.then_inc(xm_ready, 1)
                act.wait_ge(xm_ready, i + 2)
                act.dma_start(xmid_d[bass.ds(i * P, P), :].rearrange("p (f w) -> p f w", f=KF)[:, :, 0:w],
                              xmT[b][:, :, 0:w]).then_inc(xm_stored[b], 16)

            act.wait_ge(zeroed, 16 * 7)
            mixer_chunks(act, a_step)
            act.wait_ge(mrow_ps, 1)
            nc.scalar.activation(mrow[0:1, :, :], ps[0:1, 6, 0:KF * P].rearrange("p (f c) -> p f c", f=KF), ACT.Copy,
                                 scale=-1.0).then_inc(mrow_ready, 1)
            for b in (0, 1):
                act.wait_ge(xm_stored[b], 16 * (FULL // 2 + 2 - b))

            act.wait_ge(addresses, 4)
            for k, a in enumerate((ew1, ew2, ewo)):
                act.dma_start(ew_s[:, k, :, :, :].rearrange("p e k h -> p (e k) h"),
                              a.rearrange("e (k p) h -> p (e k) h", p=P)).then_inc(ew_loaded, 16)

            def load_mid(i, b, s_):
                act.dma_start(xmT[b][:, :, :].rearrange("p f w -> p (f w)"), xmid_d[bass.ds(i * P, P), :]).then_inc(s_[b], 16)

            act.wait_ge(k_ps, CHUNKS)
            load_mid(0, 0, kx)
            act.sem_inc(ek_ready, 2)

            def k_step(i, b, it, nt):
                if nt == CT:
                    act.wait_ge(kv_ps, i * CT + 1)
                    load_mid(i + 1, 1 - b, kx)
                for j in range(nt):
                    t = i * CT + j
                    act.wait_ge(kv_ps, t + 2)
                    act.wait_ge(kv_added, t + 1)
                    nc.scalar.activation(ek[:, j % 2, :, :],
                                         ps[:, j % 2, 0:KF * P].rearrange("p (f c) -> p f c", f=KF),
                                         ACT.Exp).then_inc(ek_ready, 1)

            mixer_chunks(act, k_step)
            act.wait_ge(kvw_ps, 1)
            for f in range(KF):
                ins = nc.scalar.activation(kvw[:, f, :], ps[:, 4 + f, 0:D], ACT.Copy, scale=rk[:, f:f + 1])
            ins.then_inc(kvw_ready, 1)

            def b_load(i, b):
                load_mid(i, b, bx_in)
                act.dma_start(xb_n[b][:, :, :], x_rows(xn_rows, i)).then_inc(bx_in[b], 16)
                act.dma_start(xb[b][:, :, :], x_rows(x, i)).then_inc(bx_in[b], 16)

            def q_exps(i, b):
                act.wait_ge(q_shift, i + 1)
                nc.scalar.activation(qx[:, :, :], qx[:, :, :], ACT.Exp).then_inc(q_exp, 1)

            def q_evac(i, b):
                act.wait_ge(q_T, i + 1)
                for f in range(KF):
                    ins = nc.scalar.activation(qT[:, f, :], ps[:, 2 + f, :], ACT.Copy)
                ins.then_inc(qT_ready, 1)

            def y_sqrt(i, b):
                act.wait_ge(y_stats, i + 1)
                nc.scalar.activation(sd[:, :], mv[:, :, 1], ACT.Sqrt, bias=eps_ln[:, 0:1]).then_inc(y_sd, 1)

            def y_evac(i, b):
                act.wait_ge(y_T, i + 1)
                for f in range(KF):
                    ins = nc.scalar.activation(yT[b][:, f, :], ps[:, 2 + f, :], ACT.Identity,
                                               scale=lnp[:, 2, f:f + 1], bias=lnp[:, 3, f:f + 1])
                ins.then_inc(yT_ready, 1)

            def gelus(i, w, m0, m1):
                for m in range(m0, m1):
                    act.wait_ge(hid_ps, i * HM + m + 1)
                    nc.scalar.activation(gT[:, m, 0:w], ps[:, 4 + m % 2, 0:w], ACT.Gelu,
                                         bias=b1_s[:, m:m + 1]).then_inc(hid_ready, 1)

            def store_xm(i, b, nt):
                act.wait_ge(xo_ready, i + 2)
                act.dma_start(xm_rows[bass.ds(i * CW, nt * P), :].rearrange("(t p) d -> p t d", p=P),
                              xb[b][:, 0:nt, :]).then_inc(xo_stored, 16)

            act.wait_ge(kv_ps, TILES + 1)
            for b in (0, 1):
                act.wait_ge(axn_stored[b], 16 * (FULL // 2 + 2 - b))
            act.wait_ge(hn_ready, CHUNKS)
            b_load(0, 0)

            def b_first():
                for part in (q_exps, q_evac, y_sqrt, y_evac):
                    part(0, 0)

            def b_step(i, b, it):
                act.wait_ge(xo_stored, i * 16 + 16)
                act.wait_ge(at_ps, i + 1)
                b_load(i + 1, 1 - b)
                q_exps(i + 1, 1 - b)
                gelus(i, CW, 0, HM // 2)
                q_evac(i + 1, 1 - b)
                gelus(i, CW, HM // 2, HM)
                y_sqrt(i + 1, 1 - b)
                y_evac(i + 1, 1 - b)
                store_xm(i, b, CT)

            def b_last(i, b, it):
                gelus(i, TAIL_T * P, 0, HM)
                store_xm(i, b, TAIL_T)

            ahead(act, b_first, b_step, b_last)
            act.wait_ge(xo_stored, 16 * (CHUNKS + 1))

            act.wait_ge(mix_done, 2)
            act.dma_start(cx[:, :, :], x_rows(xm_rows, 0)).then_inc(cx_in, 16)

            def c_sqrt(i):
                act.wait_ge(x1_ready, i + 1)
                nc.scalar.activation(c_sdt[:, :], c_mv[:, :, 1], ACT.Sqrt, bias=eps_ln[:, 0:1]).then_inc(c_sd, 1)

            def x2_evac(i, b):
                act.wait_ge(x2_T, i + 1)
                for f in range(KF):
                    ins = nc.scalar.activation(x2T[b][:, f, :], ps[:, f, :], ACT.Copy)
                ins.then_inc(x2T_ready, 1)

            def r_exps(i):
                act.wait_ge(r_shift, i + 1)
                nc.scalar.activation(rt[:, :, :], rt[:, :, :], ACT.Exp).then_inc(r_exp, 1)

            def experts(i, b, nt, between=None):
                w = nt * P
                act.wait_ge(w_T, i + 1)
                nc.scalar.activation(wT[b][:, 0:w], ps[0:EXP, 1, 0:w], ACT.Copy).then_inc(wT_ready, 1)

                def relu1(e):
                    for m in range(KF):
                        act.wait_ge(z1_ps, (i * EXP + e) * KF + m + 1)
                        c = e * KF + m
                        nc.scalar.activation(h1[:, e % 2, m, 0:w], ps[:, m, 0:w], ACT.Relu, scale=bn_s[:, 0, c:c + 1],
                                             bias=bn_t[:, 0, c:c + 1]).then_inc(h1_ready, 1)

                def relu2(e):
                    for m in range(KF):
                        act.wait_ge(z2_ps, (i * EXP + e) * KF + m + 1)
                        act.wait_ge(h2_ready, (i * EXP + e) * KF + m + 2)
                        c = e * KF + m
                        nc.scalar.activation(h2r[:, m, 0:w], ps[:, 2 + m, 0:w], ACT.Relu, scale=bn_s[:, 1, c:c + 1],
                                             bias=bn_t[:, 1, c:c + 1]).then_inc(h2r_ready, 1)

                relu1(0)
                for e in range(EXP):
                    if e + 1 < EXP:
                        relu1(e + 1)
                    relu2(e)
                    if e == 1 and between:
                        between()
                act.wait_ge(y_ps, i + 1)
                for f in range(KF):
                    ins = nc.scalar.activation(ys[:, f, 0:w], ps[:, 4 + f, 0:w], ACT.Copy)
                ins.then_inc(ys_ready, 1)

            def c_first():
                c_sqrt(0)
                x2_evac(0, 0)
                r_exps(0)

            def c_step(i, b, it):
                act.wait_ge(x1_ready, i + 1)
                act.dma_start(cx[:, :, :], x_rows(xm_rows, i + 1)).then_inc(cx_in, 16)
                experts(i, b, CT, between=lambda: c_sqrt(i + 1))
                x2_evac(i + 1, 1 - b)
                r_exps(i + 1)
                act.wait_ge(xout_ready, i + 2)
                act.dma_start(x_rows(out, i), xout[b][:, :, :]).then_inc(out_stored[b], 16)

            def c_last(i, b, it):
                experts(i, b, TAIL_T)
                act.wait_ge(xout_ready, i + 2)
                act.dma_start(out[FULL * CW:N, :], xout[b][0:TAIL_ROWS, 0, :]).then_inc(out_stored[b], 16)

            ahead(act, c_first, c_step, c_last)
            for b in (0, 1):
                act.wait_ge(out_stored[b], 16 * (FULL // 2 + 2 - b))

        @block.tensor
        def _(pe):
            mm = nc.tensor.matmul

            pe.sem_inc(hn_T, 1)
            pe.sem_inc(kv_ps, 1)
            pe.wait_ge(consts, 9)
            pe.wait_ge(counts_done, 1)
            mm(ps[:, 6, 0:BLOCKS], ones[:, :], cnt[:, 0:BLOCKS], start=True, stop=True)
            mm(ps[:, 7, 0:BLOCKS], lower[:, :], cnt[:, 0:BLOCKS], start=True, stop=True).then_inc(count_sums, 1)
            pe.wait_ge(params, 16 * N_PARAMS)

            def a_step(i, b, it, nt):
                w = nt * P
                pe.wait_ge(hn_ready, i + 1)
                pe.wait_ge(hT_ready, i + 1)
                for j in range(nt):
                    for f in range(KF):
                        ins = nc.tensor.transpose(ps[:, f, j * P:(j + 1) * P], hn[:, j, f * P:(f + 1) * P], ident[:, :])
                ins.then_inc(hn_T, 1)
                pe.wait_ge(hT_ready, i + 2)
                pe.wait_ge(xm_ready, i + 1)
                for m in range(KF):
                    for k in range(KF):
                        ins = mm(ps[:, 2 + m, 0:w], wx_s[:, k, m * P:(m + 1) * P], hT[:, k, 0:w], start=k == 0, stop=k == KF - 1)
                ins.then_inc(xm_ps, 1)
                pe.wait_ge(xm_ready, i + 2)
                pe.wait_ge(k_max, i + 1)
                for f in range(KF):
                    ins = mm(ps[:, 4 + f, 0:w], bdkv[:, 0, :], xmT[b][:, f, 0:w], start=True, stop=True)
                ins.then_inc(k_ps, 1)

            mixer_chunks(pe, a_step)
            pe.wait_ge(k_max, CHUNKS + 2)
            for f in range(KF):
                ins = nc.tensor.transpose(ps[0:1, 6, f * P:(f + 1) * P], kmax[:, f:f + 1], ident[:, :])
            ins.then_inc(mrow_ps, 1)

            pe.wait_ge(mrow_ready, 1)
            for f in range(KF):
                mm(ps[:, 2 + f, 0:P + 1], zero_row[0:1, 0:P], zero_row[0:1, 0:P + 1], start=True, stop=False)
            pe.sem_inc(kv_added, 2)

            def k_step(i, b, it, nt):
                pe.wait_ge(kx[b], 16 * (it + 1))

                def logits(j):
                    t = i * CT + j
                    pe.wait_ge(ek_ready, t + 1)
                    pe.wait_ge(vv_ready, t + 1)
                    for f in range(KF):
                        x_, o = xmT[b][:, f, j * P:(j + 1) * P], slice(f * P, (f + 1) * P)
                        mm(ps[:, j % 2, o], x_, bdkv[:, 0, :], start=True, stop=False)
                        mm(ps[:, j % 2, o], ones[0:1, :], mrow[0:1, f, :], start=False, stop=True)
                        ins = mm(ps[:, 4 + j % 2, o], x_, bdkv[:, 1, :], start=True, stop=True)
                    ins.then_inc(kv_ps, 1)

                def add(j):
                    t = i * CT + j
                    rows_ = P if nt == CT else TAIL_ROWS
                    pe.wait_ge(ek_ready, t + 3)
                    pe.wait_ge(vv_ready, t + 3)
                    for f in range(KF):
                        mm(ps[:, 2 + f, 0:P], vv[0:rows_, j % 2, f, :], ek[0:rows_, j % 2, f, :], start=False, stop=False)
                        ins = mm(ps[:, 2 + f, P:P + 1], ek[0:rows_, j % 2, f, :], ones[0:rows_, 0:1], start=False, stop=False)
                    ins.then_inc(kv_added, 1)

                logits(0)
                for j in range(nt):
                    if j + 1 < nt:
                        logits(j + 1)
                    add(j)

            mixer_chunks(pe, k_step)
            for f in range(KF):
                ins = mm(ps[:, 2 + f, 0:P + 1], zero_row[0:1, 0:P], zero_row[0:1, 0:P + 1], start=False, stop=True)
            ins.then_inc(kv_added, 1)
            pe.wait_ge(kvT_ready, 1)
            for f in range(KF):
                ins = mm(ps[:, 4 + f, 0:D], kvT[:, f, :], wo_s[:, f, :], start=True, stop=True)
            ins.then_inc(kvw_ps, 1)
            pe.wait_ge(kvw_ready, 1)

            def queries(i, b):
                pe.wait_ge(bx_in[b], (i + 2 - b) * 24)
                pe.wait_ge(h_ready, i + 1)
                for j in range(CT):
                    for f in range(KF):
                        ins = mm(tile(0, j)[:, f * P:(f + 1) * P], xmT[b][:, f, j * P:(j + 1) * P], bdq[:, :], start=True, stop=True)
                ins.then_inc(q_ps, 1)

            def turn_q(i, b):
                pe.wait_ge(q_norm, i + 1)
                pe.wait_ge(yT_ready, i + 1)
                for j in range(CT):
                    for f in range(KF):
                        ins = nc.tensor.transpose(ps[:, 2 + f, j * P:(j + 1) * P], qx[:, j, f * P:(f + 1) * P], ident[:, :])
                ins.then_inc(q_T, 1)

            def attend(i, b):
                pe.wait_ge(qT_ready, i + 1)
                for j in range(CT):
                    for f in range(KF):
                        mm(tile(0, j), qT[:, f, j * P:(j + 1) * P], kvw[:, f, :], start=f == 0, stop=False)
                    ins = mm(tile(0, j), ones[0:1, :], bo_row[0:1, :], start=False, stop=True)
                ins.then_inc(at_ps, 1)

            def turn_y(i, b):
                pe.wait_ge(y_ready, i + 1)
                for j in range(CT):
                    for f in range(KF):
                        ins = nc.tensor.transpose(ps[:, 2 + f, j * P:(j + 1) * P], yn[:, j, f * P:(f + 1) * P], ident[:, :])
                ins.then_inc(y_T, 1)

            def hidden(i, b, w, m0, m1):
                for m in range(m0, m1):
                    if m < 2:
                        pe.wait_ge(hid_ready, i * HM + 1)
                    else:
                        pe.wait_ge(hid_ready, i * HM + m)
                    for k in range(KF):
                        ins = mm(ps[:, 4 + m % 2, 0:w], w1_s[:, k, m * P:(m + 1) * P], yT[b][:, k, 0:w], start=k == 0, stop=k == KF - 1)
                    ins.then_inc(hid_ps, 1)

            def down(i, b, nt):
                pe.wait_ge(xo_ready, i + 1)
                for j in range(nt):
                    for m in range(HM):
                        if j == 0:
                            pe.wait_ge(hid_ready, i * HM + m + 2)
                        mm(tile(6, j), gT[:, m, j * P:(j + 1) * P], w2_s[:, m, :], start=m == 0, stop=False)
                    ins = mm(tile(6, j), ones[0:1, :], b2_row[0:1, :], start=False, stop=True)
                ins.then_inc(mlp_ps, 1)

            def b_first():
                for part in (queries, turn_q, attend, turn_y):
                    part(0, 0)

            def b_step(i, b, it):
                queries(i + 1, 1 - b)
                pe.wait_ge(yT_ready, i + 2)
                hidden(i, b, CW, 0, HM // 2)
                turn_q(i + 1, 1 - b)
                hidden(i, b, CW, HM // 2, HM)
                attend(i + 1, 1 - b)
                down(i, b, CT)
                turn_y(i + 1, 1 - b)

            def b_last(i, b, it):
                pe.wait_ge(yT_ready, i + 2)
                hidden(i, b, TAIL_T * P, 0, HM)
                down(i, b, TAIL_T)

            ahead(pe, b_first, b_step, b_last)

            pe.wait_ge(mix_done, 2)
            pe.wait_ge(idx_ready, 1)
            pe.sem_inc(tiles_used, 2)

            def segment_sums(i, first=False):
                if not first:
                    pe.wait_ge(x1_ready, i)
                    pe.wait_ge(h2_ready, (i - 1) * (EXP * KF) + 3)
                bounds = [pe.value_load(pair_i[0:1, bass.ds(i * CT + k, 1)], min_val=0, max_val=MAX_PAIRS) for k in range(CT + 1)]
                for k in range(CT):
                    mm(tile(6, k), zero_row[0:1, 0:P], zero_row[0:1, 0:D], start=True, stop=False)
                    with pe.Fori(bounds[k], bounds[k + 1]) as q:
                        for t in (0, 1):
                            pe.wait_ge(rows_ready, q * 2 + t + 1)
                            pe.wait_ge(select_ready, q * 2 + t + 1)
                            mm(tile(6, k), select[:, t, :], ring[:, bass.ds((q % HALF) * 2 + t, 1), :],
                               start=False, stop=False).then_inc(tiles_used, 1)
                    ins = mm(tile(6, k), zero_row[0:1, 0:P], zero_row[0:1, 0:D], start=False, stop=True)
                ins.then_inc(block_sums, 1)

            def turn_x2(i, b):
                pe.wait_ge(x2_ready, i + 1)
                pe.wait_ge(h1_ready, i * (EXP * KF) + 1)
                for j in range(CT):
                    for f in range(KF):
                        ins = nc.tensor.transpose(ps[:, f, j * P:(j + 1) * P], x2n[:, j, f * P:(f + 1) * P], ident[:, :])
                ins.then_inc(x2_T, 1)

            def router(i, b):
                pe.wait_ge(x2T_ready, i + 1)
                for j in range(CT):
                    o = ps[:, 0, j * EXP:(j + 1) * EXP]
                    for f in range(KF):
                        mm(o, x2T[b][:, f, j * P:(j + 1) * P], wr_s[:, f, :], start=f == 0, stop=False)
                    ins = mm(o, ones[0:1, :], br_row[0:1, :], start=False, stop=True)
                ins.then_inc(r_ps, 1)

            def turn_w(i, b, nt):
                pe.wait_ge(w_ready, i + 1)
                for j in range(nt):
                    ins = nc.tensor.transpose(ps[0:EXP, 1, j * P:(j + 1) * P], rt[:, j, :], ident[:, :])
                ins.then_inc(w_T, 1)

            def experts(i, b, nt):
                w = nt * P
                pe.wait_ge(wT_ready, i + 1)
                pe.wait_ge(ys_ready, i + 1)
                for m in range(KF):
                    mm(ps[:, 4 + m, 0:w], ebo_s[:, m * P:(m + 1) * P], wT[b][:, 0:w], start=True, stop=False)

                def share(e):
                    pe.wait_ge(h2_ready, (i * EXP + e) * KF + 1)
                    mm(ps[:, 6 + e % 2, 0:w], pick[:, e, :], wT[b][:, 0:w], start=True, stop=True).then_inc(wb_ps, 1)

                def layer(n_, e, src_, bank, done, ready, own):
                    pe.wait_ge(ready, own + 1)
                    for m in range(KF):
                        for k in range(KF):
                            ins = mm(ps[:, bank + m, 0:w], ew_s[:, n_, e, k, m * P:(m + 1) * P], src_(k), start=k == 0, stop=k == KF - 1)
                        ins.then_inc(done, 1)

                def first(e):
                    layer(0, e, lambda k: x2T[b][:, k, 0:w], 0, z1_ps, h1_ready, (i * EXP + e) * KF)

                def second(e):
                    pe.wait_ge(h2r_ready, (i * EXP + e) * KF + 1)
                    layer(1, e, lambda k: h1[:, e % 2, k, 0:w], 2, z2_ps, h1_ready, (i * EXP + e + 1) * KF)

                def third(e):
                    pe.wait_ge(h2_ready, (i * EXP + e + 1) * KF + 3)
                    for m in range(KF):
                        for k in range(KF):
                            ins = mm(ps[:, 4 + m, 0:w], ew_s[:, 2, e, k, m * P:(m + 1) * P], h2[:, e % 2, k, 0:w],
                                     start=False, stop=e == EXP - 1 and k == KF - 1)
                    if e == EXP - 1:
                        ins.then_inc(y_ps, 1)

                first(0)
                for e in range(EXP):
                    share(e)
                    if e + 1 < EXP:
                        first(e + 1)
                    second(e)
                    if e:
                        third(e - 1)
                third(EXP - 1)

            def turn_back(i, b, nt):
                pe.wait_ge(ys_ready, i + 2)
                pe.wait_ge(h2r_ready, (i + 1) * (EXP * KF) + 1)
                for j in range(nt):
                    for f in range(KF):
                        ins = nc.tensor.transpose(tile(2, j)[:, f * P:(f + 1) * P], ys[:, f, j * P:(j + 1) * P], ident[:, :])
                ins.then_inc(y_back, 1)

            def c_first():
                segment_sums(0, first=True)
                turn_x2(0, 0)
                router(0, 0)
                pe.wait_ge(ew_loaded, 16 * 3)
                pe.wait_ge(bn_ready, 2)

            def c_step(i, b, it):
                segment_sums(i + 1)
                turn_w(i, b, CT)
                pe.wait_ge(r_shift, i + 1)
                pe.wait_ge(x1_ready, i + 2)
                pe.wait_ge(xout_ready, i + 1)
                experts(i, b, CT)
                turn_x2(i + 1, 1 - b)
                turn_back(i, b, CT)
                router(i + 1, 1 - b)

            def c_last(i, b, it):
                turn_w(i, b, TAIL_T)
                pe.wait_ge(r_shift, i + 1)
                pe.wait_ge(xout_ready, i + 1)
                experts(i, b, TAIL_T)
                turn_back(i, b, TAIL_T)

            ahead(pe, c_first, c_step, c_last)

        @block.vector
        def _(v):
            V = nc.vector
            here = {"base": 0, "n": 0}

            def link(ins):
                ins.then_inc(dve_chain, 1)
                here["n"] += 1
                v.wait_ge(dve_chain, here["base"] + here["n"])

            def mark(ins):
                ins.then_inc(dve_chain, 1)
                here["n"] += 1
                return here["base"] + here["n"]

            V.memset(src_i[:, :], TILES * P - 1).then_inc(pad_set, 1)
            V.memset(dst_i[:, :], 0).then_inc(pad_set, 1)
            V.memset(w_e[:, :], 0.0).then_inc(pad_set, 1)
            V.memset(bdq[:, :], 0.0).then_inc(diag_zero, 1)
            V.memset(bdkv[:, :, :], 0.0).then_inc(diag_zero, 1)
            V.memset(rec[:, :, 3], 0.0)
            V.memset(zeros[:, :], 0.0).then_inc(recs_zero, 1)
            V.memset(zero_row[:, :], 0.0)
            V.memset(eps_ln[:, :], LN_EPS)
            link(V.memset(eps_bn[:, :], BN_EPS))
            v.sem_inc(bn_var, 1)
            v.sem_inc(h2_ready, 3)
            for s_ in (k_max, h_ready, xo_ready, xout_ready):
                v.sem_inc(s_, 1)
            v.sem_inc(vv_ready, 2)
            v.sem_inc(ax_free, 1)

            v.wait_ge(edges_loaded, 96)
            link(V.tensor_scalar(blk_i[:, :], src_i[:, :], 7, None, ALU.arith_shift_right))
            V.tensor_copy(blk[:, :], blk_i[:, :])
            link(V.tensor_scalar(adr[:, :], src_i[:, :], P - 1, None, ALU.bitwise_and))
            V.tensor_copy(rec[:, :, 1], adr[:, :])
            V.tensor_copy(rec[:, :, 0], dst_i[:, :])
            link(V.tensor_copy(rec[:, :, 2], w_e[:, :]))
            for k in range(BLOCKS):
                ins = V.tensor_scalar(mask[:, k, :], blk[:, :], float(k), 0.0, ALU.is_equal, ALU.add, accum_out=cnt[:, k:k + 1])
            ins.then_inc(counts_done, 1)
            v.wait_ge(count_sums, 1)
            link(V.tensor_scalar(tot_i[:, :], ps[:, 6, 0:BLOCKS], float(PAIR - 1), None, ALU.add))
            link(V.tensor_scalar(tot_i[:, :], tot_i[:, :], 8, None, ALU.arith_shift_right))
            link(V.tensor_copy(pairs_f[:, 0:BLOCKS], tot_i[:, :]))
            link(V.tensor_scalar(pairs_f[:, 0:BLOCKS], pairs_f[:, 0:BLOCKS], 1.0, None, ALU.max))
            V.memset(pair_x[:, 0:1], 0.0)
            link(V.tensor_tensor_scan(pair_x[:, 1:BLOCKS + 1], pairs_f[:, 0:BLOCKS], pairs_f[:, 0:BLOCKS], 0.0, ALU.add, ALU.bypass))
            V.tensor_copy(pair_i[:, :], pair_x[:, :])
            link(V.tensor_scalar(rounds_i[:, :], pair_x[:, BLOCKS:BLOCKS + 1], 2.0, float(RING - 1), ALU.mult, ALU.add))
            link(V.tensor_scalar(rounds_i[:, :], rounds_i[:, :], 5, None, ALU.arith_shift_right))
            link(V.tensor_scalar(base[:, 0:BLOCKS], pair_x[:, 0:BLOCKS], float(PAIR), -1.0, ALU.mult, ALU.add))
            link(V.tensor_tensor(base[:, 0:BLOCKS], base[:, 0:BLOCKS], ps[:, 7, 0:BLOCKS], ALU.add))
            for s_ in range(4):
                a, z = (2 * SGRP * g for g in SEGMENTS[s_:s_ + 2])
                picked = []
                for k in range(BLOCKS + 1):
                    if k < BLOCKS:
                        if k >= 2:
                            v.wait_ge(dve_chain, picked[k - 2])
                        ranked = mark(V.tensor_tensor_scan(rank[:, k % 2, a:z], mask[:, k, a:z], zeros[:, a:z],
                                                           base[:, k:k + 1], ALU.add, ALU.add))
                    if k:
                        v.wait_ge(dve_chain, before if k < BLOCKS else picked[-1])
                        V.tensor_copy(base[:, k - 1:k], rank[:, (k - 1) % 2, z - 1:z])
                        picked.append(mark(V.copy_predicated(pos[:, a:z], mask[:, k - 1, a:z], rank[:, (k - 1) % 2, a:z])))
                        if k == BLOCKS:
                            v.wait_ge(dve_chain, picked[-1])
                    before = ranked
                link(V.tensor_copy(pos_i[:, a:z], pos[:, a:z]))
                link(V.tensor_scalar(blk_i[:, a:z], pos_i[:, a:z], 7, None, ALU.arith_shift_right))
                V.tensor_copy(blk[:, a:z], blk_i[:, a:z])
                link(V.tensor_scalar(pos_i[:, a:z], pos_i[:, a:z], P - 1, None, ALU.bitwise_and))
                link(V.tensor_copy(pos[:, a:z], pos_i[:, a:z]))
                link(V.scalar_tensor_tensor(out=adr[:, a:z], in0=pos[:, a:z], scalar=float(TT), in1=blk[:, a:z],
                                            op0=ALU.mult, op1=ALU.add))
                v.sem_inc(addresses, 1)

            v.wait_ge(bn_sd, 1)
            for k in (0, 1):
                b_, g_, be_, m_ = (bnp[:, 5 * k + q, :] for q in range(4))
                link(V.reciprocal(bn_w[:, k, :], bn_w[:, k, :]))
                link(V.tensor_tensor(bn_s[:, k, :], bn_w[:, k, :], g_, ALU.mult))
                link(V.tensor_tensor(bn_t[:, k, :], b_, m_, ALU.subtract))
                link(V.tensor_tensor(bn_t[:, k, :], bn_t[:, k, :], bn_s[:, k, :], ALU.mult))
                link(V.tensor_tensor(bn_t[:, k, :], bn_t[:, k, :], be_, ALU.add))
            v.sem_inc(bn_ready, 2)
            link(V.memset(kmax[:, :], -3.0e38))

            def looped(run, step, per):
                start = here["base"] + here["n"]

                def counted(i, *rest):
                    here["base"], here["n"] = start + i * per, 0
                    step(i, *rest)
                    assert here["n"] == per, here["n"]

                run(v, counted)
                here["base"], here["n"] = start + CHUNKS * per, 0

            def row_stats(src_, nt, st_, mv_, done_):
                for j in range(nt):
                    ins = V.bn_stats(st_[:, j, :], src_[:, j, :])
                link(ins)
                v.sem_inc(dve_go, 1)
                for j in range(nt):
                    ins = V.bn_aggr(mv_[:, j, :], st_[:, j, :])
                ins.then_inc(done_, 1)

            def normalize(dst_, src_, nt, mv_, sd_, rstd_):
                link(V.reciprocal(rstd_[:, 0:nt], sd_[:, 0:nt]))
                for j in range(nt):
                    ins = V.tensor_scalar(dst_[:, j, :], src_[:, j, :], mv_[:, j, 0:1], rstd_[:, j:j + 1], ALU.subtract, ALU.mult)
                return ins

            def a_step(i, b, it, nt):
                v.wait_ge(ax[b], 16 * (it + 1))
                row_stats(xa[b], nt, stats, mv, ax_stats)
                v.wait_ge(ax_sd, 2 * i + 1)
                v.wait_ge(axn_stored[b], 16 * (it + 1))
                normalize(xa_n[b], xa[b], nt, mv, sd, rstd).then_inc(axn, 1)
                v.wait_ge(axn, i + 1)
                v.sem_inc(ax_free, 1)
                row_stats(xa_n[b], nt, stats, mv, ax_stats)
                v.wait_ge(ax_sd, 2 * i + 2)
                v.wait_ge(hn_T, i + 1)
                normalize(hn, xa_n[b], nt, mv, sd, rstd).then_inc(hn_ready, 1)
                w = CW if nt == CT else TAIL_ROWS
                v.wait_ge(k_ps, i + 1)
                ins = V.tensor_reduce(kchunk[:, :], ps[:, 4:6, 0:w], AX.X, ALU.max)
                link(ins)
                V.tensor_tensor(kmax[:, :], kmax[:, :], kchunk[:, :], ALU.max).then_inc(k_max, 1)
                v.wait_ge(k_max, i + 2)

            looped(mixer_chunks, a_step, 5)
            v.sem_inc(k_max, 1)

            def k_step(i, b, it, nt):
                for j in range(nt):
                    t = i * CT + j
                    v.wait_ge(kv_ps, t + 2)
                    v.wait_ge(kv_added, t + 1)
                    V.tensor_copy(vv[:, j % 2, :, :], ps[:, 4 + j % 2, 0:KF * P].rearrange("p (f c) -> p f c", f=KF)).then_inc(vv_ready, 1)

            looped(mixer_chunks, k_step, 0)
            v.wait_ge(kv_added, TILES + 3)
            for f in range(KF):
                V.tensor_tensor(kvT[:, f, :], ps[:, 2 + f, 0:P], head_mask[:, :], ALU.mult)
            V.reciprocal(rk[:, :], ps[:, 2:4, P]).then_inc(kvT_ready, 1)

            groups = CT * HEADS

            def q_softmax(i, b):
                q = ps[:, 0:2, :].rearrange("p a (g s) -> p (a g) s", s=HD)
                e = qx[:, :, :].rearrange("p t (g s) -> p (t g) s", s=HD)
                v.wait_ge(q_ps, i + 1)
                link(V.tensor_reduce(qmax[:, :], q, AX.X, ALU.max))
                V.tensor_tensor(e, q, qmax[:, :].unsqueeze(2).to_broadcast([P, groups, HD]), ALU.subtract).then_inc(q_shift, 1)
                v.wait_ge(q_exp, i + 1)
                link(V.tensor_reduce(qsum[:, :], e, AX.X, ALU.add))
                link(V.reciprocal(qsum[:, :], qsum[:, :]))
                V.tensor_tensor(e, e, qsum[:, :].unsqueeze(2).to_broadcast([P, groups, HD]), ALU.mult).then_inc(q_norm, 1)

            def attended(i, b):
                v.wait_ge(at_ps, i + 1)
                link(V.tensor_tensor(h[b][:, :, :], rows(0), xb_n[b][:, :, :], ALU.add))
                v.sem_inc(h_ready, 1)
                row_stats(h[b], CT, stats, mv, y_stats)

            def y_norm(i, b):
                v.wait_ge(y_sd, i + 1)
                normalize(yn, h[b], CT, mv, sd, rstd).then_inc(y_ready, 1)

            def mixed(i, b, nt):
                v.wait_ge(mlp_ps, i + 1)
                xo = xb[b][:, 0:nt, :]
                link(V.tensor_tensor(xo, xo, h[b][:, 0:nt, :], ALU.add))
                V.tensor_tensor(xo, xo, rows(6, nt), ALU.add).then_inc(xo_ready, 1)

            def b_next(i, b):
                q_softmax(i, b)
                attended(i, b)
                y_norm(i, b)

            PER_B = 7

            def b_all(v_, counted):
                start = here["base"] + here["n"]
                here["base"], here["n"] = start, 0
                b_next(0, 0)
                first_n = here["n"]
                loop0 = start + first_n

                def step(i, b, it):
                    here["base"], here["n"] = loop0 + i * PER_B, 0
                    b_next(i + 1, 1 - b)
                    mixed(i, b, CT)
                    assert here["n"] == PER_B, here["n"]

                def last(i, b, it):
                    here["base"], here["n"] = loop0 + i * PER_B, 0
                    mixed(i, b, TAIL_T)

                ahead(v_, lambda: None, step, last)

            b_all(v, None)
            v.wait_ge(xo_ready, CHUNKS + 1)
            v.wait_ge(xo_stored, 16 * (CHUNKS + 1))
            v.wait_ge(hid_ready, CHUNKS * HM + 1)
            v.wait_ge(mlp_ps, CHUNKS)
            v.sem_inc(mix_done, 2)

            v.wait_ge(table_loaded, 16)
            link(V.tensor_copy(idx[:, :], recs[:, :, 0]))
            v.sem_inc(idx_ready, 1)

            def selections(i):
                a = v.value_load(pair_i[0:1, bass.ds(i * CT, 1)], min_val=0, max_val=MAX_PAIRS)
                z = v.value_load(pair_i[0:1, bass.ds(i * CT + CT, 1)], min_val=0, max_val=MAX_PAIRS)
                with v.Fori(a, z) as q:
                    for t in (0, 1):
                        v.wait_ge(tiles_used, q * 2 + t + 1)
                        V.tensor_scalar(select[:, t, :], iota[:, :], recs[:, bass.ds(q * 2 + t, 1), 1],
                                        recs[:, bass.ds(q * 2 + t, 1), 2], ALU.is_equal, ALU.mult).then_inc(select_ready, 1)

            def summed(i, b):
                v.wait_ge(block_sums, i + 1)
                v.wait_ge(cx_in, (i + 1) * 16)
                link(V.tensor_tensor(x1[b][:, :, :], rows(6), cx[:, :, :], ALU.add))
                row_stats(x1[b], CT, c_stats, c_mv, x1_ready)

            def x2_norm(i, b):
                v.wait_ge(c_sd, i + 1)
                normalize(x2n, x1[b], CT, c_mv, c_sdt, c_rstd).then_inc(x2_ready, 1)

            def shares(i):
                v.wait_ge(r_ps, i + 1)
                r = ps[:, 0, 0:CT * EXP].rearrange("p (t e) -> p t e", e=EXP)
                link(V.tensor_reduce(rmax[:, :], r, AX.X, ALU.max))
                V.tensor_tensor(rt[:, :, :], r, rmax[:, :].unsqueeze(2).to_broadcast([P, CT, EXP]), ALU.subtract).then_inc(r_shift, 1)
                v.wait_ge(r_exp, i + 1)
                link(V.tensor_reduce(rmax[:, :], rt[:, :, :], AX.X, ALU.add))
                link(V.reciprocal(rmax[:, :], rmax[:, :]))
                V.tensor_tensor(rt[:, :, :], rt[:, :, :], rmax[:, :].unsqueeze(2).to_broadcast([P, CT, EXP]), ALU.mult).then_inc(w_ready, 1)

            def weigh(i, e, w):
                v.wait_ge(wb_ps, i * EXP + e + 1)
                for m in range(KF):
                    v.wait_ge(h2r_ready, (i * EXP + e) * KF + m + 2)
                    V.tensor_tensor(h2[:, e % 2, m, 0:w], h2r[:, m, 0:w], ps[:, 6 + e % 2, 0:w], ALU.mult).then_inc(h2_ready, 1)

            def finish(i, b, it, nt):
                v.wait_ge(y_back, i + 1)
                v.wait_ge(out_stored[b], 16 * (it + 1))
                V.tensor_tensor(xout[b][:, 0:nt, :], rows(2, nt), x1[b][:, 0:nt, :], ALU.add).then_inc(xout_ready, 1)

            start = here["base"] + here["n"]
            here["base"], here["n"] = start, 0
            selections(0)
            summed(0, 0)
            x2_norm(0, 0)
            shares(0)
            PER_C = here["n"]
            loop0 = start + PER_C

            def c_step(i, b, it):
                here["base"], here["n"] = loop0 + i * PER_C, 0
                selections(i + 1)
                summed(i + 1, 1 - b)
                for e in range(EXP):
                    weigh(i, e, CW)
                    if e == 1:
                        x2_norm(i + 1, 1 - b)
                finish(i, b, it, CT)
                shares(i + 1)
                assert here["n"] == PER_C

            def c_last(i, b, it):
                for e in range(EXP):
                    weigh(i, e, TAIL_T * P)
                finish(i, b, it, TAIL_T)

            ahead(v, lambda: None, c_step, c_last)


N_PARAMS = 25 + 3 * (P // HD)


_OUT = ((N, D), "float32")


def kernel(x, src, dst, edge_weight, L0_mix_ln1_w, L0_mix_ln1_b, L0_mix_Wx, L0_mix_bx, L0_mix_Wq, L0_mix_Wk, L0_mix_Wv,
           L0_mix_Wo, L0_mix_bo, L0_mix_ln2_w, L0_mix_ln2_b, L0_mix_W1, L0_mix_b1, L0_mix_W2, L0_mix_b2, L0_ffn_Wr,
           L0_ffn_br, L0_ffn_W1, L0_ffn_b1, L0_ffn_g1, L0_ffn_be1, L0_ffn_m1, L0_ffn_v1, L0_ffn_W2, L0_ffn_b2,
           L0_ffn_g2, L0_ffn_be2, L0_ffn_m2, L0_ffn_v2, L0_ffn_Wo, L0_ffn_bo):
    import numpy as np
    import concourse.bacc as bacc
    from concourse import mybir as mb
    from concourse.bass_utils import run_bass_kernel_spmd

    def column(a):
        return np.ascontiguousarray(np.asarray(a).reshape(-1, P).T)

    def row(a):
        return np.asarray(a).reshape(1, -1)

    def turned(a):
        return np.ascontiguousarray(np.asarray(a).T)

    padded = np.zeros((ROWS, D), np.float32)
    padded[:N] = np.asarray(x)
    arrays = {
        "x": padded, "src": np.asarray(src), "dst": np.asarray(dst), "edge_weight": np.asarray(edge_weight),
        "ln1_w": column(L0_mix_ln1_w), "ln1_b": column(L0_mix_ln1_b), "wx_t": turned(L0_mix_Wx),
        "bx": column(L0_mix_bx), "wq_t": turned(L0_mix_Wq), "wk_t": turned(L0_mix_Wk), "wv_t": turned(L0_mix_Wv),
        "wo_t": turned(L0_mix_Wo), "bo": row(L0_mix_bo), "ln2_w": column(L0_mix_ln2_w), "ln2_b": column(L0_mix_ln2_b),
        "w1_t": turned(L0_mix_W1), "b1": column(L0_mix_b1), "w2_t": turned(L0_mix_W2), "b2": row(L0_mix_b2),
        "wr": np.asarray(L0_ffn_Wr), "br": row(L0_ffn_br), "ew1": np.asarray(L0_ffn_W1), "eb1": column(L0_ffn_b1),
        "eg1": column(L0_ffn_g1), "ebe1": column(L0_ffn_be1), "em1": column(L0_ffn_m1), "ev1": column(L0_ffn_v1),
        "ew2": np.asarray(L0_ffn_W2), "eb2": column(L0_ffn_b2), "eg2": column(L0_ffn_g2), "ebe2": column(L0_ffn_be2),
        "em2": column(L0_ffn_m2), "ev2": column(L0_ffn_v2), "ewo": np.asarray(L0_ffn_Wo), "ebo": np.asarray(L0_ffn_bo),
    }
    nc = bacc.Bacc("TRN2", target_bir_lowering=False, num_devices=1)
    args = {n: nc.dram_tensor(f"in_{n}", a.shape, mb.dt.from_np(a.dtype), kind="ExternalInput").ap() for n, a in arrays.items()}
    out = nc.dram_tensor("out_0", _OUT[0], mb.dt.from_np(np.dtype(_OUT[1])), kind="ExternalOutput").ap()
    build(nc, out=out, **args)
    r = run_bass_kernel_spmd(nc, [{f"in_{n}": a for n, a in arrays.items()}], core_ids=[0])
    return r.results[0]["out_0"]
```

```python
import concourse.bass as bass
from concourse import mybir
from contextlib import ExitStack

F32 = mybir.dt.float32
BF16 = mybir.dt.bfloat16
I32 = mybir.dt.int32
U32 = mybir.dt.uint32
U8 = mybir.dt.uint8
ALU = mybir.AluOpType
ACT = mybir.ActivationFunctionType
AX = mybir.AxisListType

P = 128
N, D = 6250, 256
E = 100000
KF = D // P
TILES = -(-N // P)
CT = 4
CW = CT * P
CHUNKS = -(-TILES // CT)
FULL = CHUNKS - 1
TAIL_T = TILES - FULL * CT
TAIL_ROWS = N - FULL * CW
ROWS = CHUNKS * CW
LN_EPS = 1e-5

HEADS, HD = 8, 32
HID = 4 * D
HM = HID // P
EXP = 8
BN_EPS = 1e-3

EC = -(-E // P)
LAST_EC = E - (P - 1) * EC
BLOCKS = CHUNKS * CT
SGRP = 17
SPAIRS = EC // (2 * SGRP)
SEGMENTS = (0, 5, 11, 17, SPAIRS)
RING = 32
HALF = RING // 2
SUB = 4
GT = 4
GROUP = GT * P
GROUP_SHIFT = GROUP.bit_length() - 1
MAX_GROUPS = E // GROUP + BLOCKS + 1
MAX_ROUNDS = -(-GT * MAX_GROUPS // RING)
TT = (MAX_ROUNDS + 1) * RING
assert EC == 2 * SGRP * SPAIRS


def build(nc, x, src, dst, edge_weight, ln1_w, ln1_b, wx_t, bx, wq_t, wk_t, wv_t, wo_t, bo, ln2_w, ln2_b,
          w1_t, b1, w2_t, b2, wr, br, ew1, eb1, eg1, ebe1, em1, ev1, ew2, eb2, eg2, ebe2, em2, ev2, ewo, ebo, out):
    with ExitStack() as ctx:
        def sb(name, shape, dt=F32):
            return ctx.enter_context(nc.sbuf_tensor(name, shape, dt))

        def sem(name):
            return ctx.enter_context(nc.semaphore(name))

        def scratch(name, shape, dt=F32):
            return nc.dram_tensor(name, shape, dt).ap()

        table = scratch("edge_table", [P * TT, 4])
        xn_rows = scratch("xn_rows", [ROWS, D])
        xm_rows = scratch("xm_rows", [ROWS, D])
        xmid_d = scratch("xmid", [CHUNKS * P, KF * CW])

        ones = sb("ones", [P, P])
        ident = sb("ident", [P, P])
        lower = sb("lower", [P, P])
        iota = sb("iota", [P, P])
        zero_row = sb("zero_row", [1, D], BF16)
        eps_ln = sb("eps_ln", [P, 1])
        eps_bn = sb("eps_bn", [P, 1])
        head_mask = sb("head_mask", [P, P])
        lnp = sb("lnp", [P, 4, KF])
        bx_s = sb("bx_s", [P, KF])
        b1_s = sb("b1_s", [P, HM])
        bo_row = sb("bo_row", [1, D])
        b2_row = sb("b2_row", [1, D])
        br_row = sb("br_row", [1, EXP])
        ebo_s = sb("ebo_s", [EXP, D])
        bnp = sb("bnp", [P, 10, EXP * KF])
        bn_s = sb("bn_s", [P, 2, EXP * KF])
        bn_t = sb("bn_t", [P, 2, EXP * KF])
        bn_w = sb("bn_w", [P, 2, EXP * KF])

        wx_s = sb("wx_s", [P, KF, D])
        wo_s = sb("wo_s", [P, KF, D])
        w1_s = sb("w1_s", [P, KF, HID])
        w2_s = sb("w2_s", [P, HM, D])
        bdq = sb("bdq", [P, P])
        bdkv = sb("bdkv", [P, 2, P])
        wr_s = sb("wr_s", [P, KF, EXP])
        kvw = sb("kvw", [P, KF, D])

        with ExitStack() as early:
            rec = early.enter_context(nc.sbuf_tensor("rec", [P, EC, 4], F32))
        recs = sb("recs", [P, TT, 4])
        adr = sb("adr", [P, EC], I32)
        stage_idx = sb("stage_idx", [P, 2, SGRP], U32)
        stage_rec = sb("stage_rec", [P, 2, SGRP, 4])
        idx = sb("idx", [P, TT], U32)
        gather_idx = sb("gather_idx", [P, 2, HALF], U32)
        select = sb("select", [P, GT, P])
        group_i = sb("group_i", [P, BLOCKS + 1], I32)
        rounds_i = sb("rounds_i", [P, 1], I32)

        with ExitStack() as early:
            def eb(name, shape, dt=F32):
                return early.enter_context(nc.sbuf_tensor(name, shape, dt))

            src_i, dst_i, w_e = eb("src_i", [P, EC], I32), eb("dst_i", [P, EC], I32), eb("w_e", [P, EC])
            blk_i, blk = eb("blk_i", [P, EC], I32), eb("blk", [P, EC])
            pos, pos_i = eb("pos", [P, EC]), eb("pos_i", [P, EC], I32)
            mask = eb("mask", [P, BLOCKS, EC], U8)
            rank, zeros = eb("rank", [P, 2, EC]), eb("zeros", [P, KF * CW])
            cnt, base, groups_f, group_x = (eb(n, [P, BLOCKS + 1]) for n in ("cnt", "base", "groups_f", "group_x"))
            tot_i = eb("tot_i", [P, BLOCKS], I32)
        ew_s = sb("ew_s", [P, 3, EXP, KF, D])
        ring = sb("ring", [P, RING, D])

        with ExitStack() as early:
            def mb(name, shape, dt=F32):
                return early.enter_context(nc.sbuf_tensor(name, shape, dt))

            xa = [mb(f"xa{b}", [P, CT, D]) for b in (0, 1)]
            xa_n = [mb(f"xa_n{b}", [P, CT, D]) for b in (0, 1)]
            stats, mv = mb("stats", [P, CT, 6]), mb("mv", [P, CT, 2])
            sd, rstd = mb("sd", [P, CT]), mb("rstd", [P, CT])
            hn, hT = mb("hn", [P, CT, D]), mb("hT", [P, KF, CW])
            xmT = [mb(f"xmT{b}", [P, KF, CW]) for b in (0, 1)]
            kchunk, ksum, rk = mb("kchunk", [P, KF]), mb("ksum", [P, KF]), mb("rk", [P, KF])
            kmin = [mb(f"kmin{b}", [P, KF]) for b in (0, 1)]
            kscale = [mb(f"kscale{b}", [P, KF]) for b in (0, 1)]
            kpart = [mb(f"kpart{b}", [P, KF]) for b in (0, 1)]
            qmax, qsum = mb("qmax", [P, CT * HEADS]), mb("qsum", [P, CT * HEADS])
            qx = mb("qx", [P, CT, D])
            h = [mb(f"h_mix{b}", [P, CT, D]) for b in (0, 1)]
            yT = [mb(f"yT{b}", [P, KF, CW]) for b in (0, 1)]
            gT = mb("gT", [P, HM, CW])
            ekT = gT[:, 0:2, :]
            ek, vv = (gT[:, k:k + 2, :].rearrange("p a (t d) -> p (a t) d", d=D) for k in (2, 4))
            kv_sum, kvT = (gT[:, k, 0:KF * P].rearrange("p (f c) -> p f c", f=KF) for k in (6, 7))
            qT, yn, xb, xb_n = hT, hn, xa, xa_n
        cx = sb("cx", [P, CT, D])
        x1 = [sb(f"x1_{b}", [P, CT, D]) for b in (0, 1)]
        c_stats, c_mv = sb("c_stats", [P, CT, 6]), sb("c_mv", [P, CT, 2])
        c_sdt, c_rstd = sb("c_sdt", [P, CT]), sb("c_rstd", [P, CT])
        x2n = sb("x2n", [P, CT, D])
        x2T = sb("x2T", [P, KF, CW])
        rt, rmax = [sb(f"rt{b}", [P, CT, EXP]) for b in (0, 1)], sb("rmax", [P, CT])
        wT = sb("wT", [EXP, CW])
        h1, h2 = sb("h1", [P, 2, KF, CW]), sb("h2", [P, 2, KF, CW])

        ps = ctx.enter_context(nc.psum_tensor("ps", [P, 8, 512], F32))

        def rows(b, nt=CT):
            return ps[:, b:b + 2, :].rearrange("p a (t d) -> p (a t) d", d=D)[:, 0:nt, :]

        def tile(b, j):
            return ps[:, b + j // 2, (j % 2) * D:(j % 2) * D + D]

        pad_set, edges_loaded, consts = sem("pad_set"), sem("edges_loaded"), sem("consts")
        dve_chain, act_chain = sem("dve_chain"), sem("act_chain")
        counts_done, count_sums = sem("counts_done"), sem("count_sums")
        recs_zero, zeroed = sem("recs_zero"), sem("zeroed")
        addresses = sem("addresses")
        staged = [sem(f"staged{h_}") for h_ in (0, 1)]
        scattered = [sem(f"scattered{h_}") for h_ in (0, 1)]
        pool_go, dve_go = sem("pool_go"), sem("dve_go")
        table_loaded, idx_ready = sem("table_loaded"), sem("idx_ready")
        idx_staged = [sem(f"idx_staged{h_}") for h_ in (0, 1)]
        gathered = [sem(f"gathered{q}") for q in range(RING // SUB)]
        rows_ready, tiles_used, select_ready = sem("rows_ready"), sem("tiles_used"), sem("select_ready")
        params, diag_zero, mix_done, ew_loaded, bn_ready = (
            sem(n) for n in ("params", "diag_zero", "mix_done", "ew_loaded", "bn_ready"))
        bn_var, bn_sd = sem("bn_var"), sem("bn_sd")
        ax = [sem(f"ax{b}") for b in (0, 1)]
        ax_stats, ax_sd, axn, hn_ready, hn_T, hT_ready, xm_ps, xm_ready, k_ps, k_max, v_ps, vv_ready = (
            sem(n) for n in ("ax_stats", "ax_sd", "axn", "hn_ready", "hn_T", "hT_ready", "xm_ps", "xm_ready", "k_ps",
                             "k_max", "v_ps", "vv_ready"))
        ekT_ready, ek_T, ek_ready, kv_ps, kv_added, kv_masked, kv_T, kvT_ready, kvw_ps, kvw_ready = (
            sem(n) for n in ("ekT_ready", "ek_T", "ek_ready", "kv_ps", "kv_added", "kv_masked", "kv_T", "kvT_ready",
                             "kvw_ps", "kvw_ready"))
        axn_stored = [sem(f"axn_stored{b}") for b in (0, 1)]
        xm_stored = [sem(f"xm_stored{b}") for b in (0, 1)]
        bm_in = [sem(f"bm_in{b}") for b in (0, 1)]
        bn_in = [sem(f"bn_in{b}") for b in (0, 1)]
        bx_in = [sem(f"bx_in{b}") for b in (0, 1)]
        q_ps, q_shift, q_exp, q_norm, q_T, qT_ready, at_ps, h_ready, y_stats, y_sd, y_ready, y_T, yT_ready = (
            sem(n) for n in ("q_ps", "q_shift", "q_exp", "q_norm", "q_T", "qT_ready", "at_ps", "h_ready", "y_stats",
                             "y_sd", "y_ready", "y_T", "yT_ready"))
        hid_ps, hid_ready, mlp_ps, xo_ready, xo_stored = (
            sem(n) for n in ("hid_ps", "hid_ready", "mlp_ps", "xo_ready", "xo_stored"))
        cx_in, block_sums, block_read, x1_ready, c_sd, x2_ready, x2_T, x2T_ready = (
            sem(n) for n in ("cx_in", "block_sums", "block_read", "x1_ready", "c_sd", "x2_ready", "x2_T", "x2T_ready"))
        r_ps, r_shift, r_exp, w_ready, w_T, wT_ready, bias_ps = (
            sem(n) for n in ("r_ps", "r_shift", "r_exp", "w_ready", "w_T", "wT_ready", "bias_ps"))
        z1_ps, h1_ready, z2_ps, h2_ready, y_ps, y_added = (
            sem(n) for n in ("z1_ps", "h1_ready", "z2_ps", "h2_ready", "y_ps", "y_added"))
        out_stored = [sem(f"out_stored{b}") for b in (0, 1)]

        A_LOOPED = (CHUNKS - 3) // 2
        assert CHUNKS - 3 == 2 * A_LOOPED

        def norm_ahead(eng, first, step):
            first()
            with eng.Fori(0, A_LOOPED) as it:
                for b in (0, 1):
                    step(it * 2 + b, b, it, CT, True, True)
            for i in range(2 * A_LOOPED, CHUNKS):
                step(i, i % 2, i // 2, CT if i < FULL else TAIL_T, i + 1 < CHUNKS, i + 2 < CHUNKS)

        def ahead(eng, first, step, last):
            first()
            with eng.Fori(0, FULL // 2) as it:
                for b in (0, 1):
                    step(it * 2 + b, b, it)
            last(FULL, 0, FULL // 2)

        block = ctx.enter_context(nc.Block())

        @block.gpsimd
        def _(pool):
            nc.gpsimd.iota(iota[:, :], [[1, P]], base=0, channel_multiplier=0,
                           allow_small_or_imprecise_dtypes=True).then_inc(consts, 1)
            nc.gpsimd.memset(ones[:, :], 1.0).then_inc(consts, 1)
            nc.gpsimd.memset(head_mask[:, :], 1.0).then_inc(consts, 1)
            pool.wait_ge(consts, 3)
            nc.gpsimd.affine_select(out=lower[:, :], in_=ones[:, :], compare_op=ALU.is_gt, fill=0.0, base=0,
                                    pattern=[[1, P]], channel_multiplier=-1).then_inc(consts, 1)
            nc.gpsimd.affine_select(out=ident[:, :], in_=ones[:, :], compare_op=ALU.is_equal, fill=0.0, base=0,
                                    pattern=[[-1, P]], channel_multiplier=1).then_inc(consts, 1)
            hm = head_mask[:, :].rearrange("p (g c) -> p g c", c=HD)
            nc.gpsimd.affine_select(out=hm, in_=hm, compare_op=ALU.is_ge, fill=0.0, base=0,
                                    pattern=[[-HD, P // HD], [0, HD]], channel_multiplier=1).then_inc(consts, 1)
            pool.wait_ge(consts, 6)
            nc.gpsimd.affine_select(out=hm, in_=hm, compare_op=ALU.is_ge, fill=0.0, base=HD - 1,
                                    pattern=[[HD, P // HD], [0, HD]], channel_multiplier=-1).then_inc(consts, 1)
            pool.wait_ge(zeroed, 16 * 5)
            with pool.Fori(0, SPAIRS) as g:
                for h_ in (0, 1):
                    pool.wait_ge(staged[h_], (g + 1) * 32)
                    pool.sem_inc(pool_go, 1)
                    for j in range(SGRP):
                        pool.indirect_dma_start(table, bass.IndirectOffsetOnAxis(ap=stage_idx[:, h_, j:j + 1], axis=0),
                                                stage_rec[:, h_, j, :], None).then_inc(scattered[h_], 16)
            pool.wait_ge(table_loaded, 16)
            nc.gpsimd.tensor_copy(idx[:, :], recs[:, :, 0]).then_inc(idx_ready, 1)
            pool.wait_ge(idx_ready, 1)
            for b in (0, 1):
                pool.wait_ge(axn_stored[b], 16 * (FULL // 2 + 2 - b))
            pool.wait_ge(addresses, 4)
            rounds = pool.value_load(rounds_i[0:1, 0:1], min_val=2, max_val=MAX_ROUNDS)

            def gather_round(r, first):
                for j in range(RING):
                    half = j // HALF
                    if j % HALF == 0:
                        pool.wait_ge(idx_staged[half], (r + 1) * 16)
                    if j % SUB == 0:
                        if not first:
                            pool.wait_ge(tiles_used, r * RING + j + SUB - RING + GT)
                        pool.sem_inc(pool_go, 1)
                    pool.indirect_dma_start(
                        ring[:, j, :], None, xn_rows,
                        bass.IndirectOffsetOnAxis(ap=gather_idx[:, half, j % HALF:j % HALF + 1], axis=0),
                    ).then_inc(gathered[j // SUB], 16)

            gather_round(0, True)
            with pool.Fori(1, rounds) as r:
                gather_round(r, False)

        @block.sync
        def _(sp):
            edge_inputs = ((src_i, src), (dst_i, dst), (w_e, edge_weight))
            sp.wait_ge(pad_set, 3)
            for t, d in edge_inputs:
                sp.dma_start(t[0:P - 1, :], d[0:(P - 1) * EC].rearrange("(p c) -> p c", p=P - 1)).then_inc(edges_loaded, 16)
            for t, d in edge_inputs:
                sp.dma_start(t[P - 1:P, 0:LAST_EC], d[(P - 1) * EC:E].rearrange("(p c) -> p c", p=1)).then_inc(edges_loaded, 16)
            sp.wait_ge(recs_zero, 1)
            tab = table.rearrange("(p t) f -> p (t f)", p=P)
            quarter = TT * 4 // 4
            for q in range(4):
                sp.dma_start(tab[:, q * quarter:(q + 1) * quarter], zeros[:, 0:quarter]).then_inc(zeroed, 16)
            sp.dma_start(xm_rows[TILES * P:ROWS, :].rearrange("(p r) d -> p (r d)", p=P),
                         zeros[:, 0:(ROWS // P - TILES) * D]).then_inc(zeroed, 16)
            def stage(g, h_):
                k = (g * 2 + h_) * SGRP
                sp.dma_start(stage_idx[:, h_, :], adr[:, bass.ds(k, SGRP)].bitcast(U32)).then_inc(staged[h_], 16)
                sp.dma_start(stage_rec[:, h_, :, :], rec[:, bass.ds(k, SGRP), :]).then_inc(staged[h_], 16)

            for q in range(4):
                sp.wait_ge(addresses, q + 1)
                if q == 0:
                    for h_ in (0, 1):
                        stage(0, h_)
                with sp.Fori(max(SEGMENTS[q], 1), SEGMENTS[q + 1]) as g:
                    for h_ in (0, 1):
                        sp.wait_ge(scattered[h_], g * (16 * SGRP))
                        stage(g, h_)
            for h_ in (0, 1):
                sp.wait_ge(scattered[h_], SPAIRS * 16 * SGRP)
            sp.dma_start(recs[:, :, :].rearrange("p t f -> p (t f)"), tab).then_inc(table_loaded, 16)
            sp.wait_ge(idx_ready, 1)
            rounds = sp.value_load(rounds_i[0:1, 0:1], min_val=2, max_val=MAX_ROUNDS)
            for half in (0, 1):
                sp.dma_start(gather_idx[:, half, :], idx[:, half * HALF:(half + 1) * HALF]).then_inc(idx_staged[half], 16)
            with sp.Fori(0, rounds) as r:
                for q in range(RING // SUB):
                    sp.wait_ge(gathered[q], (r + 1) * (16 * SUB))
                    sp.sem_inc(rows_ready, SUB)
                    if (q + 1) * SUB % HALF == 0:
                        half = q * SUB // HALF
                        sp.dma_start(gather_idx[:, half, :],
                                     idx[:, bass.ds((r + 1) * RING + half * HALF, HALF)]).then_inc(idx_staged[half], 16)
            for half in (0, 1):
                sp.wait_ge(idx_staged[half], (rounds + 1) * 16)
                sp.sem_inc(pool_go, 1)

        @block.scalar
        def _(act):
            n = [0]

            def link(ins):
                ins.then_inc(act_chain, 1)
                n[0] += 1
                act.wait_ge(act_chain, n[0])

            def x_rows(a, i):
                return a[bass.ds(i * CW, CW), :].rearrange("(t p) d -> p t d", p=P)

            for s_ in (ek_ready, yT_ready, hid_ready, h1_ready, h2_ready):
                act.sem_inc(s_, 1)
            for s_ in (*axn_stored, *xm_stored, *out_stored, xo_stored):
                act.sem_inc(s_, 16)
            np_ = 0
            small = [(lnp[:, 0, :], ln1_w), (lnp[:, 1, :], ln1_b), (lnp[:, 2, :], ln2_w), (lnp[:, 3, :], ln2_b),
                     (bx_s[:, :], bx), (b1_s[:, :], b1), (bo_row[0:1, :], bo), (b2_row[0:1, :], b2),
                     (br_row[0:1, :], br), (ebo_s[:, :], ebo),
                     (wx_s[:, :, :], wx_t.rearrange("(k p) m -> p k m", p=P)),
                     (wo_s[:, :, :], wo_t.rearrange("(k p) m -> p k m", p=P)),
                     (w1_s[:, :, :], w1_t.rearrange("(k p) m -> p k m", p=P)),
                     (w2_s[:, :, :], w2_t.rearrange("(k p) m -> p k m", p=P)),
                     (wr_s[:, :, :], wr.rearrange("(k p) m -> p k m", p=P))]
            small += [(bnp[:, k, :], a) for k, a in enumerate((eb1, eg1, ebe1, em1, ev1, eb2, eg2, ebe2, em2, ev2))]
            for b in (0, 1):
                act.dma_start(xa[b][:, :, :], x_rows(x, b)).then_inc(ax[b], 16)
            for t, a in small:
                act.dma_start(t, a).then_inc(params, 16)
                np_ += 1
            act.wait_ge(diag_zero, 2)
            for g in range(P // HD):
                s_ = slice(g * HD, (g + 1) * HD)
                for t, a in ((bdq[s_, s_], wq_t), (bdkv[s_, 0, s_], wk_t), (bdkv[s_, 1, s_], wv_t)):
                    act.dma_start(t, a).then_inc(params, 16)
                    np_ += 1
            assert np_ == N_PARAMS
            act.wait_ge(params, 16 * np_)
            act.wait_ge(bn_var, 1)
            nc.scalar.activation(bn_w[:, 0, :], bnp[:, 4, :], ACT.Sqrt, bias=eps_bn[:, 0:1])
            nc.scalar.activation(bn_w[:, 1, :], bnp[:, 9, :], ACT.Sqrt, bias=eps_bn[:, 0:1]).then_inc(bn_sd, 1)

            def norm(i, b, k):
                act.wait_ge(ax_stats, 2 * i + k + 1)
                nc.scalar.activation(sd[:, :], mv[:, :, 1], ACT.Sqrt, bias=eps_ln[:, 0:1]).then_inc(ax_sd, 1)
                if k == 0:
                    act.wait_ge(axn, i + 1)
                    act.dma_start(x_rows(xn_rows, i), xa_n[b][:, :, :]).then_inc(axn_stored[b], 16)

            def h_evac(i):
                act.wait_ge(hn_T, i + 1)
                for f in range(KF):
                    ins = nc.scalar.activation(hT[:, f, :], ps[:, f, :], ACT.Identity,
                                               scale=lnp[:, 0, f:f + 1], bias=lnp[:, 1, f:f + 1])
                ins.then_inc(hT_ready, 1)

            def mid_evac(i, b, it):
                act.wait_ge(xm_ps, i + 1)
                act.wait_ge(xm_stored[b], 16 * (it + 1))
                for f in range(KF):
                    ins = nc.scalar.activation(xmT[b][:, f, :], ps[:, 2 + f, :], ACT.Identity, bias=bx_s[:, f:f + 1])
                ins.then_inc(xm_ready, 1)
                act.wait_ge(xm_ready, i + 1)
                act.dma_start(xmid_d[bass.ds(i * P, P), :].rearrange("p (f w) -> p f w", f=KF),
                              xmT[b][:, :, :]).then_inc(xm_stored[b], 16)

            def a_first():
                norm(0, 0, 0)
                norm(0, 0, 1)
                act.dma_start(xa[0][:, :, :], x_rows(x, 2)).then_inc(ax[0], 16)
                h_evac(0)
                mid_evac(0, 0, 0)
                norm(1, 1, 0)
                norm(1, 1, 1)

            def a_step(i, b, it, nt, more, norms):
                w = CW if nt == CT else TAIL_ROWS
                if norms and not (isinstance(i, int) and i + 3 >= CHUNKS):
                    act.dma_start(xa[1 - b][:, :, :], x_rows(x, i + 3)).then_inc(ax[1 - b], 16)
                act.wait_ge(k_max, i + 2)
                nc.scalar.activation(kscale[b][:, :], kscale[b][:, :], ACT.Exp)
                for f in range(KF):
                    ins = nc.scalar.activation(ekT[:, f, 0:w], ps[:, 4 + f, 0:w], ACT.Exp, bias=kmin[b][:, f:f + 1],
                                               accum_out=kpart[b][:, f:f + 1])
                ins.then_inc(ekT_ready, 1)
                if more:
                    h_evac(i + 1)
                act.wait_ge(ek_T, i + 1)
                act.wait_ge(kv_ps, i + 1)
                nc.scalar.activation(ek[:, 0:nt, :], rows(4, nt), ACT.Copy).then_inc(ek_ready, 1)
                if norms:
                    norm(i + 2, b, 0)
                if more:
                    mid_evac(i + 1, 1 - b, it + b)
                if norms:
                    norm(i + 2, b, 1)

            norm_ahead(act, a_first, a_step)
            act.wait_ge(kv_T, 1)
            nc.scalar.activation(kvT, ps[:, 4, 0:KF * P].rearrange("p (f c) -> p f c", f=KF), ACT.Copy).then_inc(kvT_ready, 1)
            act.wait_ge(kvw_ps, 1)
            for f in range(KF):
                ins = nc.scalar.activation(kvw[:, f, :], ps[:, f, 0:D], ACT.Copy, scale=rk[:, f:f + 1])
            ins.then_inc(kvw_ready, 1)

            def b_load(i, b):
                act.dma_start(xmT[b][:, :, :].rearrange("p f w -> p (f w)"), xmid_d[bass.ds(i * P, P), :]).then_inc(bm_in[b], 16)
                act.dma_start(xb_n[b][:, :, :], x_rows(xn_rows, i)).then_inc(bn_in[b], 16)

            def b_load_x(i, b):
                act.dma_start(xb[b][:, :, :], x_rows(x, i)).then_inc(bx_in[b], 16)

            def q_exps(i, b):
                act.wait_ge(q_shift, i + 1)
                nc.scalar.activation(qx[:, :, :], qx[:, :, :], ACT.Exp).then_inc(q_exp, 1)

            def q_evac(i, b):
                act.wait_ge(q_T, i + 1)
                for f in range(KF):
                    ins = nc.scalar.activation(qT[:, f, :], ps[:, 2 + f, :], ACT.Copy)
                ins.then_inc(qT_ready, 1)

            def y_sqrt(i, b):
                act.wait_ge(y_stats, i + 1)
                nc.scalar.activation(sd[:, :], mv[:, :, 1], ACT.Sqrt, bias=eps_ln[:, 0:1]).then_inc(y_sd, 1)

            def y_evac(i, b):
                act.wait_ge(y_T, i + 1)
                for f in range(KF):
                    ins = nc.scalar.activation(yT[b][:, f, :], ps[:, 2 + f, :], ACT.Identity,
                                               scale=lnp[:, 2, f:f + 1], bias=lnp[:, 3, f:f + 1])
                ins.then_inc(yT_ready, 1)

            def gelus(i, w, m0, m1):
                for m in range(m0, m1):
                    act.wait_ge(hid_ps, i * HM + m + 1)
                    nc.scalar.activation(gT[:, m, 0:w], ps[:, 4 + m % 2, 0:w], ACT.Gelu,
                                         bias=b1_s[:, m:m + 1]).then_inc(hid_ready, 1)

            def store_xm(i, b, nt):
                act.wait_ge(xo_ready, i + 2)
                act.dma_start(xm_rows[bass.ds(i * CW, nt * P), :].rearrange("(t p) d -> p t d", p=P),
                              xb[b][:, 0:nt, :]).then_inc(xo_stored, 16)

            for b in (0, 1):
                act.wait_ge(axn_stored[b], 16 * (FULL // 2 + 2 - b))
                act.wait_ge(xm_stored[b], 16 * (FULL // 2 + 2 - b))
            act.wait_ge(hn_ready, CHUNKS)
            b_load(0, 0)
            b_load_x(0, 0)

            def b_first():
                for part in (q_exps, q_evac, y_sqrt, y_evac):
                    part(0, 0)

            def b_step(i, b, it):
                b_load(i + 1, 1 - b)
                gelus(i, CW, 0, 6)
                act.wait_ge(xo_stored, i * 16 + 16)
                b_load_x(i + 1, 1 - b)
                q_exps(i + 1, 1 - b)
                gelus(i, CW, 6, HM)
                q_evac(i + 1, 1 - b)
                y_sqrt(i + 1, 1 - b)
                y_evac(i + 1, 1 - b)
                store_xm(i, b, CT)

            def b_last(i, b, it):
                gelus(i, TAIL_T * P, 0, HM)
                store_xm(i, b, TAIL_T)

            def load_experts():
                act.wait_ge(addresses, 4)
                for k, a in enumerate((ew1, ew2, ewo)):
                    act.dma_start(ew_s[:, k, :, :, :].rearrange("p e k h -> p (e k) h"),
                                  a.rearrange("e (k p) h -> p (e k) h", p=P)).then_inc(ew_loaded, 16)

            ahead(act, b_first, b_step, b_last)
            load_experts()
            act.wait_ge(xo_stored, 16 * (CHUNKS + 1))

            act.wait_ge(mix_done, 2)
            act.dma_start(cx[:, :, :], x_rows(xm_rows, 0)).then_inc(cx_in, 16)

            def c_sqrt(i):
                act.wait_ge(x1_ready, i + 1)
                nc.scalar.activation(c_sdt[:, :], c_mv[:, :, 1], ACT.Sqrt, bias=eps_ln[:, 0:1]).then_inc(c_sd, 1)

            def x2_evac(i):
                act.wait_ge(x2_T, i + 1)
                for f in range(KF):
                    ins = nc.scalar.activation(x2T[:, f, :], ps[:, f, :], ACT.Copy)
                ins.then_inc(x2T_ready, 1)

            def r_exps(i, b):
                act.wait_ge(r_shift, i + 1)
                nc.scalar.activation(rt[b][:, :, :], rt[b][:, :, :], ACT.Exp).then_inc(r_exp, 1)

            def experts(i, b, nt, between=None):
                w = nt * P

                def relu(k, e, zs, ready, h_, bank):
                    for m in range(KF):
                        act.wait_ge(zs, (i * EXP + e) * KF + m + 1)
                        c = e * KF + m
                        nc.scalar.activation(h_[:, e % 2, m, 0:w], ps[:, bank + m, 0:w], ACT.Relu, scale=bn_s[:, k, c:c + 1],
                                             bias=bn_t[:, k, c:c + 1]).then_inc(ready, 1)

                relu(0, 0, z1_ps, h1_ready, h1, 0)
                for e in range(EXP):
                    if e + 1 < EXP:
                        relu(0, e + 1, z1_ps, h1_ready, h1, 0)
                    if e == 0:
                        act.wait_ge(w_T, i + 1)
                        nc.scalar.activation(wT[:, 0:w], ps[0:EXP, 7, 0:w], ACT.Copy).then_inc(wT_ready, 1)
                    relu(1, e, z2_ps, h2_ready, h2, 2)
                    if e == EXP - 2 and between:
                        between()

            def c_first():
                c_sqrt(0)
                x2_evac(0)
                r_exps(0, 0)

            def c_step(i, b, it):
                act.wait_ge(x1_ready, i + 1)
                act.dma_start(cx[:, :, :], x_rows(xm_rows, i + 1)).then_inc(cx_in, 16)
                experts(i, b, CT, between=lambda: c_sqrt(i + 1))
                x2_evac(i + 1)
                act.wait_ge(y_added, (i + 1) * (EXP + 1) + 1)
                act.dma_start(x_rows(out, i), x1[b][:, :, :]).then_inc(out_stored[b], 16)
                r_exps(i + 1, 1 - b)

            def c_last(i, b, it):
                experts(i, b, TAIL_T)
                act.wait_ge(y_added, (i + 1) * (EXP + 1) + 1)
                act.dma_start(out[FULL * CW:N, :], x1[b][0:TAIL_ROWS, 0, :]).then_inc(out_stored[b], 16)

            ahead(act, c_first, c_step, c_last)
            for b in (0, 1):
                act.wait_ge(out_stored[b], 16 * (FULL // 2 + 2 - b))

        @block.tensor
        def _(pe):
            mm = nc.tensor.matmul

            pe.sem_inc(kv_ps, 1)
            pe.wait_ge(consts, 7)
            pe.wait_ge(counts_done, 1)
            mm(ps[:, 6, 0:BLOCKS], ones[:, :], cnt[:, 0:BLOCKS], start=True, stop=True)
            mm(ps[:, 7, 0:BLOCKS], lower[:, :], cnt[:, 0:BLOCKS], start=True, stop=True).then_inc(count_sums, 1)
            pe.wait_ge(params, 16 * N_PARAMS)

            def turn_h(i):
                pe.wait_ge(hn_ready, i + 1)
                for j in range(CT):
                    for f in range(KF):
                        ins = nc.tensor.transpose(ps[:, f, j * P:(j + 1) * P], hn[:, j, f * P:(f + 1) * P], ident[:, :])
                ins.then_inc(hn_T, 1)

            def mid(i):
                pe.wait_ge(hT_ready, i + 1)
                for m in range(KF):
                    for k in range(KF):
                        ins = mm(ps[:, 2 + m, :], wx_s[:, k, m * P:(m + 1) * P], hT[:, k, :], start=k == 0, stop=k == KF - 1)
                ins.then_inc(xm_ps, 1)

            def a_first():
                turn_h(0)
                mid(0)

            def a_step(i, b, it, nt, more, norms):
                w, rows_ = (CW, P) if nt == CT else (TAIL_ROWS, TAIL_ROWS)
                pe.wait_ge(xm_ready, i + 1)
                pe.wait_ge(ek_ready, i + 1)
                for f in range(KF):
                    ins = mm(ps[:, 4 + f, 0:w], bdkv[:, 0, :], xmT[b][:, f, 0:w], start=True, stop=True)
                ins.then_inc(k_ps, 1)
                pe.wait_ge(kv_added, i + 1)
                for j in range(nt):
                    for f in range(KF):
                        ins = mm(tile(6, j)[:, f * P:(f + 1) * P], xmT[b][:, f, j * P:(j + 1) * P], bdkv[:, 1, :], start=True, stop=True)
                ins.then_inc(v_ps, 1)
                if more:
                    turn_h(i + 1)
                pe.wait_ge(ekT_ready, i + 1)
                for j in range(nt):
                    for f in range(KF):
                        ins = nc.tensor.transpose(tile(4, j)[0:rows_, f * P:(f + 1) * P],
                                                  ekT[:, f, j * P:j * P + rows_], ident[:, :])
                ins.then_inc(ek_T, 1)
                if more:
                    mid(i + 1)
                pe.wait_ge(ek_ready, i + 2)
                pe.wait_ge(vv_ready, i + 1)
                for f in range(KF):
                    o = slice(f * P, (f + 1) * P)
                    for j in range(nt):
                        ins = mm(ps[:, 6, o], ek[0:rows_, j, o], vv[0:rows_, j, o], start=j == 0, stop=j == nt - 1)
                ins.then_inc(kv_ps, 1)

            norm_ahead(pe, a_first, a_step)
            pe.wait_ge(kv_masked, 1)
            for f in range(KF):
                ins = nc.tensor.transpose(ps[:, 4, f * P:(f + 1) * P], kv_sum[:, f, :], ident[:, :])
            ins.then_inc(kv_T, 1)
            pe.wait_ge(kvT_ready, 1)
            for f in range(KF):
                ins = mm(ps[:, f, 0:D], kvT[:, f, :], wo_s[:, f, :], start=True, stop=True)
            ins.then_inc(kvw_ps, 1)
            pe.wait_ge(kvw_ready, 1)

            def queries(i, b):
                pe.wait_ge(bm_in[b], (i + 2 - b) * 8)
                pe.wait_ge(h_ready, i + 1)
                for j in range(CT):
                    for f in range(KF):
                        ins = mm(tile(0, j)[:, f * P:(f + 1) * P], xmT[b][:, f, j * P:(j + 1) * P], bdq[:, :], start=True, stop=True)
                ins.then_inc(q_ps, 1)

            def turn_q(i, b):
                pe.wait_ge(q_norm, i + 1)
                for j in range(CT):
                    for f in range(KF):
                        ins = nc.tensor.transpose(ps[:, 2 + f, j * P:(j + 1) * P], qx[:, j, f * P:(f + 1) * P], ident[:, :])
                ins.then_inc(q_T, 1)

            def attend(i, b):
                pe.wait_ge(qT_ready, i + 1)
                for j in range(CT):
                    for f in range(KF):
                        mm(tile(0, j), qT[:, f, j * P:(j + 1) * P], kvw[:, f, :], start=f == 0, stop=False)
                    ins = mm(tile(0, j), ones[0:1, :], bo_row[0:1, :], start=False, stop=True)
                ins.then_inc(at_ps, 1)

            def turn_y(i, b):
                pe.wait_ge(y_ready, i + 1)
                for j in range(CT):
                    for f in range(KF):
                        ins = nc.tensor.transpose(ps[:, 2 + f, j * P:(j + 1) * P], yn[:, j, f * P:(f + 1) * P], ident[:, :])
                ins.then_inc(y_T, 1)

            def hidden(i, b, w, m0, m1):
                for m in range(m0, m1):
                    if m < 2:
                        pe.wait_ge(hid_ready, i * HM + 1)
                    else:
                        pe.wait_ge(hid_ready, i * HM + m)
                    for k in range(KF):
                        ins = mm(ps[:, 4 + m % 2, 0:w], w1_s[:, k, m * P:(m + 1) * P], yT[b][:, k, 0:w], start=k == 0, stop=k == KF - 1)
                    ins.then_inc(hid_ps, 1)

            def down(i, b, j0, j1, nt):
                if j0 == 0:
                    pe.wait_ge(xo_ready, i + 1)
                for j in range(j0, j1):
                    for m in range(HM):
                        if j == 0:
                            pe.wait_ge(hid_ready, i * HM + m + 2)
                        mm(tile(6, j), gT[:, m, j * P:(j + 1) * P], w2_s[:, m, :], start=m == 0, stop=False)
                    ins = mm(tile(6, j), ones[0:1, :], b2_row[0:1, :], start=False, stop=True)
                if j1 == nt:
                    ins.then_inc(mlp_ps, 1)

            def b_first():
                for part in (queries, turn_q, attend, turn_y):
                    part(0, 0)

            def b_step(i, b, it):
                pe.wait_ge(yT_ready, i + 2)
                hidden(i, b, CW, 0, HM // 2)
                queries(i + 1, 1 - b)
                hidden(i, b, CW, HM // 2, HM)
                turn_q(i + 1, 1 - b)
                down(i, b, 0, 1, CT)
                attend(i + 1, 1 - b)
                down(i, b, 1, 3, CT)
                turn_y(i + 1, 1 - b)
                down(i, b, 3, 4, CT)

            def b_last(i, b, it):
                pe.wait_ge(yT_ready, i + 2)
                hidden(i, b, TAIL_T * P, 0, HM)
                down(i, b, 0, TAIL_T, TAIL_T)

            ahead(pe, b_first, b_step, b_last)

            pe.wait_ge(mix_done, 2)
            pe.wait_ge(idx_ready, 1)
            pe.sem_inc(tiles_used, GT)

            def block_sum(i, k):
                a, z = (pe.value_load(group_i[0:1, bass.ds(i * CT + k + q, 1)], min_val=0, max_val=MAX_GROUPS) for q in (0, 1))
                pe.wait_ge(block_read, i * CT + k + 1)
                mm(ps[:, 6, 0:D], zero_row[0:1, 0:P], zero_row[0:1, 0:D], start=True, stop=False)
                with pe.Fori(a, z) as q:
                    for t in range(GT):
                        pe.wait_ge(rows_ready, q * GT + t + 1)
                        pe.wait_ge(select_ready, q * GT + t + 1)
                        mm(ps[:, 6, 0:D], select[:, t, :], ring[:, bass.ds((q % (RING // GT)) * GT + t, 1), :],
                           start=False, stop=False).then_inc(tiles_used, 1)
                mm(ps[:, 6, 0:D], zero_row[0:1, 0:P], zero_row[0:1, 0:D], start=False, stop=True).then_inc(block_sums, 1)

            def turn_x2(i):
                pe.wait_ge(x2_ready, i + 1)
                for j in range(CT):
                    for f in range(KF):
                        ins = nc.tensor.transpose(ps[:, f, j * P:(j + 1) * P], x2n[:, j, f * P:(f + 1) * P], ident[:, :])
                ins.then_inc(x2_T, 1)

            def router(i):
                pe.wait_ge(x2T_ready, i + 1)
                for j in range(CT):
                    o = ps[:, 7, j * EXP:(j + 1) * EXP]
                    for f in range(KF):
                        mm(o, x2T[:, f, j * P:(j + 1) * P], wr_s[:, f, :], start=f == 0, stop=False)
                    ins = mm(o, ones[0:1, :], br_row[0:1, :], start=False, stop=True)
                ins.then_inc(r_ps, 1)

            def experts(i, b, nt, between=None, at_end=None):
                w = nt * P

                def layer(n_, e, src_, bank, done):
                    for m in range(KF):
                        for k in range(KF):
                            ins = mm(ps[:, bank + m, 0:w], ew_s[:, n_, e, k, m * P:(m + 1) * P], src_[:, k, 0:w], start=k == 0, stop=k == KF - 1)
                        ins.then_inc(done, 1)

                def first(e):
                    if e:
                        pe.wait_ge(h1_ready, (i * EXP + e) * KF + 1)
                    layer(0, e, x2T, 0, z1_ps)

                def second(e):
                    pe.wait_ge(h1_ready, (i * EXP + e + 1) * KF + 1)
                    pe.wait_ge(h2_ready, (i * EXP + e) * KF + 1)
                    layer(1, e, h1[:, e % 2], 2, z2_ps)

                def third(e):
                    pe.wait_ge(h2_ready, (i * EXP + e + 1) * KF + 1)
                    pe.wait_ge(y_added, i * (EXP + 1) + e + 2)
                    for j in range(nt):
                        for k in range(KF):
                            ins = mm(tile(4, j), h2[:, e % 2, k, j * P:(j + 1) * P], ew_s[:, 2, e, k, :], start=k == 0, stop=k == KF - 1)
                    ins.then_inc(y_ps, 1)

                first(0)
                pe.wait_ge(w_ready, i + 1)
                for j in range(nt):
                    ins = nc.tensor.transpose(ps[0:EXP, 7, j * P:(j + 1) * P], rt[b][:, j, :], ident[:, :])
                ins.then_inc(w_T, 1)
                for e in range(EXP):
                    if e + 1 < EXP:
                        first(e + 1)
                    second(e)
                    if between and e % 2 == 0:
                        between(e // 2)
                    if e == 0:
                        pe.wait_ge(wT_ready, i + 1)
                        pe.wait_ge(y_added, i * (EXP + 1) + 1)
                        for j in range(nt):
                            ins = mm(tile(4, j), wT[:, j * P:(j + 1) * P], ebo_s[:, :], start=True, stop=True)
                        ins.then_inc(bias_ps, 1)
                    else:
                        third(e - 1)
                if at_end:
                    at_end()
                third(EXP - 1)

            def c_first():
                for k in range(CT):
                    block_sum(0, k)
                turn_x2(0)
                router(0)
                pe.wait_ge(ew_loaded, 16 * 3)
                pe.wait_ge(bn_ready, 2)

            def c_step(i, b, it):
                experts(i, b, CT, lambda k: block_sum(i + 1, k), lambda: turn_x2(i + 1))
                router(i + 1)

            def c_last(i, b, it):
                experts(i, b, TAIL_T)

            ahead(pe, c_first, c_step, c_last)

        @block.vector
        def _(v):
            V = nc.vector
            here = {"base": 0, "n": 0}

            def link(ins):
                ins.then_inc(dve_chain, 1)
                here["n"] += 1
                v.wait_ge(dve_chain, here["base"] + here["n"])

            def mark(ins):
                ins.then_inc(dve_chain, 1)
                here["n"] += 1
                return here["base"] + here["n"]

            V.memset(src_i[:, :], TILES * P - 1).then_inc(pad_set, 1)
            V.memset(dst_i[:, :], 0).then_inc(pad_set, 1)
            V.memset(w_e[:, :], 0.0).then_inc(pad_set, 1)
            V.memset(bdq[:, :], 0.0).then_inc(diag_zero, 1)
            V.memset(bdkv[:, :, :], 0.0).then_inc(diag_zero, 1)
            V.memset(rec[:, :, 3], 0.0)
            V.memset(zeros[:, :], 0.0).then_inc(recs_zero, 1)
            V.memset(zero_row[:, :], 0.0)
            V.memset(eps_ln[:, :], LN_EPS)
            link(V.memset(eps_bn[:, :], BN_EPS))
            v.sem_inc(bn_var, 1)
            for s_ in (k_max, h_ready, xo_ready, block_read, y_added):
                v.sem_inc(s_, 1)
            v.sem_inc(kv_added, 1)
            for t in (ksum[:, :], kv_sum):
                V.memset(t, 0.0)
            link(V.memset(kmin[1][:, :], 3.0e38))

            v.wait_ge(edges_loaded, 96)
            link(V.tensor_scalar(blk_i[:, :], src_i[:, :], 7, None, ALU.arith_shift_right))
            V.tensor_copy(blk[:, :], blk_i[:, :])
            link(V.tensor_scalar(adr[:, :], src_i[:, :], P - 1, None, ALU.bitwise_and))
            V.tensor_copy(rec[:, :, 1], adr[:, :])
            V.tensor_copy(rec[:, :, 0], dst_i[:, :])
            link(V.tensor_copy(rec[:, :, 2], w_e[:, :]))
            for k in range(BLOCKS):
                ins = V.tensor_scalar(mask[:, k, :], blk[:, :], float(k), 0.0, ALU.is_equal, ALU.add, accum_out=cnt[:, k:k + 1])
            ins.then_inc(counts_done, 1)
            v.wait_ge(count_sums, 1)
            link(V.tensor_scalar(tot_i[:, :], ps[:, 6, 0:BLOCKS], float(GROUP - 1), None, ALU.add))
            link(V.tensor_scalar(tot_i[:, :], tot_i[:, :], GROUP_SHIFT, None, ALU.arith_shift_right))
            link(V.tensor_copy(groups_f[:, 0:BLOCKS], tot_i[:, :]))
            link(V.tensor_scalar(groups_f[:, 0:BLOCKS], groups_f[:, 0:BLOCKS], 1.0, None, ALU.max))
            V.memset(group_x[:, 0:1], 0.0)
            link(V.tensor_tensor_scan(group_x[:, 1:BLOCKS + 1], groups_f[:, 0:BLOCKS], groups_f[:, 0:BLOCKS], 0.0, ALU.add, ALU.bypass))
            V.tensor_copy(group_i[:, :], group_x[:, :])
            link(V.tensor_scalar(rounds_i[:, :], group_x[:, BLOCKS:BLOCKS + 1], float(GT), float(RING - 1), ALU.mult, ALU.add))
            link(V.tensor_scalar(rounds_i[:, :], rounds_i[:, :], 5, None, ALU.arith_shift_right))
            link(V.tensor_scalar(base[:, 0:BLOCKS], group_x[:, 0:BLOCKS], float(GROUP), -1.0, ALU.mult, ALU.add))
            link(V.tensor_tensor(base[:, 0:BLOCKS], base[:, 0:BLOCKS], ps[:, 7, 0:BLOCKS], ALU.add))
            def places(s_):
                a, z = (2 * SGRP * g for g in SEGMENTS[s_:s_ + 2])
                picked = []
                for k in range(BLOCKS + 1):
                    if k < BLOCKS:
                        if k >= 2:
                            v.wait_ge(dve_chain, picked[k - 2])
                        ranked = mark(V.tensor_tensor_scan(rank[:, k % 2, a:z], mask[:, k, a:z], zeros[:, a:z],
                                                           base[:, k:k + 1], ALU.add, ALU.add))
                    if k:
                        v.wait_ge(dve_chain, before if k < BLOCKS else picked[-1])
                        V.tensor_copy(base[:, k - 1:k], rank[:, (k - 1) % 2, z - 1:z])
                        picked.append(mark(V.copy_predicated(pos[:, a:z], mask[:, k - 1, a:z], rank[:, (k - 1) % 2, a:z])))
                        if k == BLOCKS:
                            v.wait_ge(dve_chain, picked[-1])
                    before = ranked
                link(V.tensor_copy(pos_i[:, a:z], pos[:, a:z]))
                link(V.tensor_scalar(blk_i[:, a:z], pos_i[:, a:z], 7, None, ALU.arith_shift_right))
                V.tensor_copy(blk[:, a:z], blk_i[:, a:z])
                link(V.tensor_scalar(pos_i[:, a:z], pos_i[:, a:z], P - 1, None, ALU.bitwise_and))
                link(V.tensor_copy(pos[:, a:z], pos_i[:, a:z]))
                link(V.scalar_tensor_tensor(out=adr[:, a:z], in0=pos[:, a:z], scalar=float(TT), in1=blk[:, a:z],
                                            op0=ALU.mult, op1=ALU.add))
                v.sem_inc(addresses, 1)

            places(0)
            places(1)

            v.wait_ge(bn_sd, 1)
            for k in (0, 1):
                b_, g_, be_, m_ = (bnp[:, 5 * k + q, :] for q in range(4))
                link(V.reciprocal(bn_w[:, k, :], bn_w[:, k, :]))
                link(V.tensor_tensor(bn_s[:, k, :], bn_w[:, k, :], g_, ALU.mult))
                link(V.tensor_tensor(bn_t[:, k, :], b_, m_, ALU.subtract))
                link(V.tensor_tensor(bn_t[:, k, :], bn_t[:, k, :], bn_s[:, k, :], ALU.mult))
                link(V.tensor_tensor(bn_t[:, k, :], bn_t[:, k, :], be_, ALU.add))
            v.sem_inc(bn_ready, 2)

            def row_stats(src_, nt, st_, mv_, done_):
                for j in range(nt):
                    ins = V.bn_stats(st_[:, j, :], src_[:, j, :])
                link(ins)
                v.sem_inc(dve_go, 1)
                for j in range(nt):
                    ins = V.bn_aggr(mv_[:, j, :], st_[:, j, :])
                ins.then_inc(done_, 1)

            def normalize(dst_, src_, nt, mv_, sd_, rstd_):
                link(V.reciprocal(rstd_[:, 0:nt], sd_[:, 0:nt]))
                for j in range(nt):
                    ins = V.tensor_scalar(dst_[:, j, :], src_[:, j, :], mv_[:, j, 0:1], rstd_[:, j:j + 1], ALU.subtract, ALU.mult)
                return ins

            def norm(i, b, it):
                v.wait_ge(ax[b], 16 * (it + 1))
                row_stats(xa[b], CT, stats, mv, ax_stats)
                v.wait_ge(ax_sd, 2 * i + 1)
                v.wait_ge(axn_stored[b], 16 * (it + 1))
                normalize(xa_n[b], xa[b], CT, mv, sd, rstd).then_inc(axn, 1)
                v.wait_ge(axn, i + 1)
                row_stats(xa_n[b], CT, stats, mv, ax_stats)
                v.wait_ge(ax_sd, 2 * i + 2)

            def norm_end(i, b):
                normalize(hn, xa_n[b], CT, mv, sd, rstd).then_inc(hn_ready, 1)

            def key_max(i, b, nt):
                w = CW if nt == CT else TAIL_ROWS
                v.wait_ge(k_ps, i + 1)
                link(V.tensor_reduce(kchunk[:, :], ps[:, 4:6, 0:w], AX.X, ALU.max))
                link(V.scalar_tensor_tensor(out=kmin[b][:, :], in0=kchunk[:, :], scalar=-1.0, in1=kmin[1 - b][:, :],
                                            op0=ALU.mult, op1=ALU.min))
                V.tensor_tensor(kscale[b][:, :], kmin[b][:, :], kmin[1 - b][:, :], ALU.subtract).then_inc(k_max, 1)

            def value_rows(i, nt):
                v.wait_ge(v_ps, i + 1)
                V.tensor_copy(vv[:, 0:nt, :], rows(6, nt)).then_inc(vv_ready, 1)

            def add_kv(i, b):
                v.wait_ge(kv_ps, i + 2)
                v.wait_ge(kv_added, i + 1)
                link(V.tensor_tensor(ksum[:, :], ksum[:, :], kscale[b][:, :], ALU.mult))
                V.tensor_tensor(ksum[:, :], ksum[:, :], kpart[b][:, :], ALU.add)
                for f in range(KF):
                    ins = V.scalar_tensor_tensor(out=kv_sum[:, f, :], in0=kv_sum[:, f, :], scalar=kscale[b][:, f:f + 1],
                                                 in1=ps[:, 6, f * P:(f + 1) * P], op0=ALU.mult, op1=ALU.add)
                ins.then_inc(kv_added, 1)

            PER_A = 7
            chain_a = [0]

            def a_first():
                norm(0, 0, 0)
                norm_end(0, 0)
                norm(1, 1, 0)
                v.wait_ge(hn_T, 1)
                norm_end(1, 1)
                chain_a[0] = here["base"] + here["n"]

            def a_step(i, b, it, nt, more, norms):
                here["base"], here["n"] = chain_a[0] + i * PER_A, 0
                if isinstance(i, int) and i == CHUNKS - 1:
                    here["base"] = chain_a[0] + i * PER_A - 4
                key_max(i, b, nt)
                value_rows(i, nt)
                if norms:
                    norm(i + 2, b, it + 1)
                    v.wait_ge(hn_T, i + 2)
                    norm_end(i + 2, b)
                add_kv(i, b)

            norm_ahead(v, a_first, a_step)
            v.wait_ge(kv_added, CHUNKS + 1)
            V.reciprocal(rk[:, :], ksum[:, :])
            for f in range(KF):
                ins = V.tensor_tensor(kv_sum[:, f, :], kv_sum[:, f, :], head_mask[:, :], ALU.mult)
            ins.then_inc(kv_masked, 1)
            places(2)
            places(3)

            groups = CT * HEADS

            def q_softmax(i, b):
                q = ps[:, 0:2, :].rearrange("p a (g s) -> p (a g) s", s=HD)
                e = qx[:, :, :].rearrange("p t (g s) -> p (t g) s", s=HD)
                v.wait_ge(q_ps, i + 1)
                link(V.tensor_reduce(qmax[:, :], q, AX.X, ALU.max))
                V.tensor_tensor(e, q, qmax[:, :].unsqueeze(2).to_broadcast([P, groups, HD]), ALU.subtract).then_inc(q_shift, 1)
                v.wait_ge(q_exp, i + 1)
                link(V.tensor_reduce(qsum[:, :], e, AX.X, ALU.add))
                link(V.reciprocal(qsum[:, :], qsum[:, :]))
                V.tensor_tensor(e, e, qsum[:, :].unsqueeze(2).to_broadcast([P, groups, HD]), ALU.mult).then_inc(q_norm, 1)

            def attended(i, b):
                v.wait_ge(at_ps, i + 1)
                v.wait_ge(bn_in[b], (i + 2 - b) * 8)
                link(V.tensor_tensor(h[b][:, :, :], rows(0), xb_n[b][:, :, :], ALU.add))
                v.sem_inc(h_ready, 1)
                row_stats(h[b], CT, stats, mv, y_stats)

            def y_norm(i, b):
                v.wait_ge(y_sd, i + 1)
                normalize(yn, h[b], CT, mv, sd, rstd).then_inc(y_ready, 1)

            def mixed(i, b, nt):
                v.wait_ge(mlp_ps, i + 1)
                v.wait_ge(bx_in[b], (i + 2 - b) * 8)
                xo = xb[b][:, 0:nt, :]
                link(V.tensor_tensor(xo, xo, h[b][:, 0:nt, :], ALU.add))
                V.tensor_tensor(xo, xo, rows(6, nt), ALU.add).then_inc(xo_ready, 1)

            def b_next(i, b):
                q_softmax(i, b)
                attended(i, b)
                y_norm(i, b)

            PER_B = 7

            def b_all(v_, counted):
                start = here["base"] + here["n"]
                here["base"], here["n"] = start, 0
                b_next(0, 0)
                first_n = here["n"]
                loop0 = start + first_n

                def step(i, b, it):
                    here["base"], here["n"] = loop0 + i * PER_B, 0
                    b_next(i + 1, 1 - b)
                    mixed(i, b, CT)
                    assert here["n"] == PER_B, here["n"]

                def last(i, b, it):
                    here["base"], here["n"] = loop0 + i * PER_B, 0
                    mixed(i, b, TAIL_T)

                ahead(v_, lambda: None, step, last)

            b_all(v, None)
            v.wait_ge(xo_ready, CHUNKS + 1)
            v.wait_ge(xo_stored, 16 * (CHUNKS + 1))
            v.wait_ge(hid_ready, CHUNKS * HM + 1)
            v.wait_ge(mlp_ps, CHUNKS)
            v.sem_inc(mix_done, 2)

            def block(i, k, b, stored):
                a, z = (v.value_load(group_i[0:1, bass.ds(i * CT + k + q, 1)], min_val=0, max_val=MAX_GROUPS) for q in (0, 1))
                with v.Fori(a, z) as q:
                    for t in range(GT):
                        v.wait_ge(tiles_used, q * GT + t + 1)
                        V.tensor_scalar(select[:, t, :], iota[:, :], recs[:, bass.ds(q * GT + t, 1), 1],
                                        recs[:, bass.ds(q * GT + t, 1), 2], ALU.is_equal, ALU.mult).then_inc(select_ready, 1)
                v.wait_ge(block_sums, i * CT + k + 1)
                if k == 0:
                    v.wait_ge(cx_in, (i + 1) * 16)
                    v.wait_ge(out_stored[b], stored)
                V.tensor_tensor(x1[b][:, k, :], ps[:, 6, 0:D], cx[:, k, :], ALU.add).then_inc(block_read, 1)

            def x2_norm(i, b):
                v.wait_ge(block_read, (i + 1) * CT + 1)
                row_stats(x1[b], CT, c_stats, c_mv, x1_ready)
                v.wait_ge(c_sd, i + 1)
                normalize(x2n, x1[b], CT, c_mv, c_sdt, c_rstd).then_inc(x2_ready, 1)

            def shares(i, b):
                v.wait_ge(r_ps, i + 1)
                r = ps[:, 7, 0:CT * EXP].rearrange("p (t e) -> p t e", e=EXP)
                link(V.tensor_reduce(rmax[:, :], r, AX.X, ALU.max))
                V.tensor_tensor(rt[b][:, :, :], r, rmax[:, :].unsqueeze(2).to_broadcast([P, CT, EXP]), ALU.subtract).then_inc(r_shift, 1)
                v.wait_ge(r_exp, i + 1)
                link(V.tensor_reduce(rmax[:, :], rt[b][:, :, :], AX.X, ALU.add))
                link(V.reciprocal(rmax[:, :], rmax[:, :]))
                V.tensor_tensor(rt[b][:, :, :], rt[b][:, :, :], rmax[:, :].unsqueeze(2).to_broadcast([P, CT, EXP]),
                                ALU.mult).then_inc(w_ready, 1)

            def add_offsets(i, b, nt):
                v.wait_ge(bias_ps, i + 1)
                v.wait_ge(w_ready, i + 1)
                V.tensor_tensor(x1[b][:, 0:nt, :], rows(4, nt), x1[b][:, 0:nt, :], ALU.add).then_inc(y_added, 1)

            def add_expert(i, e, b, nt):
                v.wait_ge(y_ps, i * EXP + e + 1)
                v.wait_ge(y_added, i * (EXP + 1) + e + 2)
                for j in range(nt):
                    ins = V.scalar_tensor_tensor(out=x1[b][:, j, :], in0=tile(4, j), scalar=rt[b][:, j, e:e + 1],
                                                 in1=x1[b][:, j, :], op0=ALU.mult, op1=ALU.add)
                ins.then_inc(y_added, 1)

            start = here["base"] + here["n"]
            here["base"], here["n"] = start, 0
            for k in range(CT):
                block(0, k, 0, 16)
            x2_norm(0, 0)
            shares(0, 0)
            PER_C = here["n"]
            loop0 = start + PER_C

            def c_step(i, b, it):
                here["base"], here["n"] = loop0 + i * PER_C, 0
                for e in range(EXP):
                    if e % 2 == 0:
                        block(i + 1, e // 2, 1 - b, 16 * (it + 1 + b))
                    if e == 0:
                        add_offsets(i, b, CT)
                    else:
                        add_expert(i, e - 1, b, CT)
                    if e == EXP - 2:
                        x2_norm(i + 1, 1 - b)
                add_expert(i, EXP - 1, b, CT)
                shares(i + 1, 1 - b)
                assert here["n"] == PER_C

            def c_last(i, b, it):
                add_offsets(i, b, TAIL_T)
                for e in range(EXP):
                    add_expert(i, e, b, TAIL_T)

            ahead(v, lambda: None, c_step, c_last)


N_PARAMS = 25 + 3 * (P // HD)


_OUT = ((N, D), "float32")


def kernel(x, src, dst, edge_weight, L0_mix_ln1_w, L0_mix_ln1_b, L0_mix_Wx, L0_mix_bx, L0_mix_Wq, L0_mix_Wk, L0_mix_Wv,
           L0_mix_Wo, L0_mix_bo, L0_mix_ln2_w, L0_mix_ln2_b, L0_mix_W1, L0_mix_b1, L0_mix_W2, L0_mix_b2, L0_ffn_Wr,
           L0_ffn_br, L0_ffn_W1, L0_ffn_b1, L0_ffn_g1, L0_ffn_be1, L0_ffn_m1, L0_ffn_v1, L0_ffn_W2, L0_ffn_b2,
           L0_ffn_g2, L0_ffn_be2, L0_ffn_m2, L0_ffn_v2, L0_ffn_Wo, L0_ffn_bo):
    import numpy as np
    import concourse.bacc as bacc
    from concourse import mybir as mb
    from concourse.bass_utils import run_bass_kernel_spmd

    def column(a):
        return np.ascontiguousarray(np.asarray(a).reshape(-1, P).T)

    def row(a):
        return np.asarray(a).reshape(1, -1)

    def turned(a):
        return np.ascontiguousarray(np.asarray(a).T)

    padded = np.zeros((ROWS, D), np.float32)
    padded[:N] = np.asarray(x)
    arrays = {
        "x": padded, "src": np.asarray(src), "dst": np.asarray(dst), "edge_weight": np.asarray(edge_weight),
        "ln1_w": column(L0_mix_ln1_w), "ln1_b": column(L0_mix_ln1_b), "wx_t": turned(L0_mix_Wx),
        "bx": column(L0_mix_bx), "wq_t": turned(L0_mix_Wq), "wk_t": turned(L0_mix_Wk), "wv_t": turned(L0_mix_Wv),
        "wo_t": turned(L0_mix_Wo), "bo": row(L0_mix_bo), "ln2_w": column(L0_mix_ln2_w), "ln2_b": column(L0_mix_ln2_b),
        "w1_t": turned(L0_mix_W1), "b1": column(L0_mix_b1), "w2_t": turned(L0_mix_W2), "b2": row(L0_mix_b2),
        "wr": np.asarray(L0_ffn_Wr), "br": row(L0_ffn_br), "ew1": np.asarray(L0_ffn_W1), "eb1": column(L0_ffn_b1),
        "eg1": column(L0_ffn_g1), "ebe1": column(L0_ffn_be1), "em1": column(L0_ffn_m1), "ev1": column(L0_ffn_v1),
        "ew2": np.asarray(L0_ffn_W2), "eb2": column(L0_ffn_b2), "eg2": column(L0_ffn_g2), "ebe2": column(L0_ffn_be2),
        "em2": column(L0_ffn_m2), "ev2": column(L0_ffn_v2), "ewo": np.asarray(L0_ffn_Wo), "ebo": np.asarray(L0_ffn_bo),
    }
    nc = bacc.Bacc("TRN2", target_bir_lowering=False, num_devices=1)
    args = {n: nc.dram_tensor(f"in_{n}", a.shape, mb.dt.from_np(a.dtype), kind="ExternalInput").ap() for n, a in arrays.items()}
    out = nc.dram_tensor("out_0", _OUT[0], mb.dt.from_np(np.dtype(_OUT[1])), kind="ExternalOutput").ap()
    build(nc, out=out, **args)
    r = run_bass_kernel_spmd(nc, [{f"in_{n}": a for n, a in arrays.items()}], core_ids=[0])
    return r.results[0]["out_0"]
```

```python
import concourse.bass as bass
from concourse import mybir
from contextlib import ExitStack

F32 = mybir.dt.float32
F32R = mybir.dt.float32r
BF16 = mybir.dt.bfloat16
I32 = mybir.dt.int32
U32 = mybir.dt.uint32
U8 = mybir.dt.uint8
ALU = mybir.AluOpType
ACT = mybir.ActivationFunctionType
AX = mybir.AxisListType

P = 128
N, D = 6250, 256
E = 100000
KF = D // P
TILES = -(-N // P)
CT = 4
CW = CT * P
CHUNKS = -(-TILES // CT)
FULL = CHUNKS - 1
TAIL_T = TILES - FULL * CT
TAIL_ROWS = N - FULL * CW
ROWS = CHUNKS * CW
LN_EPS = 1e-5

HEADS, HD = 8, 32
HID = 4 * D
HM = HID // P
EXP = 8
LAYERS = 3
MIN_W = 256
LOADS = 6
EW = LAYERS * EXP * KF
BLOCK_AT = (0, 2, 4, 6)
SPLITS = 2 * EXP + 1
BN_EPS = 1e-3

EC = -(-E // P)
LAST_EC = E - (P - 1) * EC
BLOCKS = CHUNKS * CT
ACT_BLOCKS = 12
SGRP = 17
SPAIRS = EC // (2 * SGRP)
SEGMENTS = (0, 2, 12, 18, SPAIRS)
PARTS = len(SEGMENTS) - 1
SORT_CHUNKS = 2
SORT_STEP = 26
RING = 16
HALF = RING // 2
SUB = 4
GT = 4
GROUP = GT * P
GROUP_SHIFT = GROUP.bit_length() - 1
MAX_GROUPS = E // GROUP + BLOCKS + 1
MAX_ROUNDS = -(-GT * MAX_GROUPS // RING)
TT = (MAX_ROUNDS + 1) * RING
HEAD_T = 4 * RING
assert EC == 2 * SGRP * SPAIRS and SORT_CHUNKS * SORT_STEP == BLOCKS and LOADS == FULL - 2 - 2 * SORT_CHUNKS


def build(nc, x, src, dst, edge_weight, ln1_w, ln1_b, wx_t, bx, wq_t, wk_t, wv_t, wo_t, bo, ln2_w, ln2_b,
          w1_t, b1, w2_t, b2, wr, br, ew, eb1, eg1, ebe1, em1, ev1, eb2, eg2, ebe2, em2, ev2, ebo, out):
    with ExitStack() as ctx:
        def sb(name, shape, dt=F32):
            return ctx.enter_context(nc.sbuf_tensor(name, shape, dt))

        def sem(name):
            return ctx.enter_context(nc.semaphore(name))

        def scratch(name, shape, dt=F32):
            return nc.dram_tensor(name, shape, dt).ap()

        table = scratch("edge_table", [P * TT, 4])
        xn_rows = scratch("xn_rows", [ROWS, D])
        xm_rows = scratch("xm_rows", [ROWS, D])
        xmid_d = scratch("xmid", [CHUNKS * P, KF * CW])

        ones = sb("ones", [P, P])
        ident = sb("ident", [P, P])
        lower = sb("lower", [P, P])
        iota = sb("iota", [P, P])
        zero_row = sb("zero_row", [1, D], BF16)
        eps_ln = sb("eps_ln", [P, 1])
        eps_bn = sb("eps_bn", [P, 1])
        head_mask = sb("head_mask", [P, P])
        lnp = sb("lnp", [P, 4, KF])
        bx_s = sb("bx_s", [P, KF])
        b1_s = sb("b1_s", [P, HM])
        bo_row = sb("bo_row", [1, D])
        b2_row = sb("b2_row", [1, D])
        br_b = sb("br_b", [P, EXP])
        ebo_s = sb("ebo_s", [EXP, D])
        bnp = sb("bnp", [P, 10, EXP * KF])
        bn_s = sb("bn_s", [P, 2, EXP * KF])
        bn_t = sb("bn_t", [P, 2, EXP * KF])
        bn_w = sb("bn_w", [P, 2, EXP * KF])

        wr_s = sb("wr_s", [P, KF, EXP])

        with ExitStack() as early:
            rec = early.enter_context(nc.sbuf_tensor("rec", [P, EC, 4], F32))
        recs = sb("recs", [P, TT, 4])
        stage_idx = sb("stage_idx", [P, 2, SGRP], U32)
        stage_rec = sb("stage_rec", [P, 2, SGRP, 4])
        idx = sb("idx", [P, TT], U32)
        adr = idx[:, 0:EC].bitcast(I32)
        gather_idx = sb("gather_idx", [P, 2, HALF], U32)
        select = sb("select", [P, GT, P])
        group_i = sb("group_i", [P, BLOCKS + 1], I32)
        rounds_i = sb("rounds_i", [P, 1], I32)

        with ExitStack() as early:
            def eb(name, shape, dt=F32):
                return early.enter_context(nc.sbuf_tensor(name, shape, dt))

            src_i, dst_i, w_e = eb("src_i", [P, EC], I32), eb("dst_i", [P, EC], I32), eb("w_e", [P, EC])
            blk_i, blk = eb("blk_i", [P, EC], I32), eb("blk", [P, EC])
            pos, pos_i = eb("pos", [P, EC]), eb("pos_i", [P, EC], I32)
            mask = eb("mask", [P, BLOCKS, EC], U8)
            rank, zeros = eb("rank", [P, 2, EC]), eb("zeros", [P, KF * CW])
            cnt, base, groups_f, group_x = (eb(n, [P, BLOCKS + 1]) for n in ("cnt", "base", "groups_f", "group_x"))
            tot_i = eb("tot_i", [P, BLOCKS], I32)
        ew_l = sb("ew_l", [P, EW, D])
        ring = sb("ring", [P, RING, D])
        cx = sb("cx", [P, CT, D])
        x1 = [sb(f"x1_{b}", [P, CT, D]) for b in (0, 1)]

        with ExitStack() as early:
            def mb(name, shape, dt=F32):
                return early.enter_context(nc.sbuf_tensor(name, shape, dt))

            wx_s, wo_s = mb("wx_s", [P, KF, D]), mb("wo_s", [P, KF, D])
            w1_s, w2_s = mb("w1_s", [P, KF, HID]), mb("w2_s", [P, HM, D])
            bdq = mb("bdq", [P, P])
            bdkv = mb("bdkv", [P, 2, P])
            kvw = mb("kvw", [P, KF, D])
            xa = [mb(f"xa{b}", [P, CT, D]) for b in (0, 1)]
            xa_n = [mb(f"xa_n{b}", [P, CT, D]) for b in (0, 1)]
            stats, mv = mb("stats", [P, CT, 6]), mb("mv", [P, CT, 2])
            sd, rstd = mb("sd", [P, CT]), mb("rstd", [P, CT])
            hn, hT = mb("hn", [P, CT, D]), mb("hT", [P, KF, CW])
            xmT = [mb(f"xmT{b}", [P, KF, CW]) for b in (0, 1)]
            kchunk, ksum, rk = mb("kchunk", [P, KF]), mb("ksum", [P, KF]), mb("rk", [P, KF])
            kmin = [mb(f"kmin{b}", [P, KF]) for b in (0, 1)]
            kscale = [mb(f"kscale{b}", [P, KF]) for b in (0, 1)]
            kpart = [mb(f"kpart{b}", [P, KF]) for b in (0, 1)]
            qmax, qsum = mb("qmax", [P, CT * HEADS]), mb("qsum", [P, CT * HEADS])
            qx = mb("qx", [P, CT, D])
            h = [mb(f"h_mix{b}", [P, CT, D]) for b in (0, 1)]
            yT = [mb(f"yT{b}", [P, KF, CW]) for b in (0, 1)]
            gT = mb("gT", [P, HM, CW])
            ekT = gT[:, 0:2, :]
            ek, vv = (gT[:, k:k + 2, :].rearrange("p a (t d) -> p (a t) d", d=D) for k in (2, 4))
            kv_sum, kvT = (gT[:, k, 0:KF * P].rearrange("p (f c) -> p f c", f=KF) for k in (6, 7))
            qT, yn, xb, xb_n = hT, hn, xa, xa_n
        ew_h = sb("ew_h", [P, EW, D], F32R)
        c_stats, c_mv = sb("c_stats", [P, CT, 6]), sb("c_mv", [P, CT, 2])
        c_sdt, c_rstd = sb("c_sdt", [P, CT]), sb("c_rstd", [P, CT])
        x2n = sb("x2n", [P, CT, D])
        whole = sb("whole", [P, KF, CW])
        x2T = [sb(f"x2T_{q}", [P, KF, CW], F32R) for q in "hl"]
        rt, rmax = [sb(f"rt{b}", [P, CT, EXP]) for b in (0, 1)], sb("rmax", [P, CT])
        wT = sb("wT", [EXP, CW])
        h1 = [sb(f"h1_{q}", [P, 2, KF, CW], F32R) for q in "hl"]
        h2 = [sb(f"h2_{q}", [P, 2, KF, CW], F32R) for q in "hl"]

        def relu_no(i, layer, e):
            u = max(2 * e - 1, 0) if layer == 1 else 2 * e + 2
            if layer == 2 and e == EXP - 1 and isinstance(i, int) and i == FULL:
                u -= 1
            return KF + (i * SPLITS + u) * KF

        def input_no(i):
            return 0 if isinstance(i, int) and i == 0 else KF + ((i - 1) * SPLITS + 2 * EXP - 1) * KF

        ps = ctx.enter_context(nc.psum_tensor("ps", [P, 8, 512], F32))

        def rows(b, nt=CT):
            return ps[:, b:b + 2, :].rearrange("p a (t d) -> p (a t) d", d=D)[:, 0:nt, :]

        def tile(b, j):
            return ps[:, b + j // 2, (j % 2) * D:(j % 2) * D + D]

        pad_set, edges_loaded, consts = sem("pad_set"), sem("edges_loaded"), sem("consts")
        dve_chain, act_chain = sem("dve_chain"), sem("act_chain")
        blk_ready, counts_done, act_counts, count_sums = (
            sem(n) for n in ("blk_ready", "counts_done", "act_counts", "count_sums"))
        recs_zero, zeroed = sem("recs_zero"), sem("zeroed")
        addresses = sem("addresses")
        staged = [sem(f"staged{h_}") for h_ in (0, 1)]
        scattered = [sem(f"scattered{h_}") for h_ in (0, 1)]
        pool_go, dve_go = sem("pool_go"), sem("dve_go")
        head_loaded, table_loaded, idx_ready = sem("head_loaded"), sem("table_loaded"), sem("idx_ready")
        idx_staged = [sem(f"idx_staged{h_}") for h_ in (0, 1)]
        gathered = [sem(f"gathered{q}") for q in range(RING // SUB)]
        rows_ready, tiles_used, select_ready = sem("rows_ready"), sem("tiles_used"), sem("select_ready")
        params, diag_zero, mix_done, ew_loaded, bn_ready = (
            sem(n) for n in ("params", "diag_zero", "mix_done", "ew_loaded", "bn_ready"))
        bn_var, bn_sd = sem("bn_var"), sem("bn_sd")
        ax = [sem(f"ax{b}") for b in (0, 1)]
        ax_stats, ax_sd, axn, hn_ready, hn_T, hT_ready, xm_ps, xm_ready, k_ps, k_max, v_ps, vv_ready = (
            sem(n) for n in ("ax_stats", "ax_sd", "axn", "hn_ready", "hn_T", "hT_ready", "xm_ps", "xm_ready", "k_ps",
                             "k_max", "v_ps", "vv_ready"))
        ekT_ready, ek_T, ek_ready, kv_ps, kv_added, kv_masked, kv_T, kvT_ready, kvw_ps, kvw_ready = (
            sem(n) for n in ("ekT_ready", "ek_T", "ek_ready", "kv_ps", "kv_added", "kv_masked", "kv_T", "kvT_ready",
                             "kvw_ps", "kvw_ready"))
        axn_stored = [sem(f"axn_stored{b}") for b in (0, 1)]
        xm_stored = [sem(f"xm_stored{b}") for b in (0, 1)]
        bm_in = [sem(f"bm_in{b}") for b in (0, 1)]
        bn_in = [sem(f"bn_in{b}") for b in (0, 1)]
        bx_in = [sem(f"bx_in{b}") for b in (0, 1)]
        q_ps, q_shift, q_exp, q_norm, q_T, qT_ready, at_ps, h_ready, y_stats, y_sd, y_ready, y_T, yT_ready = (
            sem(n) for n in ("q_ps", "q_shift", "q_exp", "q_norm", "q_T", "qT_ready", "at_ps", "h_ready", "y_stats",
                             "y_sd", "y_ready", "y_T", "yT_ready"))
        hid_ps, hid_ready, mlp_ps, xo_ready, xo_stored = (
            sem(n) for n in ("hid_ps", "hid_ready", "mlp_ps", "xo_ready", "xo_stored"))
        cx_in, block_sums, block_read, x1_ready, c_sd, x2_ready, x2_T = (
            sem(n) for n in ("cx_in", "block_sums", "block_read", "x1_ready", "c_sd", "x2_ready", "x2_T"))
        r_ps, r_shift, r_exp, w_ready, w_T, wT_ready, bias_ps = (
            sem(n) for n in ("r_ps", "r_shift", "r_exp", "w_ready", "w_T", "wT_ready", "bias_ps"))
        z1_ps, z2_ps, high_ready, split_ready, y_ps, y_added, ew_high, ew_split = (
            sem(n) for n in ("z1_ps", "z2_ps", "high_ready", "split_ready", "y_ps", "y_added", "ew_high", "ew_split"))
        out_stored = [sem(f"out_stored{b}") for b in (0, 1)]

        A_LOOPED = (CHUNKS - 3) // 2
        assert CHUNKS - 3 == 2 * A_LOOPED

        def norm_ahead(eng, first, step):
            first()
            with eng.Fori(0, A_LOOPED) as it:
                for b in (0, 1):
                    step(it * 2 + b, b, it, CT, True, True)
            for i in range(2 * A_LOOPED, CHUNKS):
                step(i, i % 2, i // 2, CT if i < FULL else TAIL_T, i + 1 < CHUNKS, i + 2 < CHUNKS)

        def ahead(eng, first, step, last):
            first()
            with eng.Fori(0, FULL // 2) as it:
                for b in (0, 1):
                    step(it * 2 + b, b, it)
            last(FULL, 0, FULL // 2)

        block = ctx.enter_context(nc.Block())

        @block.gpsimd
        def _(pool):
            nc.gpsimd.iota(iota[:, :], [[1, P]], base=0, channel_multiplier=0,
                           allow_small_or_imprecise_dtypes=True).then_inc(consts, 1)
            nc.gpsimd.memset(ones[:, :], 1.0).then_inc(consts, 1)
            nc.gpsimd.memset(head_mask[:, :], 1.0).then_inc(consts, 1)
            pool.wait_ge(consts, 3)
            nc.gpsimd.affine_select(out=lower[:, :], in_=ones[:, :], compare_op=ALU.is_gt, fill=0.0, base=0,
                                    pattern=[[1, P]], channel_multiplier=-1).then_inc(consts, 1)
            nc.gpsimd.affine_select(out=ident[:, :], in_=ones[:, :], compare_op=ALU.is_equal, fill=0.0, base=0,
                                    pattern=[[-1, P]], channel_multiplier=1).then_inc(consts, 1)
            hm = head_mask[:, :].rearrange("p (g c) -> p g c", c=HD)
            nc.gpsimd.affine_select(out=hm, in_=hm, compare_op=ALU.is_ge, fill=0.0, base=0,
                                    pattern=[[-HD, P // HD], [0, HD]], channel_multiplier=1).then_inc(consts, 1)
            pool.wait_ge(consts, 6)
            nc.gpsimd.affine_select(out=hm, in_=hm, compare_op=ALU.is_ge, fill=0.0, base=HD - 1,
                                    pattern=[[HD, P // HD], [0, HD]], channel_multiplier=-1).then_inc(consts, 1)
            pool.wait_ge(zeroed, 16 * 5)
            with pool.Fori(0, SPAIRS) as g:
                for h_ in (0, 1):
                    pool.wait_ge(staged[h_], (g + 1) * 32)
                    pool.sem_inc(pool_go, 1)
                    for j in range(SGRP):
                        pool.indirect_dma_start(table, bass.IndirectOffsetOnAxis(ap=stage_idx[:, h_, j:j + 1], axis=0),
                                                stage_rec[:, h_, j, :], None).then_inc(scattered[h_], 16)
            pool.wait_ge(idx_ready, 1)
            for b in (0, 1):
                pool.wait_ge(axn_stored[b], 16 * (FULL // 2 + 2 - b))
            pool.wait_ge(addresses, PARTS)
            rounds = pool.value_load(rounds_i[0:1, 0:1], min_val=2, max_val=MAX_ROUNDS)

            def gather_round(r, first):
                for j in range(RING):
                    half = j // HALF
                    if j % HALF == 0:
                        pool.wait_ge(idx_staged[half], (r + 1) * 16)
                    if j % SUB == 0:
                        if not first:
                            pool.wait_ge(tiles_used, r * RING + j + SUB - RING + GT)
                        pool.sem_inc(pool_go, 1)
                    pool.indirect_dma_start(
                        ring[:, j, :], None, xn_rows,
                        bass.IndirectOffsetOnAxis(ap=gather_idx[:, half, j % HALF:j % HALF + 1], axis=0),
                    ).then_inc(gathered[j // SUB], 16)

            gather_round(0, True)
            with pool.Fori(1, rounds) as r:
                gather_round(r, False)

        @block.sync
        def _(sp):
            edge_inputs = ((src_i, src), (dst_i, dst), (w_e, edge_weight))
            sp.wait_ge(pad_set, 3)
            for t, d in edge_inputs:
                sp.dma_start(t[0:P - 1, :], d[0:(P - 1) * EC].rearrange("(p c) -> p c", p=P - 1)).then_inc(edges_loaded, 16)
            for t, d in edge_inputs:
                sp.dma_start(t[P - 1:P, 0:LAST_EC], d[(P - 1) * EC:E].rearrange("(p c) -> p c", p=1)).then_inc(edges_loaded, 16)
            sp.wait_ge(recs_zero, 1)
            tab = table.rearrange("(p t) f -> p (t f)", p=P)
            quarter = TT * 4 // 4
            for q in range(4):
                sp.dma_start(tab[:, q * quarter:(q + 1) * quarter], zeros[:, 0:quarter]).then_inc(zeroed, 16)
            sp.dma_start(xm_rows[TILES * P:ROWS, :].rearrange("(p r) d -> p (r d)", p=P),
                         zeros[:, 0:(ROWS // P - TILES) * D]).then_inc(zeroed, 16)
            def stage(g, h_):
                k = (g * 2 + h_) * SGRP
                sp.dma_start(stage_idx[:, h_, :], adr[:, bass.ds(k, SGRP)].bitcast(U32)).then_inc(staged[h_], 16)
                sp.dma_start(stage_rec[:, h_, :, :], rec[:, bass.ds(k, SGRP), :]).then_inc(staged[h_], 16)

            for q in range(PARTS):
                sp.wait_ge(addresses, q + 1)
                if q == 0:
                    for h_ in (0, 1):
                        stage(0, h_)
                with sp.Fori(max(SEGMENTS[q], 1), SEGMENTS[q + 1]) as g:
                    for h_ in (0, 1):
                        sp.wait_ge(scattered[h_], g * (16 * SGRP))
                        stage(g, h_)
            for h_ in (0, 1):
                sp.wait_ge(scattered[h_], SPAIRS * 16 * SGRP)
            for a, z, s_ in ((0, HEAD_T, head_loaded), (HEAD_T, TT, table_loaded)):
                sp.dma_start(recs[:, a:z, :].rearrange("p t f -> p (t f)"), tab[:, a * 4:z * 4]).then_inc(s_, 16)
            sp.wait_ge(idx_ready, 1)
            rounds = sp.value_load(rounds_i[0:1, 0:1], min_val=2, max_val=MAX_ROUNDS)
            for half in (0, 1):
                sp.dma_start(gather_idx[:, half, :], idx[:, half * HALF:(half + 1) * HALF]).then_inc(idx_staged[half], 16)
            sp.wait_ge(idx_ready, 2)
            with sp.Fori(0, rounds) as r:
                for q in range(RING // SUB):
                    sp.wait_ge(gathered[q], (r + 1) * (16 * SUB))
                    sp.sem_inc(rows_ready, SUB)
                    if (q + 1) * SUB % HALF == 0:
                        half = q * SUB // HALF
                        sp.dma_start(gather_idx[:, half, :],
                                     idx[:, bass.ds((r + 1) * RING + half * HALF, HALF)]).then_inc(idx_staged[half], 16)
            for half in (0, 1):
                sp.wait_ge(idx_staged[half], (rounds + 1) * 16)
                sp.sem_inc(pool_go, 1)

        @block.scalar
        def _(act):
            n = [0]

            def link(ins):
                ins.then_inc(act_chain, 1)
                n[0] += 1
                act.wait_ge(act_chain, n[0])

            def x_rows(a, i):
                return a[bass.ds(i * CW, CW), :].rearrange("(t p) d -> p t d", p=P)

            for s_ in (ek_ready, yT_ready, hid_ready):
                act.sem_inc(s_, 1)
            for s_ in (*axn_stored, *xm_stored, *out_stored, xo_stored):
                act.sem_inc(s_, 16)
            np_ = 0
            small = [(lnp[:, 0, :], ln1_w), (lnp[:, 1, :], ln1_b), (lnp[:, 2, :], ln2_w), (lnp[:, 3, :], ln2_b),
                     (bx_s[:, :], bx), (b1_s[:, :], b1), (bo_row[0:1, :], bo), (b2_row[0:1, :], b2),
                     (br_b[:, :], br), (ebo_s[:, :], ebo),
                     (wx_s[:, :, :], wx_t.rearrange("(k p) m -> p k m", p=P)),
                     (wo_s[:, :, :], wo_t.rearrange("(k p) m -> p k m", p=P)),
                     (w1_s[:, :, :], w1_t.rearrange("(k p) m -> p k m", p=P)),
                     (w2_s[:, :, :], w2_t.rearrange("(k p) m -> p k m", p=P)),
                     (wr_s[:, :, :], wr.rearrange("(k p) m -> p k m", p=P))]
            small += [(bnp[:, k, :], a) for k, a in enumerate((eb1, eg1, ebe1, em1, ev1, eb2, eg2, ebe2, em2, ev2))]
            for b in (0, 1):
                act.dma_start(xa[b][:, :, :], x_rows(x, b)).then_inc(ax[b], 16)
            for t, a in small:
                act.dma_start(t, a).then_inc(params, 16)
                np_ += 1
            act.wait_ge(diag_zero, 2)
            for g in range(P // HD):
                s_ = slice(g * HD, (g + 1) * HD)
                for t, a in ((bdq[s_, s_], wq_t), (bdkv[s_, 0, s_], wk_t), (bdkv[s_, 1, s_], wv_t)):
                    act.dma_start(t, a).then_inc(params, 16)
                    np_ += 1
            assert np_ == N_PARAMS
            act.wait_ge(consts, 7)
            act.wait_ge(blk_ready, 1)
            for k in range(BLOCKS - ACT_BLOCKS, BLOCKS + 1):
                if k < BLOCKS:
                    apart = nc.scalar.activation(rank[:, k % 2, :], blk[:, :], ACT.Abs, scale=-1.0, bias=iota[:, k:k + 1])
                    apart.then_inc(act_chain, 1)
                    n[0] += 1
                if k > BLOCKS - ACT_BLOCKS:
                    act.wait_ge(act_chain, n[0] - 1 if k < BLOCKS else n[0])
                    ins = nc.scalar.activation(mask[:, k - 1, :], rank[:, (k - 1) % 2, :], ACT.Relu, scale=-1.0, bias=ones[:, 0:1],
                                               accum_out=cnt[:, k - 1:k])
                    ins.then_inc(act_chain, 1)
                    n[0] += 1
                    act.wait_ge(act_chain, n[0])
            act.sem_inc(act_counts, 1)
            act.wait_ge(params, 16 * np_)
            act.wait_ge(bn_var, 1)
            nc.scalar.activation(bn_w[:, 0, :], bnp[:, 4, :], ACT.Sqrt, bias=eps_bn[:, 0:1])
            nc.scalar.activation(bn_w[:, 1, :], bnp[:, 9, :], ACT.Sqrt, bias=eps_bn[:, 0:1]).then_inc(bn_sd, 1)

            def norm(i, b, k):
                act.wait_ge(ax_stats, 2 * i + k + 1)
                nc.scalar.activation(sd[:, :], mv[:, :, 1], ACT.Sqrt, bias=eps_ln[:, 0:1]).then_inc(ax_sd, 1)
                if k == 0:
                    act.wait_ge(axn, i + 1)
                    act.dma_start(x_rows(xn_rows, i), xa_n[b][:, :, :]).then_inc(axn_stored[b], 16)

            def h_evac(i):
                act.wait_ge(hn_T, i + 1)
                for f in range(KF):
                    ins = nc.scalar.activation(hT[:, f, :], ps[:, f, :], ACT.Identity,
                                               scale=lnp[:, 0, f:f + 1], bias=lnp[:, 1, f:f + 1])
                ins.then_inc(hT_ready, 1)

            def mid_evac(i, b, it):
                act.wait_ge(xm_ps, i + 1)
                act.wait_ge(xm_stored[b], 16 * (it + 1))
                for f in range(KF):
                    ins = nc.scalar.activation(xmT[b][:, f, :], ps[:, 2 + f, :], ACT.Identity, bias=bx_s[:, f:f + 1])
                ins.then_inc(xm_ready, 1)
                act.wait_ge(xm_ready, i + 1)
                act.dma_start(xmid_d[bass.ds(i * P, P), :].rearrange("p (f w) -> p f w", f=KF),
                              xmT[b][:, :, :]).then_inc(xm_stored[b], 16)

            def a_first():
                norm(0, 0, 0)
                norm(0, 0, 1)
                act.dma_start(xa[0][:, :, :], x_rows(x, 2)).then_inc(ax[0], 16)
                h_evac(0)
                mid_evac(0, 0, 0)
                norm(1, 1, 0)
                norm(1, 1, 1)

            def a_step(i, b, it, nt, more, norms):
                w = CW if nt == CT else TAIL_ROWS
                if norms and not (isinstance(i, int) and i + 3 >= CHUNKS):
                    act.dma_start(xa[1 - b][:, :, :], x_rows(x, i + 3)).then_inc(ax[1 - b], 16)
                act.wait_ge(k_max, i + 2)
                nc.scalar.activation(kscale[b][:, :], kscale[b][:, :], ACT.Exp)
                for f in range(KF):
                    ins = nc.scalar.activation(ekT[:, f, 0:w], ps[:, 4 + f, 0:w], ACT.Exp, bias=kmin[b][:, f:f + 1],
                                               accum_out=kpart[b][:, f:f + 1])
                ins.then_inc(ekT_ready, 1)
                if more:
                    h_evac(i + 1)
                act.wait_ge(ek_T, i + 1)
                act.wait_ge(kv_ps, i + 1)
                nc.scalar.activation(ek[:, 0:nt, :], rows(4, nt), ACT.Copy).then_inc(ek_ready, 1)
                if norms:
                    norm(i + 2, b, 0)
                if more:
                    mid_evac(i + 1, 1 - b, it + b)
                if norms:
                    norm(i + 2, b, 1)

            norm_ahead(act, a_first, a_step)
            act.wait_ge(kv_T, 1)
            nc.scalar.activation(kvT, ps[:, 4, 0:KF * P].rearrange("p (f c) -> p f c", f=KF), ACT.Copy).then_inc(kvT_ready, 1)
            act.wait_ge(kvw_ps, 1)
            for f in range(KF):
                ins = nc.scalar.activation(kvw[:, f, :], ps[:, f, 0:D], ACT.Copy, scale=rk[:, f:f + 1])
            ins.then_inc(kvw_ready, 1)

            def b_load_mid(i, b):
                act.dma_start(xmT[b][:, :, :].rearrange("p f w -> p (f w)"), xmid_d[bass.ds(i * P, P), :]).then_inc(bm_in[b], 16)

            def b_load_n(i, b):
                act.dma_start(xb_n[b][:, :, :], x_rows(xn_rows, i)).then_inc(bn_in[b], 16)

            def b_load_x(i, b):
                act.dma_start(xb[b][:, :, :], x_rows(x, i)).then_inc(bx_in[b], 16)

            def q_exps(i, b):
                act.wait_ge(q_shift, i + 1)
                nc.scalar.activation(qx[:, :, :], qx[:, :, :], ACT.Exp).then_inc(q_exp, 1)

            def q_evac(i, b):
                act.wait_ge(q_T, i + 1)
                for f in range(KF):
                    ins = nc.scalar.activation(qT[:, f, :], ps[:, 2 + f, :], ACT.Copy)
                ins.then_inc(qT_ready, 1)

            def y_sqrt(i, b):
                act.wait_ge(y_stats, i + 1)
                nc.scalar.activation(sd[:, :], mv[:, :, 1], ACT.Sqrt, bias=eps_ln[:, 0:1]).then_inc(y_sd, 1)

            def y_evac(i, b):
                act.wait_ge(y_T, i + 1)
                for f in range(KF):
                    ins = nc.scalar.activation(yT[b][:, f, :], ps[:, 2 + f, :], ACT.Identity,
                                               scale=lnp[:, 2, f:f + 1], bias=lnp[:, 3, f:f + 1])
                ins.then_inc(yT_ready, 1)

            def gelus(i, w, m0, m1):
                for m in range(m0, m1):
                    act.wait_ge(hid_ps, i * HM + m + 1)
                    nc.scalar.activation(gT[:, m, 0:w], ps[:, 4 + m % 4, 0:w], ACT.Gelu,
                                         bias=b1_s[:, m:m + 1]).then_inc(hid_ready, 1)

            def store_xm(i, b, nt):
                act.wait_ge(xo_ready, i + 2)
                act.dma_start(xm_rows[bass.ds(i * CW, nt * P), :].rearrange("(t p) d -> p t d", p=P),
                              xb[b][:, 0:nt, :]).then_inc(xo_stored, 16)

            for b in (0, 1):
                act.wait_ge(axn_stored[b], 16 * (FULL // 2 + 2 - b))
                act.wait_ge(xm_stored[b], 16 * (FULL // 2 + 2 - b))
            act.wait_ge(hn_ready, CHUNKS)
            for b in (0, 1):
                b_load_mid(b, b)
            b_load_n(0, 0)
            b_load_x(0, 0)

            def b_first():
                for part in (q_exps, q_evac, y_sqrt, y_evac):
                    part(0, 0)

            def b_step(i, b, it, mid=True):
                b_load_n(i + 1, 1 - b)
                if mid:
                    b_load_mid(i + 2, b)
                gelus(i, CW, 0, HM // 2)
                act.wait_ge(xo_stored, i * 16 + 16)
                b_load_x(i + 1, 1 - b)
                q_exps(i + 1, 1 - b)
                gelus(i, CW, HM // 2, HM)
                q_evac(i + 1, 1 - b)
                y_sqrt(i + 1, 1 - b)
                y_evac(i + 1, 1 - b)
                store_xm(i, b, CT)

            def b_last(i, b, it):
                gelus(i, TAIL_T * P, 0, HM)
                store_xm(i, b, TAIL_T)

            def load_experts(part):
                c = EW // LOADS
                act.dma_start(ew_l[:, bass.ds(part * c, c), :],
                              ew[bass.ds(part * (c * P), c * P), :].rearrange("(c p) h -> p c h", p=P)).then_inc(ew_loaded, 16)

            b_first()
            with act.Fori(0, SORT_CHUNKS) as it:
                for b in (0, 1):
                    b_step(it * 2 + b, b, it)
            act.wait_ge(addresses, PARTS)
            with act.Fori(SORT_CHUNKS, FULL // 2 - 1) as it:
                for b in (0, 1):
                    load_experts(it * 2 + b - 2 * SORT_CHUNKS)
                    b_step(it * 2 + b, b, it)
            for i in (FULL - 2, FULL - 1):
                b_step(i, i % 2, i // 2, mid=i + 2 < CHUNKS)
            b_last(FULL, 0, FULL // 2)
            act.wait_ge(xo_stored, 16 * (CHUNKS + 1))

            act.wait_ge(mix_done, 2)
            act.wait_ge(zeroed, 16 * 5)
            act.dma_start(cx[:, :, :], x_rows(xm_rows, 0)).then_inc(cx_in, 16)
            act.wait_ge(ew_loaded, 16 * LOADS)
            for c in range(0, EW, 2):
                nc.scalar.activation(ew_h[:, c:c + 2, :], ew_l[:, c:c + 2, :], ACT.Copy).then_inc(ew_high, 1)

            def c_sqrt(i):
                act.wait_ge(x1_ready, i + 1)
                nc.scalar.activation(c_sdt[:, :], c_mv[:, :, 1], ACT.Sqrt, bias=eps_ln[:, 0:1]).then_inc(c_sd, 1)

            def split(n, half, w, high, src_, func, first=False, **k):
                if not first:
                    act.wait_ge(split_ready, n - 1)
                nc.scalar.activation(whole[:, half, 0:w], src_, func, **k)
                nc.scalar.activation(high, src_, func, **k).then_inc(high_ready, 1)

            def x2_evac(i, first=False):
                act.wait_ge(x2_T, i + 1)
                for f in range(KF):
                    split(input_no(i) + f, f, CW, x2T[0][:, f, :], ps[:, f, :], ACT.Copy, first)

            def r_exps(i, b):
                act.wait_ge(r_shift, i + 1)
                nc.scalar.activation(rt[b][:, :, :], rt[b][:, :, :], ACT.Exp).then_inc(r_exp, 1)

            def relu(i, k, e, w):
                zs, h_, bank = ((z1_ps, h1, 0), (z2_ps, h2, 2))[k]
                for m in range(KF):
                    act.wait_ge(zs, (i * EXP + e) * KF + m + 1)
                    c = e * KF + m
                    split(relu_no(i, k + 1, e) + m, m, w, h_[0][:, e % 2, m, 0:w], ps[:, bank + m, 0:w], ACT.Relu,
                          scale=bn_s[:, k, c:c + 1], bias=bn_t[:, k, c:c + 1])

            def experts(i, b, nt, between=None, next_input=None):
                w = max(nt * P, MIN_W)
                for e in range(EXP):
                    if e + 1 < EXP:
                        relu(i, 0, e + 1, w)
                    if e == 0:
                        act.wait_ge(w_T, i + 1)
                        nc.scalar.activation(wT[:, 0:nt * P], ps[0:EXP, 7, 0:nt * P], ACT.Copy).then_inc(wT_ready, 1)
                    if e == BLOCK_AT[-1] and between:
                        between()
                    if e == EXP - 1 and next_input:
                        next_input()
                    relu(i, 1, e, w)

            def c_first():
                c_sqrt(0)
                x2_evac(0, first=True)
                r_exps(0, 0)
                relu(0, 0, 0, CW)

            def c_step(i, b, it):
                act.wait_ge(x1_ready, i + 1)
                act.dma_start(cx[:, :, :], x_rows(xm_rows, i + 1)).then_inc(cx_in, 16)

                def next_input():
                    x2_evac(i + 1)
                    r_exps(i + 1, 1 - b)

                experts(i, b, CT, lambda: c_sqrt(i + 1), next_input)
                relu(i + 1, 0, 0, CW)
                act.wait_ge(y_added, (i + 1) * (EXP + 1) + 1)
                act.dma_start(x_rows(out, i), x1[b][:, :, :]).then_inc(out_stored[b], 16)

            def c_last(i, b, it):
                experts(i, b, TAIL_T)
                act.wait_ge(y_added, (i + 1) * (EXP + 1) + 1)
                act.dma_start(out[FULL * CW:N, :], x1[b][0:TAIL_ROWS, 0, :]).then_inc(out_stored[b], 16)

            ahead(act, c_first, c_step, c_last)
            for b in (0, 1):
                act.wait_ge(out_stored[b], 16 * (FULL // 2 + 2 - b))

        @block.tensor
        def _(pe):
            mm = nc.tensor.matmul

            pe.sem_inc(kv_ps, 1)
            pe.wait_ge(consts, 7)
            pe.wait_ge(counts_done, 1)
            pe.wait_ge(act_counts, 1)
            mm(ps[:, 6, 0:BLOCKS], ones[:, :], cnt[:, 0:BLOCKS], start=True, stop=True)
            mm(ps[:, 7, 0:BLOCKS], lower[:, :], cnt[:, 0:BLOCKS], start=True, stop=True).then_inc(count_sums, 1)
            pe.wait_ge(params, 16 * N_PARAMS)

            def turn_h(i):
                pe.wait_ge(hn_ready, i + 1)
                for j in range(CT):
                    for f in range(KF):
                        ins = nc.tensor.transpose(ps[:, f, j * P:(j + 1) * P], hn[:, j, f * P:(f + 1) * P], ident[:, :])
                ins.then_inc(hn_T, 1)

            def mid(i):
                pe.wait_ge(hT_ready, i + 1)
                for m in range(KF):
                    for k in range(KF):
                        ins = mm(ps[:, 2 + m, :], wx_s[:, k, m * P:(m + 1) * P], hT[:, k, :], start=k == 0, stop=k == KF - 1)
                ins.then_inc(xm_ps, 1)

            def a_first():
                turn_h(0)
                mid(0)

            def a_step(i, b, it, nt, more, norms):
                w, rows_ = (CW, P) if nt == CT else (TAIL_ROWS, TAIL_ROWS)
                pe.wait_ge(xm_ready, i + 1)
                pe.wait_ge(ek_ready, i + 1)
                for f in range(KF):
                    ins = mm(ps[:, 4 + f, 0:w], bdkv[:, 0, :], xmT[b][:, f, 0:w], start=True, stop=True)
                ins.then_inc(k_ps, 1)
                pe.wait_ge(kv_added, i + 1)
                for j in range(nt):
                    for f in range(KF):
                        ins = mm(tile(6, j)[:, f * P:(f + 1) * P], xmT[b][:, f, j * P:(j + 1) * P], bdkv[:, 1, :], start=True, stop=True)
                ins.then_inc(v_ps, 1)
                if more:
                    turn_h(i + 1)
                pe.wait_ge(ekT_ready, i + 1)
                for j in range(nt):
                    for f in range(KF):
                        ins = nc.tensor.transpose(tile(4, j)[0:rows_, f * P:(f + 1) * P],
                                                  ekT[:, f, j * P:j * P + rows_], ident[:, :])
                ins.then_inc(ek_T, 1)
                if more:
                    mid(i + 1)
                pe.wait_ge(ek_ready, i + 2)
                pe.wait_ge(vv_ready, i + 1)
                for f in range(KF):
                    o = slice(f * P, (f + 1) * P)
                    for j in range(nt):
                        ins = mm(ps[:, 6, o], ek[0:rows_, j, o], vv[0:rows_, j, o], start=j == 0, stop=j == nt - 1)
                ins.then_inc(kv_ps, 1)

            norm_ahead(pe, a_first, a_step)
            pe.wait_ge(kv_masked, 1)
            for f in range(KF):
                ins = nc.tensor.transpose(ps[:, 4, f * P:(f + 1) * P], kv_sum[:, f, :], ident[:, :])
            ins.then_inc(kv_T, 1)
            pe.wait_ge(kvT_ready, 1)
            for f in range(KF):
                ins = mm(ps[:, f, 0:D], kvT[:, f, :], wo_s[:, f, :], start=True, stop=True)
            ins.then_inc(kvw_ps, 1)
            pe.wait_ge(kvw_ready, 1)

            def queries(i, b):
                pe.wait_ge(bm_in[b], (i + 2 - b) * 8)
                pe.wait_ge(h_ready, i + 1)
                for j in range(CT):
                    for f in range(KF):
                        ins = mm(tile(0, j)[:, f * P:(f + 1) * P], xmT[b][:, f, j * P:(j + 1) * P], bdq[:, :], start=True, stop=True)
                ins.then_inc(q_ps, 1)

            def turn_q(i, b):
                pe.wait_ge(q_norm, i + 1)
                for j in range(CT):
                    for f in range(KF):
                        ins = nc.tensor.transpose(ps[:, 2 + f, j * P:(j + 1) * P], qx[:, j, f * P:(f + 1) * P], ident[:, :])
                ins.then_inc(q_T, 1)

            def attend(i, b):
                pe.wait_ge(qT_ready, i + 1)
                for j in range(CT):
                    for f in range(KF):
                        mm(tile(0, j), qT[:, f, j * P:(j + 1) * P], kvw[:, f, :], start=f == 0, stop=False)
                    ins = mm(tile(0, j), ones[0:1, :], bo_row[0:1, :], start=False, stop=True)
                ins.then_inc(at_ps, 1)

            def turn_y(i, b):
                pe.wait_ge(y_ready, i + 1)
                for j in range(CT):
                    for f in range(KF):
                        ins = nc.tensor.transpose(ps[:, 2 + f, j * P:(j + 1) * P], yn[:, j, f * P:(f + 1) * P], ident[:, :])
                ins.then_inc(y_T, 1)

            def hidden(i, b, w, m0, m1):
                for m in range(m0, m1):
                    if m == 2:
                        pe.wait_ge(xo_ready, i + 1)
                    elif m >= 4:
                        pe.wait_ge(hid_ready, i * HM + m - 2)
                    for k in range(KF):
                        ins = mm(ps[:, 4 + m % 4, 0:w], w1_s[:, k, m * P:(m + 1) * P], yT[b][:, k, 0:w], start=k == 0, stop=k == KF - 1)
                    ins.then_inc(hid_ps, 1)

            def down(i, b, j0, j1, nt):
                if j0 == 0:
                    pe.wait_ge(hid_ready, (i + 1) * HM + 1)
                for j in range(j0, j1):
                    for m in range(HM):
                        mm(tile(6, j), gT[:, m, j * P:(j + 1) * P], w2_s[:, m, :], start=m == 0, stop=False)
                    ins = mm(tile(6, j), ones[0:1, :], b2_row[0:1, :], start=False, stop=True)
                if j1 == nt:
                    ins.then_inc(mlp_ps, 1)

            def b_first():
                for part in (queries, turn_q, attend, turn_y):
                    part(0, 0)

            def b_step(i, b, it):
                pe.wait_ge(yT_ready, i + 2)
                hidden(i, b, CW, 0, 2)
                queries(i + 1, 1 - b)
                hidden(i, b, CW, 2, HM)
                turn_q(i + 1, 1 - b)
                down(i, b, 0, 1, CT)
                attend(i + 1, 1 - b)
                down(i, b, 1, 3, CT)
                turn_y(i + 1, 1 - b)
                down(i, b, 3, 4, CT)

            def b_last(i, b, it):
                pe.wait_ge(yT_ready, i + 2)
                hidden(i, b, TAIL_T * P, 0, HM)
                down(i, b, 0, TAIL_T, TAIL_T)

            ahead(pe, b_first, b_step, b_last)

            pe.wait_ge(mix_done, 2)
            pe.wait_ge(idx_ready, 2)
            pe.sem_inc(tiles_used, GT)

            def block_sum(i, k):
                a, z = (pe.value_load(group_i[0:1, bass.ds(i * CT + k + q, 1)], min_val=0, max_val=MAX_GROUPS) for q in (0, 1))
                pe.wait_ge(block_read, i * CT + k + 1)
                mm(ps[:, 6, 0:D], zero_row[0:1, 0:P], zero_row[0:1, 0:D], start=True, stop=False)
                with pe.Fori(a, z) as q:
                    for t in range(GT):
                        if t == 0:
                            pe.wait_ge(rows_ready, (q + 1) * GT)
                        pe.wait_ge(select_ready, q * GT + t + 1)
                        mm(ps[:, 6, 0:D], select[:, t, :], ring[:, bass.ds((q % (RING // GT)) * GT + t, 1), :],
                           start=False, stop=False).then_inc(tiles_used, 1)
                mm(ps[:, 6, 0:D], zero_row[0:1, 0:P], zero_row[0:1, 0:D], start=False, stop=True).then_inc(block_sums, 1)

            def turn_x2(i):
                pe.wait_ge(x2_ready, i + 1)
                for j in range(CT):
                    for f in range(KF):
                        ins = nc.tensor.transpose(ps[:, f, j * P:(j + 1) * P], x2n[:, j, f * P:(f + 1) * P], ident[:, :])
                ins.then_inc(x2_T, 1)

            def router(i):
                pe.wait_ge(high_ready, input_no(i) + KF)
                for j in range(CT):
                    o = ps[:, 7, j * EXP:(j + 1) * EXP]
                    for f in range(KF):
                        ins = mm(o, whole[:, f, j * P:(j + 1) * P], wr_s[:, f, :], start=f == 0, stop=f == KF - 1)
                ins.then_inc(r_ps, 1)

            def parts(layer_, e, k):
                c = (layer_ * EXP + e) * KF + k
                return ew_h[:, c, :], ew_l[:, c, :].bitcast(F32R)

            def layer(n_, e, src_, bank, w, done):
                for m in range(KF):
                    o, c = ps[:, bank + m, 0:w], slice(m * P, (m + 1) * P)
                    for k in range(KF):
                        wh, wl = parts(n_, e, k)
                        xh, xl = (a[:, k, 0:w] for a in src_)
                        mm(o, wh[:, c], xh, start=k == 0, stop=False)
                        mm(o, wh[:, c], xl, start=False, stop=False)
                        ins = mm(o, wl[:, c], xh, start=False, stop=k == KF - 1)
                    ins.then_inc(done, 1)

            def first(i, e, w):
                if e:
                    pe.wait_ge(high_ready, relu_no(i, 1, e - 1) + KF)
                else:
                    pe.wait_ge(split_ready, input_no(i) + KF)
                layer(0, e, x2T, 0, w, z1_ps)

            def second(i, e, w):
                pe.wait_ge(split_ready, relu_no(i, 1, e) + KF)
                if e:
                    pe.wait_ge(high_ready, relu_no(i, 2, e - 1) + KF)
                layer(1, e, [a[:, e % 2] for a in h1], 2, w, z2_ps)

            def third(i, e, nt):
                pe.wait_ge(split_ready, relu_no(i, 2, e) + KF)
                pe.wait_ge(y_added, i * (EXP + 1) + e + 2)
                for j in range(nt):
                    o, c = tile(4, j), slice(j * P, (j + 1) * P)
                    for k in range(KF):
                        wh, wl = parts(2, e, k)
                        xh, xl = (a[:, e % 2, k, c] for a in h2)
                        mm(o, xh, wh, start=k == 0, stop=False)
                        mm(o, xh, wl, start=False, stop=False)
                        ins = mm(o, xl, wh, start=False, stop=k == KF - 1)
                ins.then_inc(y_ps, 1)

            def experts(i, b, nt, between=None, next_input=False):
                w = max(nt * P, MIN_W)
                pe.wait_ge(w_ready, i + 1)
                for j in range(nt):
                    ins = nc.tensor.transpose(ps[0:EXP, 7, j * P:(j + 1) * P], rt[b][:, j, :], ident[:, :])
                ins.then_inc(w_T, 1)
                for e in range(EXP):
                    if e + 1 < EXP:
                        first(i, e + 1, w)
                    if between and e in BLOCK_AT:
                        between(BLOCK_AT.index(e))
                    if next_input and e == EXP - 1:
                        pe.wait_ge(high_ready, relu_no(i, 1, e) + KF)
                        turn_x2(i + 1)
                    second(i, e, w)
                    if e == 0:
                        pe.wait_ge(wT_ready, i + 1)
                        pe.wait_ge(y_added, i * (EXP + 1) + 1)
                        for j in range(nt):
                            ins = mm(tile(4, j), wT[:, j * P:(j + 1) * P], ebo_s[:, :], start=True, stop=True)
                        ins.then_inc(bias_ps, 1)
                    else:
                        if next_input and e == EXP - 1:
                            router(i + 1)
                        third(i, e - 1, nt)

            def c_first():
                for k in range(CT):
                    block_sum(0, k)
                turn_x2(0)
                router(0)
                pe.wait_ge(ew_split, EW // 2)
                pe.wait_ge(bn_ready, 2)
                first(0, 0, CW)

            def c_step(i, b, it):
                experts(i, b, CT, lambda k: block_sum(i + 1, k), next_input=True)
                first(i + 1, 0, CW)
                third(i, EXP - 1, CT)

            def c_last(i, b, it):
                experts(i, b, TAIL_T)
                third(i, EXP - 1, TAIL_T)

            ahead(pe, c_first, c_step, c_last)

        @block.vector
        def _(v):
            V = nc.vector
            here = {"base": 0, "n": 0}

            def link(ins):
                ins.then_inc(dve_chain, 1)
                here["n"] += 1
                v.wait_ge(dve_chain, here["base"] + here["n"])

            def mark(ins):
                ins.then_inc(dve_chain, 1)
                here["n"] += 1
                return here["base"] + here["n"]

            V.memset(src_i[:, :], TILES * P - 1).then_inc(pad_set, 1)
            V.memset(dst_i[:, :], 0).then_inc(pad_set, 1)
            V.memset(w_e[:, :], 0.0).then_inc(pad_set, 1)
            V.memset(bdq[:, :], 0.0).then_inc(diag_zero, 1)
            V.memset(bdkv[:, :, :], 0.0).then_inc(diag_zero, 1)
            V.memset(rec[:, :, 3], 0.0)
            V.memset(pos[:, :], 0.0)
            hit = (w_e, dst_i.bitcast(F32))
            V.memset(zeros[:, :], 0.0).then_inc(recs_zero, 1)
            V.memset(zero_row[:, :], 0.0)
            V.memset(eps_ln[:, :], LN_EPS)
            link(V.memset(eps_bn[:, :], BN_EPS))
            v.sem_inc(bn_var, 1)
            for s_ in (k_max, h_ready, xo_ready, block_read, y_added):
                v.sem_inc(s_, 1)
            v.sem_inc(kv_added, 1)
            for t in (ksum[:, :], kv_sum):
                V.memset(t, 0.0)
            link(V.memset(kmin[1][:, :], 3.0e38))

            v.wait_ge(edges_loaded, 96)
            link(V.tensor_scalar(blk_i[:, :], src_i[:, :], 7, None, ALU.arith_shift_right))
            V.tensor_copy(blk[:, :], blk_i[:, :]).then_inc(blk_ready, 1)
            link(V.tensor_scalar(adr[:, :], src_i[:, :], P - 1, None, ALU.bitwise_and))
            V.tensor_copy(rec[:, :, 1], adr[:, :])
            V.tensor_copy(rec[:, :, 0], dst_i[:, :])
            link(V.tensor_copy(rec[:, :, 2], w_e[:, :]))
            for k in range(BLOCKS - ACT_BLOCKS):
                ins = V.tensor_scalar(mask[:, k, :], blk[:, :], float(k), 0.0, ALU.is_equal, ALU.add, accum_out=cnt[:, k:k + 1])
            ins.then_inc(counts_done, 1)
            v.wait_ge(count_sums, 1)
            link(V.tensor_scalar(tot_i[:, :], ps[:, 6, 0:BLOCKS], float(GROUP - 1), None, ALU.add))
            link(V.tensor_scalar(tot_i[:, :], tot_i[:, :], GROUP_SHIFT, None, ALU.arith_shift_right))
            link(V.tensor_copy(groups_f[:, 0:BLOCKS], tot_i[:, :]))
            link(V.tensor_scalar(groups_f[:, 0:BLOCKS], groups_f[:, 0:BLOCKS], 1.0, None, ALU.max))
            V.memset(group_x[:, 0:1], 0.0)
            link(V.tensor_tensor_scan(group_x[:, 1:BLOCKS + 1], groups_f[:, 0:BLOCKS], groups_f[:, 0:BLOCKS], 0.0, ALU.add, ALU.bypass))
            V.tensor_copy(group_i[:, :], group_x[:, :])
            link(V.tensor_scalar(rounds_i[:, :], group_x[:, BLOCKS:BLOCKS + 1], float(GT), float(RING - 1), ALU.mult, ALU.add))
            link(V.tensor_scalar(rounds_i[:, :], rounds_i[:, :], RING.bit_length() - 1, None, ALU.arith_shift_right))
            link(V.tensor_scalar(base[:, 0:BLOCKS], group_x[:, 0:BLOCKS], float(GROUP), -1.0, ALU.mult, ALU.add))
            link(V.tensor_tensor(base[:, 0:BLOCKS], base[:, 0:BLOCKS], ps[:, 7, 0:BLOCKS], ALU.add))
            def all_places(s_):
                a, z = (2 * SGRP * g for g in SEGMENTS[s_:s_ + 2])
                picked = []
                for k in range(BLOCKS + 1):
                    if k < BLOCKS:
                        if k >= 2:
                            v.wait_ge(dve_chain, picked[k - 2])
                        ranked = mark(V.tensor_tensor_scan(rank[:, k % 2, a:z], mask[:, k, a:z], zeros[:, a:z],
                                                           base[:, k:k + 1], ALU.add, ALU.add))
                    if k:
                        v.wait_ge(dve_chain, before if k < BLOCKS else picked[-1])
                        V.tensor_copy(base[:, k - 1:k], rank[:, (k - 1) % 2, z - 1:z])
                        picked.append(mark(V.copy_predicated(pos[:, a:z], mask[:, k - 1, a:z], rank[:, (k - 1) % 2, a:z])))
                        if k == BLOCKS:
                            v.wait_ge(dve_chain, picked[-1])
                    before = ranked

            def places(s_, k0, n):
                a, z = (2 * SGRP * g for g in SEGMENTS[s_:s_ + 2])
                picked = []
                masks = mask[:, :, :].rearrange("p b e -> p (b e)")

                def of(q):
                    return masks[:, bass.ds((k0 + q) * EC + a, z - a)]

                last = {}
                for q in range(n + 2):
                    if q < n:
                        if q >= 2:
                            v.wait_ge(dve_chain, last["hit", q - 2])
                        last["rank", q] = mark(V.tensor_tensor_scan(rank[:, q % 2, a:z], of(q), zeros[:, a:z],
                                                                    base[:, bass.ds(k0 + q, 1)], ALU.add, ALU.add))
                    if 1 <= q <= n:
                        v.wait_ge(dve_chain, last.get(("pos", q - 3), last["rank", q - 1]))
                        v.sem_inc(dve_go, 1)
                        V.tensor_copy(base[:, bass.ds(k0 + q - 1, 1)], rank[:, (q - 1) % 2, z - 1:z])
                        last["hit", q - 1] = mark(V.tensor_tensor(hit[(q - 1) % 2][:, a:z], of(q - 1), rank[:, (q - 1) % 2, a:z], ALU.mult))
                    if q >= 2:
                        v.wait_ge(dve_chain, last.get(("pos", q - 3), last["hit", q - 2]))
                        last["pos", q - 2] = mark(V.tensor_tensor(pos[:, a:z], pos[:, a:z], hit[q % 2][:, a:z], ALU.add))
                v.wait_ge(dve_chain, last["pos", n - 1])

            def place_addresses(s_):
                a, z = (2 * SGRP * g for g in SEGMENTS[s_:s_ + 2])
                link(V.tensor_copy(pos_i[:, a:z], pos[:, a:z]))
                link(V.tensor_scalar(blk_i[:, a:z], pos_i[:, a:z], 7, None, ALU.arith_shift_right))
                V.tensor_copy(blk[:, a:z], blk_i[:, a:z])
                link(V.tensor_scalar(pos_i[:, a:z], pos_i[:, a:z], P - 1, None, ALU.bitwise_and))
                link(V.tensor_copy(pos[:, a:z], pos_i[:, a:z]))
                link(V.scalar_tensor_tensor(out=adr[:, a:z], in0=pos[:, a:z], scalar=float(TT), in1=blk[:, a:z],
                                            op0=ALU.mult, op1=ALU.add))
                v.sem_inc(addresses, 1)

            for s_ in range(PARTS - 2):
                all_places(s_)
                place_addresses(s_)

            v.wait_ge(bn_sd, 1)
            for k in (0, 1):
                b_, g_, be_, m_ = (bnp[:, 5 * k + q, :] for q in range(4))
                link(V.reciprocal(bn_w[:, k, :], bn_w[:, k, :]))
                link(V.tensor_tensor(bn_s[:, k, :], bn_w[:, k, :], g_, ALU.mult))
                link(V.tensor_tensor(bn_t[:, k, :], b_, m_, ALU.subtract))
                link(V.tensor_tensor(bn_t[:, k, :], bn_t[:, k, :], bn_s[:, k, :], ALU.mult))
                link(V.tensor_tensor(bn_t[:, k, :], bn_t[:, k, :], be_, ALU.add))
            v.sem_inc(bn_ready, 2)

            def row_stats(src_, nt, st_, mv_, done_):
                for j in range(nt):
                    ins = V.bn_stats(st_[:, j, :], src_[:, j, :])
                link(ins)
                v.sem_inc(dve_go, 1)
                for j in range(nt):
                    ins = V.bn_aggr(mv_[:, j, :], st_[:, j, :])
                ins.then_inc(done_, 1)

            def normalize(dst_, src_, nt, mv_, sd_, rstd_):
                link(V.reciprocal(rstd_[:, 0:nt], sd_[:, 0:nt]))
                for j in range(nt):
                    ins = V.tensor_scalar(dst_[:, j, :], src_[:, j, :], mv_[:, j, 0:1], rstd_[:, j:j + 1], ALU.subtract, ALU.mult)
                return ins

            def norm(i, b, it):
                v.wait_ge(ax[b], 16 * (it + 1))
                row_stats(xa[b], CT, stats, mv, ax_stats)
                v.wait_ge(ax_sd, 2 * i + 1)
                v.wait_ge(axn_stored[b], 16 * (it + 1))
                normalize(xa_n[b], xa[b], CT, mv, sd, rstd).then_inc(axn, 1)
                v.wait_ge(axn, i + 1)
                row_stats(xa_n[b], CT, stats, mv, ax_stats)
                v.wait_ge(ax_sd, 2 * i + 2)

            def norm_end(i, b):
                normalize(hn, xa_n[b], CT, mv, sd, rstd).then_inc(hn_ready, 1)

            def key_max(i, b, nt):
                w = CW if nt == CT else TAIL_ROWS
                v.wait_ge(k_ps, i + 1)
                link(V.tensor_reduce(kchunk[:, :], ps[:, 4:6, 0:w], AX.X, ALU.max))
                link(V.scalar_tensor_tensor(out=kmin[b][:, :], in0=kchunk[:, :], scalar=-1.0, in1=kmin[1 - b][:, :],
                                            op0=ALU.mult, op1=ALU.min))
                V.tensor_tensor(kscale[b][:, :], kmin[b][:, :], kmin[1 - b][:, :], ALU.subtract).then_inc(k_max, 1)

            def value_rows(i, nt):
                v.wait_ge(v_ps, i + 1)
                V.tensor_copy(vv[:, 0:nt, :], rows(6, nt)).then_inc(vv_ready, 1)

            def add_kv(i, b):
                v.wait_ge(kv_ps, i + 2)
                v.wait_ge(kv_added, i + 1)
                link(V.tensor_tensor(ksum[:, :], ksum[:, :], kscale[b][:, :], ALU.mult))
                V.tensor_tensor(ksum[:, :], ksum[:, :], kpart[b][:, :], ALU.add)
                for f in range(KF):
                    ins = V.scalar_tensor_tensor(out=kv_sum[:, f, :], in0=kv_sum[:, f, :], scalar=kscale[b][:, f:f + 1],
                                                 in1=ps[:, 6, f * P:(f + 1) * P], op0=ALU.mult, op1=ALU.add)
                ins.then_inc(kv_added, 1)

            PER_A = 7
            chain_a = [0]

            def a_first():
                norm(0, 0, 0)
                norm_end(0, 0)
                norm(1, 1, 0)
                v.wait_ge(hn_T, 1)
                norm_end(1, 1)
                chain_a[0] = here["base"] + here["n"]

            def a_step(i, b, it, nt, more, norms):
                here["base"], here["n"] = chain_a[0] + i * PER_A, 0
                if isinstance(i, int) and i == CHUNKS - 1:
                    here["base"] = chain_a[0] + i * PER_A - 4
                key_max(i, b, nt)
                value_rows(i, nt)
                if norms:
                    norm(i + 2, b, it + 1)
                    v.wait_ge(hn_T, i + 2)
                    norm_end(i + 2, b)
                add_kv(i, b)

            norm_ahead(v, a_first, a_step)
            v.wait_ge(kv_added, CHUNKS + 1)
            V.reciprocal(rk[:, :], ksum[:, :])
            for f in range(KF):
                ins = V.tensor_tensor(kv_sum[:, f, :], kv_sum[:, f, :], head_mask[:, :], ALU.mult)
            ins.then_inc(kv_masked, 1)

            groups = CT * HEADS

            def q_softmax(i, b):
                q = ps[:, 0:2, :].rearrange("p a (g s) -> p (a g) s", s=HD)
                e = qx[:, :, :].rearrange("p t (g s) -> p (t g) s", s=HD)
                v.wait_ge(q_ps, i + 1)
                link(V.tensor_reduce(qmax[:, :], q, AX.X, ALU.max))
                V.tensor_tensor(e, q, qmax[:, :].unsqueeze(2).to_broadcast([P, groups, HD]), ALU.subtract).then_inc(q_shift, 1)
                v.wait_ge(q_exp, i + 1)
                link(V.tensor_reduce(qsum[:, :], e, AX.X, ALU.add))
                link(V.reciprocal(qsum[:, :], qsum[:, :]))
                V.tensor_tensor(e, e, qsum[:, :].unsqueeze(2).to_broadcast([P, groups, HD]), ALU.mult).then_inc(q_norm, 1)

            def attended(i, b):
                v.wait_ge(at_ps, i + 1)
                v.wait_ge(bn_in[b], (i + 2 - b) * 8)
                link(V.tensor_tensor(h[b][:, :, :], rows(0), xb_n[b][:, :, :], ALU.add))
                v.sem_inc(h_ready, 1)
                row_stats(h[b], CT, stats, mv, y_stats)

            def y_norm(i, b):
                v.wait_ge(y_sd, i + 1)
                normalize(yn, h[b], CT, mv, sd, rstd).then_inc(y_ready, 1)

            def mixed(i, b, nt):
                v.wait_ge(bx_in[b], (i + 2 - b) * 8)
                xo = xb[b][:, 0:nt, :]
                link(V.tensor_tensor(xo, xo, h[b][:, 0:nt, :], ALU.add))
                v.wait_ge(mlp_ps, i + 1)
                V.tensor_tensor(xo, xo, rows(6, nt), ALU.add).then_inc(xo_ready, 1)

            def b_next(i, b, sorting=lambda n0, n: None):
                sorting(0, SORT_STEP // 2)
                q_softmax(i, b)
                sorting(SORT_STEP // 2, SORT_STEP - SORT_STEP // 2)
                attended(i, b)
                y_norm(i, b)

            b_next(0, 0)
            at, per = here["base"] + here["n"], 7
            for s_, c0, c1 in ((PARTS - 2, 0, SORT_CHUNKS), (PARTS - 1, SORT_CHUNKS, 2 * SORT_CHUNKS), (None, 2 * SORT_CHUNKS, FULL)):
                per_chunk = per + (3 * SORT_STEP if s_ else 0)
                with v.Fori(c0 // 2, c1 // 2) as it:
                    for b in (0, 1):
                        i = it * 2 + b
                        here["base"], here["n"] = at + (i - c0) * per_chunk, 0
                        if s_:
                            b_next(i + 1, 1 - b, lambda n0, n, i=i: places(s_, (i - c0) * SORT_STEP + n0, n))
                        else:
                            b_next(i + 1, 1 - b)
                        mixed(i, b, CT)
                        assert here["n"] == per_chunk, here["n"]
                here["base"], here["n"] = at + (c1 - c0) * per_chunk, 0
                if s_:
                    place_addresses(s_)
                at = here["base"] + here["n"]
            mixed(FULL, 0, TAIL_T)
            v.wait_ge(xo_ready, CHUNKS + 1)
            v.wait_ge(xo_stored, 16 * (CHUNKS + 1))
            v.wait_ge(hid_ready, CHUNKS * HM + 1)
            v.wait_ge(mlp_ps, CHUNKS)
            v.sem_inc(mix_done, 2)
            v.wait_ge(head_loaded, 16)
            V.tensor_copy(idx[:, 0:HEAD_T], recs[:, 0:HEAD_T, 0]).then_inc(idx_ready, 1)
            v.wait_ge(table_loaded, 16)
            V.tensor_copy(idx[:, HEAD_T:TT], recs[:, HEAD_T:TT, 0]).then_inc(idx_ready, 1)

            def block(i, k, b, stored):
                a, z = (v.value_load(group_i[0:1, bass.ds(i * CT + k + q, 1)], min_val=0, max_val=MAX_GROUPS) for q in (0, 1))
                with v.Fori(a, z) as q:
                    for t in range(GT):
                        if t % 2 == 0:
                            v.wait_ge(tiles_used, q * GT + t + 2)
                        V.tensor_scalar(select[:, t, :], iota[:, :], recs[:, bass.ds(q * GT + t, 1), 1],
                                        recs[:, bass.ds(q * GT + t, 1), 2], ALU.is_equal, ALU.mult).then_inc(select_ready, 1)
                v.wait_ge(block_sums, i * CT + k + 1)
                if k == 0:
                    v.wait_ge(cx_in, (i + 1) * 16)
                    v.wait_ge(out_stored[b], stored)
                V.tensor_tensor(x1[b][:, k, :], ps[:, 6, 0:D], cx[:, k, :], ALU.add).then_inc(block_read, 1)

            def x2_norm(i, b):
                v.wait_ge(block_read, (i + 1) * CT + 1)
                row_stats(x1[b], CT, c_stats, c_mv, x1_ready)
                v.wait_ge(c_sd, i + 1)
                normalize(x2n, x1[b], CT, c_mv, c_sdt, c_rstd).then_inc(x2_ready, 1)

            def shares(i, b):
                v.wait_ge(r_ps, i + 1)
                r = ps[:, 7, 0:CT * EXP].rearrange("p (t e) -> p t e", e=EXP)
                link(V.tensor_tensor(rt[b][:, :, :], r, br_b[:, :].unsqueeze(1).to_broadcast([P, CT, EXP]), ALU.add))
                link(V.tensor_reduce(rmax[:, :], rt[b][:, :, :], AX.X, ALU.max))
                V.tensor_tensor(rt[b][:, :, :], rt[b][:, :, :], rmax[:, :].unsqueeze(2).to_broadcast([P, CT, EXP]), ALU.subtract).then_inc(r_shift, 1)
                v.wait_ge(r_exp, i + 1)
                link(V.tensor_reduce(rmax[:, :], rt[b][:, :, :], AX.X, ALU.add))
                link(V.reciprocal(rmax[:, :], rmax[:, :]))
                V.tensor_tensor(rt[b][:, :, :], rt[b][:, :, :], rmax[:, :].unsqueeze(2).to_broadcast([P, CT, EXP]),
                                ALU.mult).then_inc(w_ready, 1)

            def add_offsets(i, b, nt):
                v.wait_ge(bias_ps, i + 1)
                v.wait_ge(w_ready, i + 1)
                V.tensor_tensor(x1[b][:, 0:nt, :], rows(4, nt), x1[b][:, 0:nt, :], ALU.add).then_inc(y_added, 1)

            def add_expert(i, e, b, nt):
                v.wait_ge(y_ps, i * EXP + e + 1)
                v.wait_ge(y_added, i * (EXP + 1) + e + 2)
                for j in range(nt):
                    ins = V.scalar_tensor_tensor(out=x1[b][:, j, :], in0=tile(4, j), scalar=rt[b][:, j, e:e + 1],
                                                 in1=x1[b][:, j, :], op0=ALU.mult, op1=ALU.add)
                ins.then_inc(y_added, 1)

            def low_part(n, half, high, low):
                v.wait_ge(high_ready, n + 1)
                V.tensor_tensor(low, whole[:, half, 0:low.shape[1]], high.bitcast(F32), ALU.subtract).then_inc(split_ready, 1)

            def low_x2(i):
                for f in range(KF):
                    low_part(input_no(i) + f, f, x2T[0][:, f, :], x2T[1][:, f, :])

            def low_layer(i, layer, e, w):
                h_ = (h1, h2)[layer - 1]
                for m in range(KF):
                    low_part(relu_no(i, layer, e) + m, m, *(a[:, e % 2, m, 0:w] for a in h_))

            start = here["base"] + here["n"]
            here["base"], here["n"] = start, 0
            for k in range(CT):
                block(0, k, 0, 16)
                for c in range(k * EW // CT, (k + 1) * EW // CT, 2):
                    v.wait_ge(ew_high, c // 2 + 1)
                    V.tensor_tensor(ew_l[:, c:c + 2, :].bitcast(F32R), ew_l[:, c:c + 2, :], ew_h[:, c:c + 2, :].bitcast(F32),
                                    ALU.subtract).then_inc(ew_split, 1)
            x2_norm(0, 0)
            low_x2(0)
            shares(0, 0)
            low_layer(0, 1, 0, CW)
            PER_C = here["n"]
            loop0 = start + PER_C

            def c_step(i, b, it):
                here["base"], here["n"] = loop0 + i * PER_C, 0
                for e in range(EXP):
                    if e in BLOCK_AT:
                        block(i + 1, BLOCK_AT.index(e), 1 - b, 16 * (it + 1 + b))
                    if e + 1 < EXP:
                        low_layer(i, 1, e + 1, CW)
                    if e == BLOCK_AT[-1]:
                        x2_norm(i + 1, 1 - b)
                    if e == EXP - 1:
                        low_x2(i + 1)
                        shares(i + 1, 1 - b)
                    low_layer(i, 2, e, CW)
                    if e == 0:
                        add_offsets(i, b, CT)
                    else:
                        add_expert(i, e - 1, b, CT)
                low_layer(i + 1, 1, 0, CW)
                add_expert(i, EXP - 1, b, CT)
                assert here["n"] == PER_C

            def c_last(i, b, it):
                w = max(TAIL_T * P, MIN_W)
                for e in range(EXP):
                    if e + 1 < EXP:
                        low_layer(i, 1, e + 1, w)
                    low_layer(i, 2, e, w)
                    if e == 0:
                        add_offsets(i, b, TAIL_T)
                    else:
                        add_expert(i, e - 1, b, TAIL_T)
                add_expert(i, EXP - 1, b, TAIL_T)

            ahead(v, lambda: None, c_step, c_last)


N_PARAMS = 25 + 3 * (P // HD)


_OUT = ((N, D), "float32")


def kernel(x, src, dst, edge_weight, L0_mix_ln1_w, L0_mix_ln1_b, L0_mix_Wx, L0_mix_bx, L0_mix_Wq, L0_mix_Wk, L0_mix_Wv,
           L0_mix_Wo, L0_mix_bo, L0_mix_ln2_w, L0_mix_ln2_b, L0_mix_W1, L0_mix_b1, L0_mix_W2, L0_mix_b2, L0_ffn_Wr,
           L0_ffn_br, L0_ffn_W1, L0_ffn_b1, L0_ffn_g1, L0_ffn_be1, L0_ffn_m1, L0_ffn_v1, L0_ffn_W2, L0_ffn_b2,
           L0_ffn_g2, L0_ffn_be2, L0_ffn_m2, L0_ffn_v2, L0_ffn_Wo, L0_ffn_bo):
    import numpy as np
    import concourse.bacc as bacc
    from concourse import mybir as mb
    from concourse.bass_utils import run_bass_kernel_spmd

    def column(a):
        return np.ascontiguousarray(np.asarray(a).reshape(-1, P).T)

    def row(a):
        return np.asarray(a).reshape(1, -1)

    def turned(a):
        return np.ascontiguousarray(np.asarray(a).T)

    padded = np.zeros((ROWS, D), np.float32)
    padded[:N] = np.asarray(x)
    arrays = {
        "x": padded, "src": np.asarray(src), "dst": np.asarray(dst), "edge_weight": np.asarray(edge_weight),
        "ln1_w": column(L0_mix_ln1_w), "ln1_b": column(L0_mix_ln1_b), "wx_t": turned(L0_mix_Wx),
        "bx": column(L0_mix_bx), "wq_t": turned(L0_mix_Wq), "wk_t": turned(L0_mix_Wk), "wv_t": turned(L0_mix_Wv),
        "wo_t": turned(L0_mix_Wo), "bo": row(L0_mix_bo), "ln2_w": column(L0_mix_ln2_w), "ln2_b": column(L0_mix_ln2_b),
        "w1_t": turned(L0_mix_W1), "b1": column(L0_mix_b1), "w2_t": turned(L0_mix_W2), "b2": row(L0_mix_b2),
        "wr": np.asarray(L0_ffn_Wr), "br": np.ascontiguousarray(np.broadcast_to(row(L0_ffn_br), (P, EXP))), "ew": np.stack([np.asarray(L0_ffn_W1), np.asarray(L0_ffn_W2), np.asarray(L0_ffn_Wo)]).reshape(-1, D),
        "eb1": column(L0_ffn_b1),
        "eg1": column(L0_ffn_g1), "ebe1": column(L0_ffn_be1), "em1": column(L0_ffn_m1), "ev1": column(L0_ffn_v1),
        "eb2": column(L0_ffn_b2), "eg2": column(L0_ffn_g2), "ebe2": column(L0_ffn_be2),
        "em2": column(L0_ffn_m2), "ev2": column(L0_ffn_v2), "ebo": np.asarray(L0_ffn_bo),
    }
    nc = bacc.Bacc("TRN2", target_bir_lowering=False, num_devices=1)
    args = {n: nc.dram_tensor(f"in_{n}", a.shape, mb.dt.from_np(a.dtype), kind="ExternalInput").ap() for n, a in arrays.items()}
    out = nc.dram_tensor("out_0", _OUT[0], mb.dt.from_np(np.dtype(_OUT[1])), kind="ExternalOutput").ap()
    build(nc, out=out, **args)
    r = run_bass_kernel_spmd(nc, [{f"in_{n}": a for n, a in arrays.items()}], core_ids=[0])
    return r.results[0]["out_0"]
```
